# Optimizing a Trainium2 kernel written in Bass

```python
import numpy as np
import jax
import jax.numpy as jnp

def _softmax(x, axis=-1):
    return jax.nn.softmax(x, axis=axis)

def _gelu(x):
    return jax.nn.gelu(x, approximate=True)

def _silu(x):
    return jax.nn.silu(x)

def _sigmoid(x):
    return jax.nn.sigmoid(x)

def _layernorm(x, axis=-1, eps=1e-05):
    m = jnp.mean(x, axis=axis, keepdims=True)
    v = jnp.var(x, axis=axis, keepdims=True)
    return (x - m) / jnp.sqrt(v + eps)

def _scatter_add(tgt, idx, src, axis=0):
    return tgt.at[idx].add(src)

def _segment_sum(src, seg, n):
    return jax.ops.segment_sum(src, seg, n)
kernel_name = 'mk_xattn_seq_d2_seqx_r8_d2d27d'

def setup_inputs(seed: int=0):
    np.random.seed(seed)
    _w = jnp.asarray

    def _rec_inputs():
        import jax
        import jax.numpy as jnp
        _rk = jax.random.key(seed)
        x = 7.22e-05 + 1 * jax.random.normal(jax.random.fold_in(_rk, 1), (4, 256, 256), jnp.float32)
        _lenS = 256 - jax.random.randint(jax.random.fold_in(_rk, 7), (4,), 0, max(1, 256 // 4) + 1, jnp.int32)
        _lenS2 = 512 - jax.random.randint(jax.random.fold_in(_rk, 8), (4,), 0, max(1, 512 // 4) + 1, jnp.int32)
        _ctx_2048P = jax.random.normal(jax.random.fold_in(_rk, 11), (4, 16, 256), jnp.float32)
        _ctx_2048c = jax.random.dirichlet(jax.random.fold_in(_rk, 511), 0.3 * jnp.ones((16,), jnp.float32), (4, 512))
        _ctx_2048t = jnp.einsum('bsk,bkd->bsd', _ctx_2048c, _ctx_2048P)
        _ctx_2048t = _ctx_2048t * jax.lax.rsqrt(jnp.mean(jnp.square(_ctx_2048t)) + 1e-12) * 0.953939
        ctx_2048 = 2.81802e-05 + 1.00001 * (_ctx_2048t + 0.3 * jax.random.normal(jax.random.fold_in(_rk, 611), (4, 512, 256), jnp.float32))
        _validS = jnp.arange(256)[None, :] < _lenS[:, None]
        _validS2 = jnp.arange(512)[None, :] < _lenS2[:, None]
        _causal = jnp.tril(jnp.ones((256, 256), dtype=bool))
        mask_BxS2_bf1 = jnp.ones((4, 512), dtype=bool)
        return (x, ctx_2048, mask_BxS2_bf1)
    x, ctx_2048, mask_BxS2_bf1 = _rec_inputs()

    def _L0_xattn_setup():
        import jax, jax.numpy as jnp
        import numpy as np
        D = 256
        H = 16
        HD = D // H
        INNER = 4 * D
        EPS = 1e-05

        def layer_norm(x, w, b):
            mu = jnp.mean(x, axis=-1, keepdims=True)
            var = jnp.mean(jnp.square(x - mu), axis=-1, keepdims=True)
            return (x - mu) * jax.lax.rsqrt(var + EPS) * w + b
        key = jax.random.key(seed)
        ks = jax.random.split(key, 12)
        B, LQ, LK = (4, 128, 256)
        std = 0.02
        inp = {'hidden_states': jax.random.normal(ks[0], (B, LQ, D), jnp.float32), 'encoder_hidden_states': jax.random.normal(ks[1], (B, LK, D), jnp.float32), 'encoder_attention_mask': jnp.ones((B, LK), dtype=bool), 'ln1_w': jnp.ones((D,), jnp.float32), 'ln1_b': jnp.zeros((D,), jnp.float32), 'q_w': jax.random.normal(ks[2], (D, D), jnp.float32) * std, 'q_b': jnp.zeros((D,), jnp.float32), 'k_w': jax.random.normal(ks[3], (D, D), jnp.float32) * std, 'k_b': jnp.zeros((D,), jnp.float32), 'v_w': jax.random.normal(ks[4], (D, D), jnp.float32) * std, 'v_b': jnp.zeros((D,), jnp.float32), 'cproj_w': jax.random.normal(ks[5], (D, D), jnp.float32) * std, 'cproj_b': jnp.zeros((D,), jnp.float32), 'ln2_w': jnp.ones((D,), jnp.float32), 'ln2_b': jnp.zeros((D,), jnp.float32), 'fc_w': jax.random.normal(ks[6], (D, INNER), jnp.float32) * std, 'fc_b': jnp.zeros((INNER,), jnp.float32), 'proj_w': jax.random.normal(ks[7], (INNER, D), jnp.float32) * std, 'proj_b': jnp.zeros((D,), jnp.float32)}
        return inp
    _L0_xattn_all = _L0_xattn_setup()
    _L0_xattn_in = {k: v for k, v in _L0_xattn_all.items() if k in ('ln1_w', 'ln1_b', 'q_w', 'q_b', 'k_w', 'k_b', 'v_w', 'v_b', 'cproj_w', 'cproj_b', 'ln2_w', 'ln2_b', 'fc_w', 'fc_b', 'proj_w', 'proj_b')}
    del _L0_xattn_all

    def _L1_xattn_setup():
        import jax, jax.numpy as jnp
        import numpy as np
        H = 256
        B, L, S = (4, 512, 10)
        key = jax.random.key(seed)
        k1, k2, k3, k4, k5, k6 = jax.random.split(key, 6)
        scale = 1.0 / np.sqrt(H)
        return {'h_english': jax.random.normal(k1, (B, L, H), dtype=jnp.float32), 'h_lojban': jax.random.normal(k2, (B, S, H), dtype=jnp.float32), 'w_q': jax.random.normal(k3, (H, H), dtype=jnp.float32) * scale, 'w_k': jax.random.normal(k4, (H, H), dtype=jnp.float32) * scale, 'w_v': jax.random.normal(k5, (H, H), dtype=jnp.float32) * scale, 'w_o': jax.random.normal(k6, (H, H), dtype=jnp.float32) * scale, 'alpha': jnp.float32(0.1)}
    _L1_xattn_all = _L1_xattn_setup()
    _L1_xattn_in = {k: v for k, v in _L1_xattn_all.items() if k in ('w_q', 'w_k', 'w_v', 'w_o', 'alpha')}
    del _L1_xattn_all
    return {'x': x, 'ctx_2048': ctx_2048, 'mask_BxS2_bf1': mask_BxS2_bf1, 'L0_xattn_ln1_w': _L0_xattn_in['ln1_w'], 'L0_xattn_ln1_b': _L0_xattn_in['ln1_b'], 'L0_xattn_q_w': _L0_xattn_in['q_w'], 'L0_xattn_q_b': _L0_xattn_in['q_b'], 'L0_xattn_k_w': _L0_xattn_in['k_w'], 'L0_xattn_k_b': _L0_xattn_in['k_b'], 'L0_xattn_v_w': _L0_xattn_in['v_w'], 'L0_xattn_v_b': _L0_xattn_in['v_b'], 'L0_xattn_cproj_w': _L0_xattn_in['cproj_w'], 'L0_xattn_cproj_b': _L0_xattn_in['cproj_b'], 'L0_xattn_ln2_w': _L0_xattn_in['ln2_w'], 'L0_xattn_ln2_b': _L0_xattn_in['ln2_b'], 'L0_xattn_fc_w': _L0_xattn_in['fc_w'], 'L0_xattn_fc_b': _L0_xattn_in['fc_b'], 'L0_xattn_proj_w': _L0_xattn_in['proj_w'], 'L0_xattn_proj_b': _L0_xattn_in['proj_b'], 'L1_xattn_w_q': _L1_xattn_in['w_q'], 'L1_xattn_w_k': _L1_xattn_in['w_k'], 'L1_xattn_w_v': _L1_xattn_in['w_v'], 'L1_xattn_w_o': _L1_xattn_in['w_o'], 'L1_xattn_alpha': _L1_xattn_in['alpha']}

def reference(x, ctx_2048, mask_BxS2_bf1, L0_xattn_ln1_w, L0_xattn_ln1_b, L0_xattn_q_w, L0_xattn_q_b, L0_xattn_k_w, L0_xattn_k_b, L0_xattn_v_w, L0_xattn_v_b, L0_xattn_cproj_w, L0_xattn_cproj_b, L0_xattn_ln2_w, L0_xattn_ln2_b, L0_xattn_fc_w, L0_xattn_fc_b, L0_xattn_proj_w, L0_xattn_proj_b, L1_xattn_w_q, L1_xattn_w_k, L1_xattn_w_v, L1_xattn_w_o, L1_xattn_alpha):
    import jax
    import jax.numpy as jnp

    def _L0_xattn_ref(hidden_states, encoder_hidden_states, encoder_attention_mask, ln1_w, ln1_b, q_w, q_b, k_w, k_b, v_w, v_b, cproj_w, cproj_b, ln2_w, ln2_b, fc_w, fc_b, proj_w, proj_b):
        import jax, jax.numpy as jnp
        import numpy as np
        D = 256
        H = 16
        HD = D // H
        INNER = 4 * D
        EPS = 1e-05

        def layer_norm(x, w, b):
            mu = jnp.mean(x, axis=-1, keepdims=True)
            var = jnp.mean(jnp.square(x - mu), axis=-1, keepdims=True)
            return (x - mu) * jax.lax.rsqrt(var + EPS) * w + b
        B, LQ, _ = hidden_states.shape
        LK = encoder_hidden_states.shape[1]
        residual = hidden_states
        x = layer_norm(hidden_states, ln1_w, ln1_b)
        q = (x @ q_w + q_b).reshape(B, LQ, H, HD).transpose(0, 2, 1, 3)
        k = (encoder_hidden_states @ k_w + k_b).reshape(B, LK, H, HD).transpose(0, 2, 1, 3)
        v = (encoder_hidden_states @ v_w + v_b).reshape(B, LK, H, HD).transpose(0, 2, 1, 3)
        scale = 1.0 / np.sqrt(HD).astype(np.float32)
        scores = jnp.einsum('bhqd,bhkd->bhqk', q, k) * scale
        mask = encoder_attention_mask[:, None, None, :]
        mask_value = jnp.finfo(scores.dtype).min
        scores = jnp.where(mask, scores, mask_value)
        attn = jax.nn.softmax(scores, axis=-1)
        out = jnp.einsum('bhqk,bhkd->bhqd', attn, v)
        out = out.transpose(0, 2, 1, 3).reshape(B, LQ, D)
        out = out @ cproj_w + cproj_b
        hidden = out + residual
        residual = hidden
        y = layer_norm(hidden, ln2_w, ln2_b)
        y = jax.nn.gelu(y @ fc_w + fc_b, approximate=True)
        y = y @ proj_w + proj_b
        return residual + y

    def _L1_xattn_ref(h_english, h_lojban, w_q, w_k, w_v, w_o, alpha):
        import jax, jax.numpy as jnp
        import numpy as np
        H = 256
        B, L, S = (4, 512, 10)
        h = h_english.shape[-1]
        q = jnp.einsum('blh,oh->blo', h_english, w_q)
        k = jnp.einsum('bsh,oh->bso', h_lojban, w_k)
        v = jnp.einsum('bsh,oh->bso', h_lojban, w_v)
        scores = jnp.einsum('blh,bsh->bls', q, k) / jnp.sqrt(jnp.float32(h))
        probs = jax.nn.softmax(scores, axis=-1)
        context = jnp.einsum('bls,bsh->blh', probs, v)
        delta = jnp.einsum('blh,oh->blo', context, w_o)
        return h_english + alpha * delta
    x = _L0_xattn_ref(x, ctx_2048, mask_BxS2_bf1, L0_xattn_ln1_w, L0_xattn_ln1_b, L0_xattn_q_w, L0_xattn_q_b, L0_xattn_k_w, L0_xattn_k_b, L0_xattn_v_w, L0_xattn_v_b, L0_xattn_cproj_w, L0_xattn_cproj_b, L0_xattn_ln2_w, L0_xattn_ln2_b, L0_xattn_fc_w, L0_xattn_fc_b, L0_xattn_proj_w, L0_xattn_proj_b)
    x = _L1_xattn_ref(x, ctx_2048, L1_xattn_w_q, L1_xattn_w_k, L1_xattn_w_v, L1_xattn_w_o, L1_xattn_alpha)
    return x

_drawn_inputs = setup_inputs


def setup_inputs(seed=0):
    import zlib

    import numpy as np

    out = dict(_drawn_inputs(seed))
    spreads = {'L0_xattn_ln1_w': (1.0, 0.6),
     'L0_xattn_ln1_b': (0.0, 0.8),
     'L0_xattn_q_b': (0.0, 0.8),
     'L0_xattn_k_b': (0.0, 0.8),
     'L0_xattn_v_b': (0.0, 0.1),
     'L0_xattn_cproj_b': (0.0, 0.1),
     'L0_xattn_ln2_w': (1.0, 0.6),
     'L0_xattn_ln2_b': (0.0, 0.735),
     'L0_xattn_fc_b': (0.0, 0.1),
     'L0_xattn_proj_b': (0.0, 0.1)}
    factors = {'L0_xattn_q_w': 8.0, 'L0_xattn_k_w': 8.0, 'L1_xattn_w_q': 2.855, 'L1_xattn_w_k': 2.856}
    for name, (base, spread) in spreads.items():
        noise = np.random.default_rng([zlib.crc32(name.encode()), seed]).standard_normal(out[name].shape)
        drawn = base * np.exp(spread * noise) if base else spread * noise
        out[name] = jnp.asarray(drawn.astype(out[name].dtype))
    for name, factor in factors.items():
        out[name] = (out[name] * factor).astype(out[name].dtype)
    return out
```

```python
from contextlib import ExitStack

import concourse.bass as bass
from concourse import mybir

F32 = mybir.dt.float32
F32R = mybir.dt.float32r
BF16 = mybir.dt.bfloat16
U8 = mybir.dt.uint8
ACT = mybir.ActivationFunctionType
ALU = mybir.AluOpType
AX = mybir.AxisListType

P = 128
B, LQ, D = 4, 256, 256
LK = 512
H, HD = 16, 16
INNER = 4 * D
EPS = 1e-5
GELU_SCALE = (2.0 / 3.141592653589793) ** 0.5
GELU_CUBIC = 0.044715
DC = D // P
TQ = LQ // P
TK = LK // P
FC = INNER // P
GH = 4
NG = H // GH
HC = P // HD
SLOTS = 8
VW = HD + 1
TERMS_Q = (0, 0, 1, 0, 1, 2)
TERMS_K = (0, 1, 0, 2, 1, 0)
ROW_MASK = len(TERMS_Q) * HD
ROW_MAX = ROW_MASK + 1
ROWS = ROW_MAX + 3 * GH
MASKED = 2.0 ** 126
Q_SCALE = HD ** -0.5
L1_SCALE = D ** -0.5
NS = NG * SLOTS

START = 7
V_AT = {36: 0, 38: 1}
LN1_AT = 7
PRE_AT = {8: 0, 10: 1, 12: 2, 14: 3, 16: 4, 24: 5}
POST_AT = {7: "OT", 9: "NT", 10: "CP", 11: "CT0", 12: "CT1", 13: "ZT", 14: "F0", 16: "F1", 18: "F2", 20: "F3",
           24: "PJ0", 26: "PJ1", 27: "PJ2", 28: "PJ3", 29: "HT", 31: "G", 32: "S0", 33: "S1", 35: "PT0",
           36: "PT1", 37: "PC", 38: "DL"}
GELU_CUBE, GELU_TANH, GELU_Y, GELU_SPLIT = 1, 2, 3, 4
LOAD_AT, CX_HIGH_AT, STORE_AT = 8, 12, 38
MAX_TILES = ((0, 1), (2, 3), (4,), (5,), (6,), (7,), (), ())
SPLIT_AT, ROWS_AT, O_AT = 5, 7, 5

U_ZT, U_CT, U_Q, U_K, U_V, PRE_USES = 0, 1, 3, 4, 6, 8
(W_OT, W_NT, W_CP, W_CT, W_ZT, W_F, W_PJ, W_HT, W_G, W_S, W_PT, W_PC, W_DL,
 POST_USES) = 0, 2, 3, 4, 6, 7, 11, 12, 13, 14, 16, 18, 19, 20
POST_SPLITS = [W_NT, W_CT, W_CT + 1, W_ZT, W_HT, W_G, W_PT, W_PT + 1, W_PC]
PRE_SPLITS = [U_ZT, U_CT, U_CT + 1]
V_VB, V_LN1W, V_LN1B, V_LN2W, V_LN2B, V_FCB, VECS = 0, 2, 4, 6, 8, 10, 18
STACK_DMAS = 2 * len(TERMS_Q) + 1


def build(nc, x, ctx, mask, ln1_w, ln1_b, q_w, q_b, k_w, k_b, v_w, v_b, cproj_w, cproj_b, ln2_w, ln2_b,
          fc_w, fc_b, proj_w, proj_b, l1_q, l1_k, l1_v, l1_o, alpha, out):
    with ExitStack() as stack:
        def sb(name, shape, dt=F32):
            return stack.enter_context(nc.sbuf_tensor(name, shape, dt))

        def ps(name, shape):
            return stack.enter_context(nc.psum_tensor(name, shape, F32))

        def sem(name):
            return stack.enter_context(nc.semaphore(name))

        ident = sb("ident", [P, P])
        ident_b = sb("ident_b", [P, P], BF16)
        sel_small = sb("sel_small", [3 * GH, GH])
        def pair(name, shape):
            return sb(name + "_h", shape, F32R), sb(name + "_l", shape, F32R)
        wq = pair("wq", [P, DC, D])
        wk = pair("wk", [P, DC, D])
        wv = pair("wv", [P, DC, D])
        wc = pair("wc", [P, DC, D])
        wf = pair("wf", [P, DC, INNER])
        wp = pair("wp", [P, FC, D])
        wa = pair("wa", [P, DC, D])
        wo = pair("wo", [P, DC, D])
        vec_rows = sb("vec_rows", [VECS, P])
        vecs = sb("vecs", [P, VECS])
        lnq = sb("lnq", [P, DC])
        bq = sb("bq", [P, DC])
        bk = sb("bk", [P, DC])
        bf = sb("bf", [P, FC])
        cb = sb("cb", [P, D])
        pb = sb("pb", [P, D])
        alpha_c = sb("alpha_c", [P, 1])
        xz = sb("xz", [P, TQ, D])
        minus_half = sb("minus_half", [P, TQ])
        ln1 = sb("ln1", [P, TQ, 9])
        cx = sb("cx", [P, TK, D])
        zT = pair("zT", [P, DC, LQ])
        cT = pair("cT", [P, DC, LK])
        mask_u = sb("mask_u", [P, LK], U8)
        mask_f = sb("mask_f", [P, LK])
        mask_row = sb("mask_row", [1, LK], BF16)
        qf = sb("qf", [P, DC, LQ])
        qp = sb("qp", [P, 3, DC, LQ], BF16)
        kf = sb("kf", [P, LK])
        kp = sb("kp", [P, 3, DC, LK], BF16)
        q_stack = sb("q_stack", [ROWS, H, LQ], BF16)
        k_stack = sb("k_stack", [ROWS, H, LK], BF16)
        vals = sb("vals", [P, TK, H, VW])
        neg_max = sb("neg_max", [P, 2, TQ, GH])
        max_rest = sb("max_rest", [P, TQ, GH])
        max_cols = sb("max_cols", [P, TQ, ROWS], BF16)
        probs = sb("probs", [P, 2, GH, TK, LQ])
        oT = sb("oT", [P, NG, LQ])
        qk_rows = oT[0:1, 0:2, :]
        qk_perm = oT[0:1, 2:4, :]
        h = sb("h", [P, TQ, D])
        ln2 = sb("ln2", [P, TQ, 9])
        z2 = sb("z2", [P, TQ, D])
        pcx = sb("pcx", [P, TK, D])
        pc = pair("pc", [P, TK, D])
        pT = pair("pT", [P, DC, LK])
        aT = pair("aT", [P, DC, LQ])
        rden = sb("rden", [P, TQ, H])
        fx2 = sb("fx2", [P, 2, 2 * LQ])
        y = pair("y", [P, FC, LQ])
        stat1 = sb("stat1", [P, 4, TQ])
        sel = fx2[0:3 * GH].rearrange("p a n -> p (a n)").bitcast(BF16).rearrange("p (h n) -> p h n", h=GH)
        fx = [fx2[:, 0, :], fx2[:, 1, :], z2[:].rearrange("p c n -> p (c n)")]
        ft = [pcx[:, 0:2, :].rearrange("p k d -> p (k d)"), pcx[:, 2:4, :].rearrange("p k d -> p (k d)"),
              qf[:].rearrange("p c n -> p (c n)")]
        prob1 = pcx[:].rearrange("p (t k) d -> p t (k d)", t=TQ)
        p1T = [t[:, 0:TK, :] for t in y]
        mixT = [t[:, TK:TK + DC, :] for t in y]
        gT = [t[:, TK + DC:TK + 2 * DC, :] for t in y]

        def raw(s, j, half):
            return probs[:, s, j, 2 * half:2 * half + 2, :]
        raw_q, raw_k, raw_v, raw_c = raw(0, 0, 0), raw(0, 0, 1), raw(0, 1, 0), raw(0, 1, 1)
        raw_l1 = [raw(0, 2, 0), raw(0, 2, 1), raw(0, 3, 0), raw(0, 3, 1)]
        raw_f = probs[:, 1, 0:2, :, :].rearrange("p c k n -> p c (k n)")
        raw_p = probs[:, 1, 2:4, :, :].rearrange("p c k n -> p (c k) n")

        s1 = ps("s1", [P, 2, 512])
        s2 = ps("s2", [P, 2, 512])
        om = ps("om", [P, 512])
        pre_ps = ps("pre_ps", [P, 512])
        post_ps = ps("post_ps", [P, 2, 512])
        om_rows = om[:, LQ:LQ + LQ // 2].bitcast(BF16)

        vec_in, bc_in = sem("vec_in"), sem("bc_in")
        wq_in, wk_in, wv_in, wc_in = sem("wq_in"), sem("wk_in"), sem("wv_in"), sem("wc_in")
        l1_in, wf_in, wp_in = sem("l1_in"), sem("wf_in"), sem("wp_in")
        x_in, mask_in, cx_in = sem("x_in"), sem("mask_in"), sem("cx_in")
        h_in, pcx_in, h_free = sem("h_in"), sem("pcx_in"), sem("h_free")
        sel_in = sem("sel_in")
        pool_step = sem("pool_step")
        consts = sem("consts")
        dve_const = sem("dve_const")
        vec_ps, vec_done = sem("vec_ps"), sem("vec_done")
        bq_ps, bq_done, prep_ps, prep_done = sem("bq_ps"), sem("bq_done"), sem("prep_ps"), sem("prep_done")
        w_hi, w_lo = sem("w_hi"), sem("w_lo")
        wp_done, prep_step = sem("wp_done"), sem("prep_step")
        ln1_step, z1_done = sem("ln1_step"), sem("z1_done")
        rstd1, rstd2 = sem("rstd1"), sem("rstd2")
        pre_full, pre_free, pre_hi = sem("pre_full"), sem("pre_free"), sem("pre_hi")
        mask_done, row_done = sem("mask_done"), sem("row_done")
        qr_done, qm_done, q_parts = sem("qr_done"), sem("qm_done"), sem("q_parts")
        kh_done, kr_done, km_done, k_parts = (
            sem("kh_done"), sem("kr_done"), sem("km_done"), sem("k_parts"))
        stacked = [sem("stacked0"), sem("stacked1")]
        s1_full, s1_free = sem("s1_full"), sem("s1_free")
        s2_full, s2_free = sem("s2_full"), sem("s2_free")
        max_step, max_split, rows_ps, rows_in = sem("max_step"), sem("max_split"), sem("rows_ps"), sem("rows_in")
        pv_done, o_done = sem("pv_done"), sem("o_done")
        post_full = [sem("post_full0"), sem("post_full1")]
        post_free = [sem("post_free0"), sem("post_free1")]
        post_hi = sem("post_hi")
        cx_high, cx_split, xb_done, rden_done = sem("cx_high"), sem("cx_split"), sem("xb_done"), sem("rden_done")
        h1_done, ln2_step, z2_done, hb_done = sem("h1_done"), sem("ln2_step"), sem("z2_done"), sem("hb_done")
        square, cube_step, cube, tanh_done = sem("square"), sem("cube_step"), sem("cube"), sem("tanh_done")
        y_done, y_hi, y_split = sem("y_done"), sem("y_hi"), sem("y_split")
        max1, d_step = sem("max1"), sem("d_step")

        def await_(eng, s, n):
            if not isinstance(n, int) or n > 0:
                eng.wait_ge(s, n)

        def await_alone(eng, s, n):
            await_(eng, s, n)
            if not isinstance(n, int):
                eng.nop(nofuse=True)

        def post_use(b, n):
            return n % 2, POST_USES // 2 * b + n // 2 + 1

        def by_head(ap):
            return ap.rearrange("p (c h d) -> p c d h", c=DC, h=HC)

        def parts_of(ap):
            return ap.rearrange("p (c d h) -> p c d h", c=DC, h=HC)

        def chunk(i):
            return slice(i * P, (i + 1) * P)

        block = stack.enter_context(nc.Block())

        def run(eng, iteration, prologue, epilogue):
            prologue()
            iteration(0, True, False)
            with eng.Fori(1, B - 1) as b:
                iteration(b, False, False)
            iteration(B - 1, False, True)
            epilogue()

        def slots(b, last):
            for at in range(START, START + NS):
                ab = b + 1 if at >= NS else b
                yield at, ab, at % NS // SLOTS, at % SLOTS, not (last and at >= NS)

        def ahead(b, g):
            return (b, g + 1) if g + 1 < NG else (b + 1, 0)

        def behind(b, g):
            return (b, g - 1) if g > 0 else (b - 1, NG - 1)

        @block.sync
        def _(sp):
            def load_pre(b):
                await_alone(sp, pre_full, PRE_USES * (b - 1) + 1)
                sp.dma_start(xz[:], x[b].rearrange("(p t) d -> p t d", t=TQ)).then_inc(x_in, 16)
                await_alone(sp, row_done, b)
                sp.dma_start(mask_u[:], mask[b:b + 1, :].partition_broadcast(P) if isinstance(b, int)
                             else mask[bass.ds(b, 1), :].partition_broadcast(P)).then_inc(mask_in, 16)
                await_alone(sp, pre_full, PRE_USES * (b - 1) + 3)
                sp.dma_start(cx[:], ctx[b].rearrange("(p k) d -> p k d", k=TK)).then_inc(cx_in, 16)

            def stack_heads(b, c):
                heads = slice(c * HC, (c + 1) * HC)
                await_alone(sp, s2_full, NS * (b - 1) + SLOTS * (2 * c + 2))
                await_alone(sp, q_parts, b + 1)
                for i, part in enumerate(TERMS_Q):
                    sp.dma_start(q_stack[i * HD:(i + 1) * HD, heads, :], qp[:, part, c, :]).then_inc(stacked[c], 16)
                await_alone(sp, row_done, b + 1)
                sp.dma_start(k_stack[ROW_MASK:ROW_MASK + 1, heads, :],
                             mask_row[0:1, :].unsqueeze(1).to_broadcast([1, HC, LK])).then_inc(stacked[c], 16)
                await_alone(sp, k_parts, 2 * b + c + 1)
                for i, part in enumerate(TERMS_K):
                    sp.dma_start(k_stack[i * HD:(i + 1) * HD, heads, :], kp[:, part, c, :]).then_inc(stacked[c], 16)

            def prologue():
                load_pre(0)
                sp.dma_start(raw_q, q_w.rearrange("(c p) n -> p c n", p=P)).then_inc(wq_in, 16)
                row = 0
                for v in (v_b, ln1_w, ln1_b, ln2_w, ln2_b, fc_b):
                    n = v.shape[0] // P
                    sp.dma_start(vec_rows[row:row + n, :], v.rearrange("(r p) -> r p", p=P)).then_inc(vec_in, 16)
                    row += n
                for i, v in enumerate((q_b, k_b)):
                    sp.dma_start(qk_rows[:, i, :], v.rearrange("(o n) -> o n", o=1)).then_inc(vec_in, 16)
                sp.dma_start(raw_k, k_w.rearrange("(c p) n -> p c n", p=P)).then_inc(wk_in, 16)
                sp.dma_start(raw_v, v_w.rearrange("(c p) n -> p c n", p=P)).then_inc(wv_in, 16)
                for r, w in zip(raw_l1, (l1_q, l1_k, l1_v, l1_o)):
                    sp.dma_start(r, w.rearrange("(c p) n -> p c n", p=P)).then_inc(l1_in, 16)
                sp.dma_start(raw_c, cproj_w.rearrange("(c p) n -> p c n", p=P)).then_inc(wc_in, 16)
                sp.dma_start(raw_f, fc_w.rearrange("(c p) n -> p c n", p=P)).then_inc(wf_in, 16)
                sp.dma_start(raw_p, proj_w.rearrange("(c p) n -> p c n", p=P)).then_inc(wp_in, 16)
                sp.dma_start(cb[:], cproj_b.rearrange("(o n) -> o n", o=1).partition_broadcast(P)).then_inc(bc_in, 16)
                sp.dma_start(pb[:], proj_b.rearrange("(o n) -> o n", o=1).partition_broadcast(P)).then_inc(bc_in, 16)
                sp.dma_start(alpha_c[:], alpha.partition_broadcast(P)).then_inc(bc_in, 16)
                sp.wait_ge(consts, 2)
                for g in range(NG):
                    sp.dma_start(k_stack[ROW_MAX:ROWS, g * GH:(g + 1) * GH, :], sel[:]).then_inc(sel_in, 16)
                stack_heads(0, 0)

            def iteration(b, first, last):
                if not last:
                    load_pre(b + 1)
                stack_heads(b, 1)
                if not last:
                    stack_heads(b + 1, 0)

            def epilogue():
                sp.wait_ge(h_free, 16 * (B + 1))

            run(sp, iteration, prologue, epilogue)

        @block.tensor
        def _(pe):
            def product(o, w, wi, v, vi, n, start=True, stop=True):
                for k in range(n):
                    for i, (a, c) in enumerate(((0, 0), (0, 1), (1, 0))):
                        mm = pe.matmul(o, wi(w[a], k), vi(v[c], k), start=start and k == 0 and i == 0,
                                       stop=stop and k == n - 1 and i == 2)
                return mm

            def pre(b, n):
                await_(pe, pre_free, PRE_USES * b + n)
                if n == U_ZT:
                    pe.wait_ge(z1_done, b + 1)
                    for c in range(DC):
                        for t in range(TQ):
                            mm = pe.transpose(pre_ps[:, c * LQ + t * P:c * LQ + (t + 1) * P], xz[:, t, chunk(c)], ident[:])
                elif n < U_Q:
                    c = n - U_CT
                    pe.wait_ge(cx_in, 16 * (b + 1))
                    for k in range(TK):
                        mm = pe.transpose(pre_ps[:, chunk(k)], cx[:, k, chunk(c)], ident[:])
                elif n == U_Q:
                    for c in range(DC):
                        mm = product(pre_ps[:, c * LQ:(c + 1) * LQ], wq, lambda w, k: w[:, k, chunk(c)],
                                     zT, lambda v, k: v[:, k, :], DC)
                elif n < U_V:
                    c = n - U_K
                    mm = product(pre_ps[:], wk, lambda w, k: w[:, k, chunk(c)],
                                 cT, lambda v, k: v[:, k, :], DC)
                else:
                    for i in range(2):
                        t = 2 * (n - U_V) + i
                        mm = product(pre_ps[:, i * D:(i + 1) * D], cT, lambda v, k: v[:, k, chunk(t)],
                                     wv, lambda w, k: w[:, k, :], DC)
                mm.then_inc(pre_full, 1)

            def max_tile(b, g, s):
                hd, t = g * GH + s // 2, s % 2
                if s == 0:
                    pe.wait_ge(stacked[g // 2], 16 * STACK_DMAS * (b + 1))
                n = NS * b + SLOTS * g + s
                await_(pe, s1_free, n - 1)
                pe.matmul(s1[:, s % 2, :], q_stack[0:ROW_MAX, hd, chunk(t)], k_stack[0:ROW_MAX, hd, :],
                          start=True, stop=True).then_inc(s1_full, 1)

            def max_rows(b, g):
                pe.wait_ge(max_split, NG * b + g + 1)
                await_(pe, o_done, NG * b + g - 1)
                for t in range(TQ):
                    mm = pe.transpose(om_rows[0:ROWS, chunk(t)], max_cols[:, t, :], ident_b[:])
                mm.then_inc(rows_ps, 1)

            def exp_tile(b, g, s):
                hd = g * GH + s // 2
                n = NS * b + SLOTS * g + s
                await_(pe, s2_free, n - 1)
                for i in range(2):
                    k = 2 * (s % 2) + i
                    mm = pe.matmul(s2[:, s % 2, i * LQ:(i + 1) * LQ], k_stack[:, hd, chunk(k)], q_stack[:, hd, :],
                                   start=True, stop=True)
                mm.then_inc(s2_full, 1)

            def pv(b, g, k):
                if k == 0:
                    await_(pe, s2_free, NS * b + SLOTS * (g + 1))
                    pe.wait_ge(pre_free, PRE_USES * (b + 1))
                for j in range(GH):
                    mm = pe.matmul(om[32 * j:32 * j + VW, 0:LQ], vals[:, k, g * GH + j, :], probs[:, g % 2, j, k, :],
                                   start=k == 0, stop=k == TK - 1)
                if k == TK - 1:
                    mm.then_inc(pv_done, 1)

            def post(b, step):
                def open_(n):
                    bank, count = post_use(b, n)
                    await_(pe, post_free[bank], count)
                    return post_ps[:, bank, :]

                def ready(n):
                    bank, count = post_use(b, n)
                    pe.wait_ge(post_free[bank], count + 1)

                def fill(mm, n):
                    mm.then_inc(post_full[n % 2], 1)

                if step in ("CT0", "CT1"):
                    c = int(step[2])
                    pe.wait_ge(pcx_in, 16 * (b + 1))
                    o = open_(W_CT + c)
                    for k in range(TK):
                        mm = pe.transpose(o[:, chunk(k)], pcx[:, k, chunk(c)], ident[:])
                    fill(mm, W_CT + c)
                elif step == "OT":
                    pe.wait_ge(o_done, NG * (b + 1))
                    for t in range(TQ):
                        o = open_(W_OT + t)
                        for g in range(NG):
                            mm = pe.transpose(o[:, chunk(g)], oT[:, g, chunk(t)], ident[:])
                        fill(mm, W_OT + t)
                elif step in ("NT", "ZT", "HT"):
                    n = {"NT": W_NT, "ZT": W_ZT, "HT": W_HT}[step]
                    src = {"NT": z2, "ZT": z2, "HT": h}[step]
                    if step == "NT":
                        ready(W_OT)
                        ready(W_OT + 1)
                    elif step == "ZT":
                        pe.wait_ge(z2_done, b + 1)
                    else:
                        ready(W_PJ)
                    o = open_(n)
                    for c in range(DC):
                        for t in range(TQ):
                            mm = pe.transpose(o[:, c * LQ + t * P:c * LQ + (t + 1) * P], src[:, t, chunk(c)], ident[:])
                    fill(mm, n)
                elif step in ("CP", "DL"):
                    n, act, w = (W_CP, aT, wc) if step == "CP" else (W_DL, mixT, wo)
                    ready(W_NT if step == "CP" else W_PC)
                    o = open_(n)
                    for t in range(TQ):
                        mm = product(o[:, t * D:(t + 1) * D], act, lambda v, k: v[:, k, chunk(t)],
                                     w, lambda v, k: v[:, k, :], DC)
                    fill(mm, n)
                elif step[0] == "F":
                    i = int(step[1])
                    ready(W_ZT)
                    o = open_(W_F + i)
                    for j in range(2):
                        f = 2 * i + j
                        mm = product(o[:, j * LQ:(j + 1) * LQ], wf, lambda w, k: w[:, k, chunk(f)],
                                     aT, lambda v, k: v[:, k, :], DC)
                    fill(mm, W_F + i)
                elif step[:2] == "PJ":
                    i = int(step[2])
                    t, half = i // 2, i % 2
                    if i < 2:
                        pe.wait_ge(y_split, 4 * b + 2 * half + 2)
                    o = open_(W_PJ) if i == 0 else post_ps[:, W_PJ % 2, :]
                    mm = product(o[:, t * D:(t + 1) * D], y, lambda v, k: v[:, k + 4 * half, chunk(t)],
                                 wp, lambda v, k: v[:, k + 4 * half, :], 4, start=half == 0, stop=half == 1)
                    if i == 3:
                        fill(mm, W_PJ)
                elif step == "G":
                    ready(W_HT)
                    o = open_(W_G)
                    for c in range(DC):
                        mm = product(o[:, c * LQ:(c + 1) * LQ], wa, lambda w, k: w[:, k, chunk(c)],
                                     aT, lambda v, k: v[:, k, :], DC)
                    fill(mm, W_G)
                elif step in ("S0", "S1"):
                    t = int(step[1])
                    ready(W_G)
                    o = open_(W_S + t)
                    mm = product(o, gT, lambda v, k: v[:, k, chunk(t)], pT, lambda v, k: v[:, k, :], DC)
                    fill(mm, W_S + t)
                elif step in ("PT0", "PT1"):
                    i = int(step[2])
                    ready(W_S)
                    ready(W_S + 1)
                    o = open_(W_PT + i)
                    for j in range(2):
                        for t in range(TQ):
                            mm = pe.transpose(o[:, j * LQ + t * P:j * LQ + (t + 1) * P],
                                              prob1[:, t, chunk(2 * i + j)], ident[:])
                    fill(mm, W_PT + i)
                elif step == "PC":
                    pe.wait_ge(cx_split, b + 1)
                    ready(W_PT)
                    ready(W_PT + 1)
                    o = open_(W_PC)
                    for c in range(DC):
                        mm = product(o[:, c * LQ:(c + 1) * LQ], pc, lambda v, k: v[:, k, chunk(c)],
                                     p1T, lambda v, k: v[:, k, :], TK)
                    fill(mm, W_PC)

            def prologue():
                pe.wait_ge(consts, 2)
                pe.wait_ge(vec_in, 16 * 8)
                pe.transpose(s2[:, 0, 0:VECS], vec_rows[:], ident[0:VECS, 0:VECS]).then_inc(vec_ps, 1)
                pre(0, U_ZT)
                pe.wait_ge(wq_in, 16)
                pe.wait_ge(vec_done, 2)
                for k in range(DC):
                    mm = pe.matmul(s2[0:1, 1, 0:D], vecs[:, V_LN1B + k:V_LN1B + k + 1], raw_q[:, k, :],
                                   start=k == 0, stop=k == DC - 1)
                mm.then_inc(bq_ps, 1)
                for n in range(U_CT, U_CT + DC):
                    pre(0, n)
                pe.wait_ge(bq_done, 2)
                for i in range(2 * DC):
                    mm = pe.matmul(s2[:, 1, D + i:D + i + 1], qk_perm[:, i // DC, chunk(i % DC)], ident[0:1, 0:1],
                                   start=True, stop=True)
                mm.then_inc(bq_ps, 1)
                pe.wait_ge(w_lo, 1)
                pre(0, U_Q)
                pe.wait_ge(w_lo, 2)
                pre(0, U_K)
                pre(0, U_K + 1)
                pe.wait_ge(l1_in, 16 * 4)
                for c in range(DC):
                    for k in range(DC):
                        mm = pe.matmul(s2[:, 0, c * D:(c + 1) * D], raw_l1[0][:, k, chunk(c)], raw_l1[1][:, k, :],
                                       start=k == 0, stop=k == DC - 1)
                mm.then_inc(prep_ps, 1)
                pe.wait_ge(bq_done, 4)
                for c in range(DC):
                    for k in range(DC):
                        mm = pe.transpose(s2[:, 1, c * D + k * P:c * D + (k + 1) * P], raw_l1[3][:, k, chunk(c)], ident[:])
                mm.then_inc(prep_ps, 1)
                pe.wait_ge(wc_in, 16)
                pe.wait_ge(prep_step, 1)
                for k in range(DC):
                    pe.matmul(s1[:, 1, 0:D], h[:, k, 0:P], raw_c[:, k, :], start=k == 0, stop=k == DC - 1)
                pe.wait_ge(wf_in, 16)
                for f in range(FC):
                    for k in range(DC):
                        mm = pe.matmul(s1[:, 1, D + f:D + f + 1], raw_f[:, k, chunk(f)], vecs[:, V_LN2B + k:V_LN2B + k + 1],
                                       start=k == 0, stop=k == DC - 1)
                mm.then_inc(prep_ps, 1)
                pe.wait_ge(prep_done, 1)
                for c in range(DC):
                    for k in range(DC):
                        mm = pe.matmul(s1[:, 0, c * D:(c + 1) * D], raw_l1[2][:, k, chunk(c)], z2[:, k, :],
                                       start=k == 0, stop=k == DC - 1)
                mm.then_inc(prep_ps, 1)
                pe.wait_ge(prep_done, 2)
                pe.wait_ge(w_lo, 6)
                pe.wait_ge(sel_in, 16 * NG)
                for s in range(SLOTS):
                    max_tile(0, 0, s)
                pre(0, U_V)
                pre(0, U_V + 1)
                max_rows(0, 0)
                for s in range(START):
                    attend(0, 0, s, 0)
                    attend(0, 0, s, 1)

            def attend(b, g, s, part):
                if part == 0:
                    nb, ng = ahead(b, g)
                    if not (isinstance(nb, int) and nb == B):
                        for i in MAX_TILES[s]:
                            max_tile(nb, ng, i)
                        if s == ROWS_AT:
                            max_rows(nb, ng)
                else:
                    pb_, pg = behind(b, g)
                    if s == 0:
                        pe.wait_ge(rows_in, NG * b + g + 1)
                    if s < TK and not (isinstance(pb_, int) and pb_ < 0):
                        pv(pb_, pg, s)
                    exp_tile(b, g, s)

            def iteration(b, first, last):
                for at, ab, g, s, attends in slots(b, last):
                    if attends:
                        attend(ab, g, s, 0)
                    if not last and at in PRE_AT:
                        pre(b + 1, PRE_AT[at])
                    if not last and at in V_AT:
                        pre(b + 1, U_V + V_AT[at])
                    if not first and at in POST_AT:
                        post(b - 1, POST_AT[at])
                    if attends:
                        attend(ab, g, s, 1)

            def epilogue():
                for k in range(TK):
                    pv(B - 1, NG - 1, k)
                for step in POST_AT.values():
                    post(B - 1, step)

            run(pe, iteration, prologue, epilogue)

        @block.scalar
        def _(act):
            def pre(b, n):
                act.wait_ge(pre_full, PRE_USES * b + n + 1)
                if n < U_Q:
                    dst = zT[0][:].rearrange("p c n -> p (c n)") if n == U_ZT else cT[0][:, n - U_CT, :]
                    act.activation(dst, pre_ps[:], ACT.Copy).then_inc(pre_hi, 1)
                elif n == U_Q:
                    await_(act, stacked[0], 16 * STACK_DMAS * b)
                    await_(act, stacked[1], 16 * STACK_DMAS * b)
                    await_(act, q_parts, b)
                    for c in range(DC):
                        act.activation(qf[:, c, :], pre_ps[:, c * LQ:(c + 1) * LQ], ACT.Identity, bias=bq[:, c:c + 1])
                    for c in range(DC):
                        a = act.activation(qp[:, 0, c, :], pre_ps[:, c * LQ:(c + 1) * LQ], ACT.Identity, bias=bq[:, c:c + 1])
                    a.then_inc(pre_free, 1)
                    act.wait_ge(qr_done, b + 1)
                    act.activation(qp[:, 1, :, :], qf[:], ACT.Copy).then_inc(qm_done, 1)
                elif n < U_V:
                    c = n - U_K
                    await_(act, stacked[c], 16 * STACK_DMAS * b)
                    act.wait_ge(pre_free, PRE_USES * b + n + 1)
                    act.activation(kp[:, 0, c, :], kf[:], ACT.Copy).then_inc(kh_done, 1)
                    act.wait_ge(kr_done, 2 * b + c + 1)
                    act.activation(kp[:, 1, c, :], kf[:], ACT.Copy).then_inc(km_done, 1)
                else:
                    i = n - U_V
                    await_(act, pv_done, NG * b)
                    act.activation(vals[:, 2 * i:2 * i + 2, :, 0:HD],
                                   pre_ps[:].rearrange("p (t h d) -> p t h d", t=2, h=H), ACT.Copy).then_inc(pre_free, 1)

            def rows(b, g):
                act.wait_ge(rows_ps, NG * b + g + 1)
                act.activation(q_stack[ROW_MASK:ROWS, g * GH:(g + 1) * GH, :],
                               om_rows[ROW_MASK:ROWS, :].unsqueeze(1).to_broadcast([ROWS - ROW_MASK, GH, LQ]),
                               ACT.Copy).then_inc(rows_in, 1)

            def exp(b, g, s):
                if s == 0:
                    await_(act, pv_done, NG * b + g - 1)
                act.wait_ge(s2_full, NS * b + SLOTS * g + s + 1)
                k = 2 * (s % 2)
                act.activation(probs[:, g % 2, s // 2, k:k + 2, :],
                               s2[:, s % 2, :].rearrange("p (k n) -> p k n", k=2), ACT.Exp).then_inc(s2_free, 1)

            def o_out(b, g):
                act.wait_ge(pv_done, NG * b + g + 1)
                act.activation(oT[:, g, :], om[:, 0:LQ], ACT.Copy).then_inc(o_done, 1)

            def post(b, step):
                def full(n):
                    bank, count = post_use(b, n)
                    act.wait_ge(post_full[bank], count)
                    return post_ps[:, bank, :]

                def high(dst, n):
                    act.activation(dst.rearrange("p c n -> p (c n)"), full(n), ACT.Copy).then_inc(post_hi, 1)

                if step in ("CT0", "CT1"):
                    c = int(step[2])
                    act.activation(pT[0][:, c, :], full(W_CT + c), ACT.Copy).then_inc(post_hi, 1)
                elif step in ("NT", "ZT", "HT"):
                    high(aT[0][:], {"NT": W_NT, "ZT": W_ZT, "HT": W_HT}[step])
                elif step[0] == "F":
                    i = int(step[1])
                    ps_ = full(W_F + i)
                    if i == 3:
                        act.wait_ge(y_split, 4 * b + 1)
                    for j in range(2):
                        a = act.activation(fx[i % 3][:, j * LQ:(j + 1) * LQ], ps_[:, j * LQ:(j + 1) * LQ], ACT.Identity,
                                           bias=bf[:, 2 * i + j:2 * i + j + 1])
                    a.then_inc(post_free[(W_F + i) % 2], 1)
                elif step == "G":
                    high(gT[0], W_G)
                elif step in ("S0", "S1"):
                    t = int(step[1])
                    ps_ = full(W_S + t)
                    act.wait_ge(max1, 2 * b + t + 1)
                    act.wait_ge(cx_split, b + 1)
                    act.activation(prob1[:, t, :], ps_, ACT.Exp, bias=stat1[:, 0, t:t + 1],
                                   accum_out=stat1[:, 1, t:t + 1]).then_inc(post_free[(W_S + t) % 2], 1)
                elif step in ("PT0", "PT1"):
                    i = int(step[2])
                    high(p1T[0][:, 2 * i:2 * i + 2, :], W_PT + i)
                elif step == "PC":
                    high(mixT[0], W_PC)

            def gelu_tanh(b, i):
                act.wait_ge(cube, 4 * b + i + 1)
                act.activation(ft[i % 3], ft[i % 3], ACT.Tanh, scale=GELU_SCALE).then_inc(tanh_done, 1)

            def gelu_high(b, i):
                act.wait_ge(y_done, 4 * b + i + 1)
                act.activation(y[0][:, 2 * i:2 * i + 2, :].rearrange("p c n -> p (c n)"), fx[i % 3], ACT.Copy)\
                   .then_inc(y_hi, 1)

            def post_slot(b, at):
                if POST_AT.get(at - GELU_SPLIT, "")[:1] == "F":
                    gelu_high(b, int(POST_AT[at - GELU_SPLIT][1]))
                if at == CX_HIGH_AT:
                    act.wait_ge(pcx_in, 16 * (b + 1))
                    act.activation(pc[0][:], pcx[:], ACT.Copy).then_inc(cx_high, 1)
                if at in POST_AT:
                    post(b, POST_AT[at])
                if POST_AT.get(at - GELU_TANH, "")[:1] == "F":
                    gelu_tanh(b, int(POST_AT[at - GELU_TANH][1]))

            def load_post(b):
                act.wait_ge(h_free, 16 * (b + 1))
                act.dma_start(h[:], x[b].rearrange("(p t) d -> p t d", t=TQ)).then_inc(h_in, 16)
                act.dma_start(pcx[:], ctx[b].rearrange("(p k) d -> p k d", k=TK)).then_inc(pcx_in, 16)

            def store(b):
                bank, count = post_use(b, W_DL)
                act.wait_ge(post_free[bank], count + 1)
                act.dma_start(out[b].rearrange("(p t) d -> p t d", t=TQ), h[:]).then_inc(h_free, 16)

            def prologue():
                act.wait_ge(vec_done, 2)
                pre(0, U_ZT)
                act.wait_ge(wq_in, 16)
                for k in range(DC):
                    a = act.activation(parts_of(wq[0][:, k, :]), by_head(raw_q[:, k, :]), ACT.Copy, scale=lnq[:, k:k + 1])
                a.then_inc(w_hi, 1)
                for n in range(U_CT, U_CT + DC):
                    pre(0, n)
                act.wait_ge(wk_in, 16)
                for k in range(DC):
                    a = act.activation(parts_of(wk[0][:, k, :]), by_head(raw_k[:, k, :]), ACT.Copy)
                a.then_inc(w_hi, 1)
                act.wait_ge(bq_done, 4)
                pre(0, U_Q)
                pre(0, U_K)
                pre(0, U_K + 1)
                act.wait_ge(wv_in, 16)
                act.activation(wv[0][:], raw_v, ACT.Copy).then_inc(w_hi, 1)
                act.wait_ge(prep_ps, 1)
                act.activation(wa[0][:].rearrange("p c n -> p (c n)"), s2[:, 0, :], ACT.Copy, scale=L1_SCALE).then_inc(w_hi, 1)
                act.wait_ge(wc_in, 16)
                act.activation(wc[0][:], raw_c, ACT.Copy).then_inc(w_hi, 1)
                act.wait_ge(prep_ps, 4)
                act.activation(wo[0][:].rearrange("p c n -> p (c n)"), s1[:, 0, :], ACT.Copy).then_inc(w_hi, 1)
                act.wait_ge(wf_in, 16)
                for k in range(DC):
                    a = act.activation(wf[0][:, k, :], raw_f[:, k, :], ACT.Copy, scale=vecs[:, V_LN2W + k:V_LN2W + k + 1])
                a.then_inc(w_hi, 1)
                act.wait_ge(w_lo, 7)
                act.wait_ge(wp_done, 3)
                pre(0, U_V)
                pre(0, U_V + 1)
                rows(0, 0)
                for s in range(START):
                    attend(0, 0, s)

            def attend(b, g, s):
                nb, ng = ahead(b, g)
                if s == ROWS_AT and not (isinstance(nb, int) and nb == B):
                    rows(nb, ng)
                pb_, pg = behind(b, g)
                if s == O_AT and not (isinstance(pb_, int) and pb_ < 0):
                    o_out(pb_, pg)
                exp(b, g, s)

            def iteration(b, first, last):
                for at, ab, g, s, attends in slots(b, last):
                    if not first and at == LOAD_AT:
                        load_post(b - 1)
                    if not last and at in PRE_AT:
                        pre(b + 1, PRE_AT[at])
                    if not last and at in V_AT:
                        pre(b + 1, U_V + V_AT[at])
                    if not first:
                        post_slot(b - 1, at)
                    if attends:
                        attend(ab, g, s)
                    if not first and at == STORE_AT:
                        store(b - 1)

            def epilogue():
                load_post(B - 1)
                o_out(B - 1, NG - 1)
                for at in range(START, START + NS):
                    post_slot(B - 1, at)
                store(B - 1)

            run(act, iteration, prologue, epilogue)

        @block.vector
        def _(dve):
            def layer_norm(src, st, z, step, rstd, b, done):
                for t in range(TQ):
                    i = dve.bn_stats(st[:, t, 0:6], src[:, t, :])
                i.then_inc(step, 1)
                await_alone(dve, step, 3 * b + 1)
                for t in range(TQ):
                    i = dve.bn_aggr(st[:, t, 6:8], st[:, t, 0:6])
                i.then_inc(step, 1)
                dve.wait_ge(step, 3 * b + 2)
                dve.tensor_scalar(st[:, :, 8], st[:, :, 7], EPS, None, ALU.add).then_inc(step, 1)
                dve.wait_ge(rstd, b + 1)
                for t in range(TQ):
                    i = dve.tensor_scalar(z[:, t, :], src[:, t, :], st[:, t, 6:7], st[:, t, 8:9], ALU.subtract, ALU.mult)
                i.then_inc(done, 1)

            def norm_x(b):
                dve.wait_ge(x_in, 16 * (b + 1))
                layer_norm(xz, ln1, xz, ln1_step, rstd1, b, z1_done)

            def take_mask(b):
                dve.wait_ge(mask_in, 16 * (b + 1))
                dve.tensor_copy(mask_f[:].rearrange("q (k p) -> q k p", k=TK),
                                mask_u[:].rearrange("q (p k) -> q k p", k=TK)).then_inc(mask_done, 1)

            def pre(b, n):
                if n < U_Q:
                    i = PRE_SPLITS.index(n)
                    dve.wait_ge(pre_hi, len(PRE_SPLITS) * b + i + 1)
                    j = 0 if n == U_ZT else n - U_CT
                    dst, hi = [t[:].rearrange("p c n -> p (c n)") if n == U_ZT else t[:, j, :]
                               for t in ((zT[1], zT[0]) if n == U_ZT else (cT[1], cT[0]))]
                    dve.tensor_tensor(dst, pre_ps[:], hi.bitcast(F32), ALU.subtract).then_inc(pre_free, 1)
                elif n == U_Q:
                    dve.wait_ge(pre_free, PRE_USES * b + U_Q + 1)
                    dve.tensor_tensor(qf[:], qf[:], qp[:, 0, :, :], ALU.subtract).then_inc(qr_done, 1)
                elif n < U_V:
                    c = n - U_K
                    dve.wait_ge(pre_full, PRE_USES * b + n + 1)
                    dve.wait_ge(mask_done, b + 1)
                    await_(dve, k_parts, 2 * b + c)
                    dve.scalar_tensor_tensor(kf[:], pre_ps[:], bk[:, c:c + 1], mask_f[:], ALU.add, ALU.mult)\
                       .then_inc(pre_free, 1)
                    dve.wait_ge(pre_free, PRE_USES * b + n + 1)
                    dve.wait_ge(kh_done, 2 * b + c + 1)
                    dve.tensor_tensor(kf[:], kf[:], kp[:, 0, c, :], ALU.subtract).then_inc(kr_done, 1)

            def take_max(b, g, s):
                dve.wait_ge(s1_full, NS * b + SLOTS * g + s + 1)
                dve.tensor_reduce(neg_max[:, g % 2, s % 2, s // 2:s // 2 + 1], s1[:, s % 2, :], AX.X, ALU.max,
                                  negate=True).then_inc(s1_free, 1)

            def split_max(b, g):
                step = 3 * (NG * b + g)
                part = [max_cols[:, :, ROW_MAX + i:ROWS:3] for i in range(3)]
                neg = neg_max[:, g % 2, :, :]
                dve.wait_ge(s1_free, NS * b + SLOTS * (g + 1))
                await_(dve, rows_ps, NG * b + g)
                dve.tensor_copy(part[0], neg).then_inc(max_step, 1)
                dve.wait_ge(max_step, step + 1)
                dve.tensor_tensor(max_rest[:], neg, part[0], ALU.subtract).then_inc(max_step, 1)
                dve.wait_ge(max_step, step + 2)
                dve.tensor_copy(part[1], max_rest[:]).then_inc(max_step, 1)
                dve.wait_ge(max_step, step + 3)
                dve.tensor_tensor(part[2], max_rest[:], part[1], ALU.subtract).then_inc(max_split, 1)

            def post(b, step):
                def full(n):
                    bank, count = post_use(b, n)
                    dve.wait_ge(post_full[bank], count)
                    return post_ps[:, bank, :]

                def low(dst, hi, n):
                    dve.wait_ge(post_hi, len(POST_SPLITS) * b + POST_SPLITS.index(n) + 1)
                    dve.tensor_tensor(dst, post_ps[:, n % 2, :].rearrange("p (c n) -> p c n", c=dst.shape[1]),
                                      hi.bitcast(F32), ALU.subtract).then_inc(post_free[n % 2], 1)

                if step in ("CT0", "CT1"):
                    c = int(step[2])
                    low(pT[1][:, c:c + 1, :], pT[0][:, c:c + 1, :], W_CT + c)
                elif step == "OT":
                    for t in range(TQ):
                        o = full(W_OT + t).rearrange("p (h e) -> p h e", h=H)
                        dve.reciprocal(rden[:, t, :], o[:, :, HD]).then_inc(rden_done, 1)
                        dve.wait_ge(rden_done, 2 * b + t + 1)
                        dve.tensor_tensor(z2[:, t, :].rearrange("p (h d) -> p h d", h=H), o[:, :, 0:HD],
                                          rden[:, t, :].unsqueeze(2).to_broadcast([P, H, HD]), ALU.mult)\
                           .then_inc(post_free[(W_OT + t) % 2], 1)
                elif step in ("NT", "ZT", "HT"):
                    low(aT[1][:], aT[0][:], {"NT": W_NT, "ZT": W_ZT, "HT": W_HT}[step])
                elif step == "CP":
                    o = full(W_CP)
                    dve.wait_ge(xb_done, b + 1)
                    dve.tensor_tensor(h[:].rearrange("p t n -> p (t n)"), o, h[:].rearrange("p t n -> p (t n)"), ALU.add)\
                       .then_inc(post_free[W_CP % 2], 1)
                    bank, count = post_use(b, W_CP)
                    dve.wait_ge(post_free[bank], count + 1)
                    layer_norm(h, ln2, z2, ln2_step, rstd2, b, z2_done)
                elif step == "PJ3":
                    o = full(W_PJ)
                    dve.wait_ge(hb_done, b + 1)
                    dve.tensor_tensor(h[:].rearrange("p t n -> p (t n)"), o, h[:].rearrange("p t n -> p (t n)"), ALU.add)\
                       .then_inc(post_free[W_PJ % 2], 1)
                elif step == "G":
                    low(gT[1], gT[0], W_G)
                elif step in ("S0", "S1"):
                    t = int(step[1])
                    dve.tensor_reduce(stat1[:, 0, t:t + 1], full(W_S + t), AX.X, ALU.max, negate=True).then_inc(max1, 1)
                elif step in ("PT0", "PT1"):
                    i = int(step[2])
                    low(p1T[1][:, 2 * i:2 * i + 2, :], p1T[0][:, 2 * i:2 * i + 2, :], W_PT + i)
                elif step == "PC":
                    low(mixT[1], mixT[0], W_PC)
                elif step == "DL":
                    for n in range(2):
                        bank, count = post_use(b, W_S + n)
                        dve.wait_ge(post_free[bank], count + 1)
                    dve.reciprocal(stat1[:, 2, :], stat1[:, 1, :]).then_inc(d_step, 1)
                    dve.wait_ge(d_step, 2 * b + 1)
                    dve.tensor_scalar(stat1[:, 3, :], stat1[:, 2, :], alpha_c[:, 0:1], None, ALU.mult).then_inc(d_step, 1)
                    dve.wait_ge(d_step, 2 * b + 2)
                    o = full(W_DL)
                    for t in range(TQ):
                        i = dve.scalar_tensor_tensor(h[:, t, :], o[:, t * D:(t + 1) * D], stat1[:, 3, t:t + 1], h[:, t, :],
                                                     ALU.mult, ALU.add)
                    i.then_inc(post_free[W_DL % 2], 1)

            def gelu_cube(b, i):
                f = ft[i % 3]
                dve.wait_ge(square, 4 * b + i + 1)
                dve.tensor_scalar(f, f, GELU_CUBIC, 1.0, ALU.mult, ALU.add).then_inc(cube_step, 1)
                dve.wait_ge(cube_step, 4 * b + i + 1)
                dve.tensor_tensor(f, f, fx[i % 3], ALU.mult).then_inc(cube, 1)

            def gelu_y(b, i):
                dve.wait_ge(tanh_done, 4 * b + i + 1)
                dve.scalar_tensor_tensor(fx[i % 3], ft[i % 3], 1.0, fx[i % 3], ALU.add, ALU.mult)\
                   .then_inc(y_done, 1)

            def low_weights(dst, src, hi, n):
                dve.wait_ge(w_hi, n)
                return dve.tensor_tensor(dst, src, hi.bitcast(F32), ALU.subtract).then_inc(w_lo, 1)

            def prologue():
                dve.memset(max_cols[:], 0.0).then_inc(dve_const, 1)
                dve.wait_ge(dve_const, 1)
                dve.memset(max_cols[:, :, ROW_MASK:ROW_MAX], 1.0).then_inc(dve_const, 1)
                dve.memset(om[:], 0.0).then_inc(post_free[0], 1)
                dve.memset(vals[:, :, :, HD:VW], 1.0).then_inc(post_free[1], 1)
                norm_x(0)
                dve.memset(q_stack[ROW_MASK:ROWS, :, :], 1.0).then_inc(dve_const, 1)
                dve.wait_ge(vec_ps, 1)
                dve.tensor_copy(vecs[:], s2[:, 0, 0:VECS]).then_inc(vec_done, 1)
                dve.wait_ge(vec_done, 1)
                dve.tensor_scalar(lnq[:], vecs[:, V_LN1W:V_LN1W + DC], Q_SCALE, None, ALU.mult).then_inc(vec_done, 1)
                pre(0, U_ZT)
                take_mask(0)
                dve.wait_ge(w_hi, 1)
                for k in range(DC):
                    for c in range(DC):
                        i = dve.scalar_tensor_tensor(
                            parts_of(wq[1][:, k, :])[:, c], by_head(raw_q[:, k, :])[:, c], lnq[:, k:k + 1],
                            parts_of(wq[0][:, k, :])[:, c].bitcast(F32), ALU.mult, ALU.subtract)
                i.then_inc(w_lo, 1)
                for n in range(U_CT, U_CT + DC):
                    pre(0, n)
                dve.wait_ge(bq_ps, 1)
                dve.tensor_tensor(parts_of(qk_perm[:, 0, :]), by_head(s2[0:1, 1, 0:D]), by_head(qk_rows[:, 0, :]), ALU.add)\
                   .then_inc(bq_done, 1)
                dve.tensor_copy(parts_of(qk_perm[:, 1, :]), by_head(qk_rows[:, 1, :])).then_inc(bq_done, 1)
                dve.wait_ge(w_hi, 2)
                for k in range(DC):
                    i = dve.tensor_tensor(parts_of(wk[1][:, k, :]), by_head(raw_k[:, k, :]),
                                          parts_of(wk[0][:, k, :]).bitcast(F32), ALU.subtract)
                i.then_inc(w_lo, 1)
                dve.wait_ge(bq_ps, 2)
                dve.tensor_scalar(bq[:], s2[:, 1, D:D + DC], Q_SCALE, None, ALU.mult).then_inc(bq_done, 1)
                dve.tensor_copy(bk[:], s2[:, 1, D + DC:D + 2 * DC]).then_inc(bq_done, 1)
                pre(0, U_Q)
                pre(0, U_K)
                pre(0, U_K + 1)
                low_weights(wv[1][:], raw_v, wv[0][:], 3)
                dve.wait_ge(w_hi, 4)
                dve.scalar_tensor_tensor(wa[1][:].rearrange("p c n -> p (c n)"), s2[:, 0, :], L1_SCALE,
                                         wa[0][:].rearrange("p c n -> p (c n)").bitcast(F32), ALU.mult, ALU.subtract)\
                   .then_inc(w_lo, 1)
                dve.wait_ge(prep_ps, 2)
                dve.tensor_copy(z2[:].rearrange("p c n -> p (c n)"), s2[:, 1, :]).then_inc(prep_done, 1)
                dve.wait_ge(bc_in, 48)
                dve.wait_ge(prep_ps, 3)
                dve.tensor_tensor(cb[:], s1[:, 1, 0:D], cb[:], ALU.add).then_inc(h_free, 16)
                dve.tensor_tensor(bf[:], s1[:, 1, D:D + FC], vecs[:, V_FCB:VECS], ALU.add).then_inc(prep_done, 1)
                low_weights(wc[1][:], raw_c, wc[0][:], 5)
                low_weights(wo[1][:].rearrange("p c n -> p (c n)"), s1[:, 0, :],
                            wo[0][:].rearrange("p c n -> p (c n)"), 6)
                dve.wait_ge(w_hi, 7)
                for k in range(DC):
                    i = dve.scalar_tensor_tensor(wf[1][:, k, :], raw_f[:, k, :], vecs[:, V_LN2W + k:V_LN2W + k + 1],
                                                 wf[0][:, k, :].bitcast(F32), ALU.mult, ALU.subtract)
                i.then_inc(w_lo, 1)
                for s in range(SLOTS):
                    take_max(0, 0, s)
                split_max(0, 0)
                for s in range(START):
                    attend(0, 0, s)

            def attend(b, g, s):
                nb, ng = ahead(b, g)
                if not (isinstance(nb, int) and nb == B):
                    for i in MAX_TILES[s]:
                        take_max(nb, ng, i)
                    if s == SPLIT_AT:
                        split_max(nb, ng)

            def post_slot(b, at):
                if POST_AT.get(at - GELU_Y, "")[:1] == "F":
                    gelu_y(b, int(POST_AT[at - GELU_Y][1]))
                if at in POST_AT:
                    post(b, POST_AT[at])
                if POST_AT.get(at - GELU_CUBE, "")[:1] == "F":
                    gelu_cube(b, int(POST_AT[at - GELU_CUBE][1]))

            def iteration(b, first, last):
                for at, ab, g, s, attends in slots(b, last):
                    if attends:
                        attend(ab, g, s)
                    if not last:
                        if at == LN1_AT:
                            norm_x(b + 1)
                        if at in PRE_AT:
                            if PRE_AT[at] == U_Q:
                                take_mask(b + 1)
                            pre(b + 1, PRE_AT[at])
                    if not first:
                        post_slot(b - 1, at)

            def epilogue():
                for at in range(START, START + NS):
                    post_slot(B - 1, at)

            run(dve, iteration, prologue, epilogue)

        @block.gpsimd
        def _(pool):
            def rstd(st, step, b, done):
                pool.wait_ge(step, 3 * b + 3)
                pool.tensor_tensor(st[:, :, 8], st[:, :, 8], minus_half[:], ALU.pow).then_inc(done, 1)

            def mask_row_of(b):
                await_alone(pool, mask_done, b + 1)
                for c in range(2):
                    await_alone(pool, stacked[c], 16 * STACK_DMAS * b)
                pool.tensor_scalar(mask_row[:], mask_f[0:1, :], -1.0, MASKED, ALU.add, ALU.mult).then_inc(row_done, 1)

            def pre(b, n):
                if n == U_Q:
                    mask_row_of(b)
                    pool.wait_ge(qm_done, b + 1)
                    pool.tensor_tensor(qp[:, 2, :, :], qf[:], qp[:, 1, :, :], ALU.subtract).then_inc(q_parts, 1)
                elif U_K <= n < U_V:
                    c = n - U_K
                    pool.wait_ge(km_done, 2 * b + c + 1)
                    pool.tensor_tensor(kp[:, 2, c, :], kf[:], kp[:, 1, c, :], ALU.subtract).then_inc(k_parts, 1)

            def post(b, step):
                if step == "OT":
                    pool.wait_ge(h_in, 16 * (b + 1))
                    pool.tensor_tensor(h[:], h[:], cb[:].unsqueeze(1).to_broadcast([P, TQ, D]), ALU.add).then_inc(xb_done, 1)
                elif step == "CT1":
                    pool.wait_ge(cx_high, b + 1)
                    pool.tensor_tensor(pc[1][:], pcx[:], pc[0][:].bitcast(F32), ALU.subtract).then_inc(cx_split, 1)
                elif step == "CP":
                    rstd(ln2, ln2_step, b, rstd2)
                    pool.wait_ge(z2_done, b + 1)
                    pool.tensor_tensor(h[:], h[:], pb[:].unsqueeze(1).to_broadcast([P, TQ, D]), ALU.add).then_inc(hb_done, 1)
                elif step[0] == "F":
                    i = int(step[1])
                    bank, count = post_use(b, W_F + i)
                    if i < 2:
                        pool.wait_ge(cx_split, b + 1)
                    elif i == 2:
                        pool.wait_ge(q_parts, min(b + 3, B) if isinstance(b, int) else b + 3)
                    pool.wait_ge(post_free[bank], count + 1)
                    pool.tensor_tensor(ft[i % 3], fx[i % 3], fx[i % 3], ALU.mult).then_inc(square, 1)

            def gelu_split(b, i):
                hi, lo = [t[:, 2 * i:2 * i + 2, :].rearrange("p c n -> p (c n)") for t in y]
                pool.wait_ge(y_hi, 4 * b + i + 1)
                pool.tensor_tensor(lo, fx[i % 3], hi.bitcast(F32), ALU.subtract).then_inc(y_split, 1)

            def post_slot(b, at):
                if POST_AT.get(at - GELU_SPLIT, "")[:1] == "F":
                    gelu_split(b, int(POST_AT[at - GELU_SPLIT][1]))
                if at in POST_AT:
                    post(b, POST_AT[at])

            def prologue():
                pool.memset(ident[:], 0.0).then_inc(pool_step, 1)
                pool.memset(sel_small[:], 1.0).then_inc(pool_step, 1)
                pool.wait_ge(pool_step, 2)
                pool.affine_select(out=ident[:], in_=ident[:], compare_op=ALU.not_equal, fill=1.0, base=0,
                                   pattern=[[-1, P]], channel_multiplier=1).then_inc(pool_step, 1)
                pool.affine_select(out=sel_small[:], in_=sel_small[:], compare_op=ALU.is_ge, fill=0.0, base=0,
                                   pattern=[[-3, GH]], channel_multiplier=1).then_inc(pool_step, 1)
                pool.memset(minus_half[:], -0.5).then_inc(pool_step, 1)
                pool.wait_ge(pool_step, 5)
                pool.affine_select(out=sel_small[:], in_=sel_small[:], compare_op=ALU.is_ge, fill=0.0, base=2,
                                   pattern=[[3, GH]], channel_multiplier=-1).then_inc(pool_step, 1)
                pool.tensor_scalar(ident_b[:], ident[:], 1.0, None, ALU.mult).then_inc(consts, 1)
                rstd(ln1, ln1_step, 0, rstd1)
                pool.wait_ge(pool_step, 6)
                pool.tensor_scalar(sel[:], sel_small[:].unsqueeze(2).to_broadcast([3 * GH, GH, LK]), 1.0, None, ALU.mult)\
                    .then_inc(consts, 1)
                pool.wait_ge(vec_done, 1)
                pool.tensor_scalar(h[:, :, 0:P], vecs[:, V_VB:V_VB + DC].unsqueeze(2).to_broadcast([P, DC, P]), 1.0, None, ALU.mult)\
                    .then_inc(prep_step, 1)
                for n in (U_Q, U_K, U_K + 1):
                    pre(0, n)
                pool.wait_ge(wp_in, 16)
                pool.tensor_scalar(raw_p, raw_p, 0.5, None, ALU.mult).then_inc(wp_done, 1)
                pool.wait_ge(wp_done, 1)
                pool.tensor_scalar(wp[0][:], raw_p, 1.0, None, ALU.mult).then_inc(wp_done, 1)
                pool.wait_ge(wp_done, 2)
                pool.tensor_tensor(wp[1][:], raw_p, wp[0][:].bitcast(F32), ALU.subtract).then_inc(wp_done, 1)

            def iteration(b, first, last):
                for at in range(START, START + NS):
                    if not last and at == LN1_AT:
                        rstd(ln1, ln1_step, b + 1, rstd1)
                    if not last and at in PRE_AT:
                        pre(b + 1, PRE_AT[at])
                    if not first:
                        post_slot(b - 1, at)

            def epilogue():
                for at in range(START, START + NS):
                    post_slot(B - 1, at)

            run(pool, iteration, prologue, epilogue)


_INS = ["x", "ctx_2048", "mask_BxS2_bf1", "L0_xattn_ln1_w", "L0_xattn_ln1_b", "L0_xattn_q_w", "L0_xattn_q_b",
        "L0_xattn_k_w", "L0_xattn_k_b", "L0_xattn_v_w", "L0_xattn_v_b", "L0_xattn_cproj_w", "L0_xattn_cproj_b",
        "L0_xattn_ln2_w", "L0_xattn_ln2_b", "L0_xattn_fc_w", "L0_xattn_fc_b", "L0_xattn_proj_w",
        "L0_xattn_proj_b", "L1_xattn_w_q", "L1_xattn_w_k", "L1_xattn_w_v", "L1_xattn_w_o", "L1_xattn_alpha"]


def kernel(**inputs):
    import numpy as _np
    import concourse.bacc as _bacc
    from concourse import mybir as _mybir
    from concourse.bass_utils import run_bass_kernel_spmd as _run

    nc = _bacc.Bacc("TRN2", target_bir_lowering=False, num_devices=1)
    arrays, args = {}, []
    for name in _INS:
        a = _np.ascontiguousarray(inputs[name])
        if a.dtype == _np.bool_:
            a = a.view(_np.uint8)
        if a.ndim == 0 or name.endswith("alpha"):
            a = a.reshape(1, 1)
        arrays[f"in_{name}_dram"] = a
        args.append(nc.dram_tensor(f"in_{name}_dram", a.shape, _mybir.dt.from_np(a.dtype), kind="ExternalInput").ap())
    args.append(nc.dram_tensor("out_0_dram", (B, LQ, D), _mybir.dt.float32, kind="ExternalOutput").ap())
    build(nc, *args)
    r = _run(nc, [arrays], core_ids=[0])
    return r.results[0]["out_0_dram"]
```

```python
from contextlib import ExitStack

import concourse.bass as bass
from concourse import mybir

F32 = mybir.dt.float32
F32R = mybir.dt.float32r
BF16 = mybir.dt.bfloat16
U8 = mybir.dt.uint8
ACT = mybir.ActivationFunctionType
ALU = mybir.AluOpType
AX = mybir.AxisListType

P = 128
B, LQ, D = 4, 256, 256
LK = 512
H, HD = 16, 16
INNER = 4 * D
EPS = 1e-5
GELU_SCALE = (2.0 / 3.141592653589793) ** 0.5
GELU_CUBIC = 0.044715
DC = D // P
TQ = LQ // P
TK = LK // P
FC = INNER // P
GH = 4
NG = H // GH
HC = P // HD
SLOTS = 8
VW = HD + 1
TERMS_Q = (0, 0, 1, 0, 1, 2)
TERMS_K = (0, 1, 0, 2, 1, 0)
ROW_MASK = len(TERMS_Q) * HD
ROW_MAX = ROW_MASK + 1
ROWS = ROW_MAX + 3 * GH
MASKED = 2.0 ** 126
Q_SCALE = HD ** -0.5
L1_SCALE = D ** -0.5
NS = NG * SLOTS

START = 7
U_CT, U_ZT, U_Q, U_K, U_V, PRE_USES = 0, 2, 3, 4, 6, 8
V_AT = {36: 0, 38: 1}
LN1_AT = 7
PRE_AT = {7: U_CT, 8: U_CT + 1, 9: U_ZT, 10: U_Q, 15: U_K, 19: U_K + 1}
POST_AT = {7: "OT", 9: "NT", 10: "CP", 11: "CT0", 12: "CT1", 13: "ZT", 14: "F0", 16: "F1", 18: "F2", 19: "PJ0",
           20: "F3", 22: "PJ1", 24: "PJ2", 26: "PJ3", 28: "HT", 29: "G", 30: "S0", 31: "S1", 33: "PT0",
           34: "PT1", 35: "PC", 37: "DL"}
PREP_AT = {8: "WA", 10: "WT", 12: "CB", 13: "WO", 14: "WC", 21: "WF0", 22: "WF1", 29: "WP0", 30: "WP1", 38: "END"}
GELU_CUBE, GELU_TANH, GELU_Y, GELU_SPLIT = 1, 2, 3, 4
LOAD_AT, CX_HIGH_AT, STORE_AT = 8, 12, 38
MAX_TILES = ((0, 1), (2, 3), (4,), (5,), (6,), (7,), (), ())
SPLIT_AT, ROWS_AT, O_AT = 5, 6, 5

(W_OT, W_NT, W_CP, W_CT, W_ZT, W_F, W_PJ, W_HT, W_G, W_S, W_PT, W_PC, W_DL,
 POST_USES) = 0, 2, 3, 4, 6, 7, 11, 12, 13, 14, 16, 18, 19, 20
POST_SPLITS = [W_NT, W_CT, W_CT + 1, W_ZT, W_HT, W_G, W_PT, W_PT + 1, W_PC]
PRE_SPLITS = [U_CT, U_CT + 1, U_ZT]
V_LN1W, V_LN1B, V_VB, V_LN2W, V_LN2B, V_FCB, VECS = 0, 2, 4, 6, 8, 10, 18
STACK_DMAS = 2 * len(TERMS_Q) + 1


def build(nc, x, ctx, mask, ln1_w, ln1_b, q_w, q_b, k_w, k_b, v_w, v_b, cproj_w, cproj_b, ln2_w, ln2_b,
          fc_w, fc_b, proj_w, proj_b, l1_q, l1_k, l1_v, l1_o, alpha, out):
    with ExitStack() as stack:
        def sb(name, shape, dt=F32):
            return stack.enter_context(nc.sbuf_tensor(name, shape, dt))

        def ps(name, shape):
            return stack.enter_context(nc.psum_tensor(name, shape, F32))

        def sem(name):
            return stack.enter_context(nc.semaphore(name))

        ident = sb("ident", [P, P])
        ident_b = sb("ident_b", [P, P], BF16)
        sel_small = sb("sel_small", [3 * GH, GH])
        def pair(name, shape):
            return sb(name + "_h", shape, F32R), sb(name + "_l", shape, F32R)
        wq = pair("wq", [P, DC, D])
        wk = pair("wk", [P, DC, D])
        wv = pair("wv", [P, DC, D])
        wc = pair("wc", [P, DC, D])
        wf = pair("wf", [P, DC, INNER])
        wp = pair("wp", [P, FC, D])
        wa = pair("wa", [P, DC, D])
        wo = pair("wo", [P, DC, D])
        vec_rows = sb("vec_rows", [VECS, P])
        vecs = sb("vecs", [P, VECS])
        lnq = sb("lnq", [P, DC])
        bq = sb("bq", [P, DC])
        bk = sb("bk", [P, DC])
        bf = sb("bf", [P, FC])
        cb = sb("cb", [P, D])
        pb = sb("pb", [P, D])
        alpha_c = sb("alpha_c", [P, 1])
        xz = sb("xz", [P, TQ, D])
        minus_half = sb("minus_half", [P, TQ])
        ln1 = sb("ln1", [P, TQ, 9])
        cx = sb("cx", [P, TK, D])
        zT = pair("zT", [P, DC, LQ])
        cT = pair("cT", [P, DC, LK])
        mask_u = sb("mask_u", [P, LK], U8)
        mask_f = sb("mask_f", [P, LK])
        mask_row = sb("mask_row", [1, LK], BF16)
        qf = sb("qf", [P, DC, LQ])
        qp = sb("qp", [P, 3, DC, LQ], BF16)
        kf = sb("kf", [P, LK])
        kp = sb("kp", [P, 3, DC, LK], BF16)
        q_stack = sb("q_stack", [ROWS, H, LQ], BF16)
        k_stack = sb("k_stack", [ROWS, H, LK], BF16)
        vals = sb("vals", [P, TK, H, VW])
        neg_max = sb("neg_max", [P, 2, TQ, GH])
        max_rest = sb("max_rest", [P, TQ, GH])
        max_cols = sb("max_cols", [P, TQ, ROWS], BF16)
        probs = sb("probs", [P, 2, GH, TK, LQ])
        oT = sb("oT", [P, NG, LQ])
        qk_rows = oT[0:1, 0:2, :]
        qk_perm = oT[0:1, 2:4, :]
        with nc.sbuf_tensor("raw_late", [P, 5 * DC * D + 2 * FC * D], F32) as raw_late:
            raw_l1 = [raw_late[:, i * DC * D:(i + 1) * DC * D].rearrange("p (c n) -> p c n", c=DC) for i in range(5)]
            raw_c = raw_l1.pop()
            raw_f, raw_p = [raw_late[:, 5 * DC * D + i * FC * D:5 * DC * D + (i + 1) * FC * D] for i in range(2)]
            raw_f = raw_f.rearrange("p (c n) -> p c n", c=DC)
            raw_p = raw_p.rearrange("p (c n) -> p c n", c=FC)
        y = pair("y", [P, FC, LQ])
        pc = pair("pc", [P, TK, D])
        pT = pair("pT", [P, DC, LK])
        h = sb("h", [P, TQ, D])
        ln2 = sb("ln2", [P, TQ, 9])
        z2 = sb("z2", [P, TQ, D])
        pcx = sb("pcx", [P, TK, D])
        aT = pair("aT", [P, DC, LQ])
        rden = sb("rden", [P, TQ, H])
        fx2 = sb("fx2", [P, 2, 2 * LQ])
        stat1 = sb("stat1", [P, 4, TQ])
        sel = fx2[0:3 * GH].rearrange("p a n -> p (a n)").bitcast(BF16).rearrange("p (h n) -> p h n", h=GH)
        fx = [fx2[:, 0, :], fx2[:, 1, :], z2[:].rearrange("p c n -> p (c n)")]
        ft = [pcx[:, 0:2, :].rearrange("p k d -> p (k d)"), pcx[:, 2:4, :].rearrange("p k d -> p (k d)"),
              qf[:].rearrange("p c n -> p (c n)")]
        prob1 = pcx[:].rearrange("p (t k) d -> p t (k d)", t=TQ)
        p1T = [t[:, 0:TK, :] for t in y]
        mixT = [t[:, TK:TK + DC, :] for t in y]
        gT = [t[:, TK + DC:TK + 2 * DC, :] for t in y]

        raw_q, raw_k, raw_v = [probs[:, 1, 0, 0:2, :], probs[:, 1, 0, 2:4, :], probs[:, 1, 1, 0:2, :]]
        s1 = ps("s1", [P, 2, 512])
        s2 = ps("s2", [P, 2, 512])
        om = ps("om", [P, 512])
        pre_ps = ps("pre_ps", [P, 512])
        post_ps = ps("post_ps", [P, 2, 512])
        om_rows = om[:, LQ:LQ + LQ // 2].bitcast(BF16)

        vec_in, bias_in, bc_in = sem("vec_in"), sem("bias_in"), sem("bc_in")
        wq_in, wk_in, wv_in, wc_in = sem("wq_in"), sem("wk_in"), sem("wv_in"), sem("wc_in")
        l1_in, wf_in, wp_in = sem("l1_in"), sem("wf_in"), sem("wp_in")
        x_in, mask_in, cx_in = sem("x_in"), sem("mask_in"), sem("cx_in")
        h_in, pcx_in, h_free = sem("h_in"), sem("pcx_in"), sem("h_free")
        sel_in = sem("sel_in")
        pool_step = sem("pool_step")
        consts = sem("consts")
        dve_const = sem("dve_const")
        vec_ps, vec_done = sem("vec_ps"), sem("vec_done")
        bq_ps, bq_done, prep_ps, prep_done = sem("bq_ps"), sem("bq_done"), sem("prep_ps"), sem("prep_done")
        w_hi, w_lo = sem("w_hi"), sem("w_lo")
        prep_step, sel_done = sem("prep_step"), sem("sel_done")
        ln1_step, z1_done = sem("ln1_step"), sem("z1_done")
        rstd1, rstd2 = sem("rstd1"), sem("rstd2")
        pre_full, pre_free, pre_hi = sem("pre_full"), sem("pre_free"), sem("pre_hi")
        mask_done, row_done = sem("mask_done"), sem("row_done")
        qr_done, qm_done, q_parts = sem("qr_done"), sem("qm_done"), sem("q_parts")
        kh_done, kr_done, km_done, k_parts = (
            sem("kh_done"), sem("kr_done"), sem("km_done"), sem("k_parts"))
        stacked = [sem("stacked0"), sem("stacked1")]
        s1_full, s1_free = sem("s1_full"), sem("s1_free")
        s2_full, s2_free = sem("s2_full"), sem("s2_free")
        max_step, max_split, rows_ps, rows_in = sem("max_step"), sem("max_split"), sem("rows_ps"), sem("rows_in")
        pv_done, o_done = sem("pv_done"), sem("o_done")
        post_full = [sem("post_full0"), sem("post_full1")]
        post_free = [sem("post_free0"), sem("post_free1")]
        post_hi = sem("post_hi")
        cx_high, cx_split, xb_done, rden_done = sem("cx_high"), sem("cx_split"), sem("xb_done"), sem("rden_done")
        h1_done, ln2_step, z2_done, hb_done = sem("h1_done"), sem("ln2_step"), sem("z2_done"), sem("hb_done")
        square, cube, tanh_done = sem("square"), sem("cube"), sem("tanh_done")
        y_done, y_hi, y_split = sem("y_done"), sem("y_hi"), sem("y_split")
        max1, d_step = sem("max1"), sem("d_step")

        def await_(eng, s, n):
            if not isinstance(n, int) or n > 0:
                eng.wait_ge(s, n)

        def await_alone(eng, s, n):
            await_(eng, s, n)
            if not isinstance(n, int):
                eng.nop(nofuse=True)

        def post_use(b, n):
            return n % 2, POST_USES // 2 * b + n // 2 + 1

        def by_head(ap):
            return ap.rearrange("p (c h d) -> p c d h", c=DC, h=HC)

        def parts_of(ap):
            return ap.rearrange("p (c d h) -> p c d h", c=DC, h=HC)

        def chunk(i):
            return slice(i * P, (i + 1) * P)

        block = stack.enter_context(nc.Block())

        def run(eng, iteration, prologue, epilogue):
            prologue()
            iteration(0, True, False)
            with eng.Fori(1, B - 1) as b:
                iteration(b, False, False)
            iteration(B - 1, False, True)
            epilogue()

        def slots(b, last):
            for at in range(START, START + NS):
                ab = b + 1 if at >= NS else b
                yield at, ab, at % NS // SLOTS, at % SLOTS, not (last and at >= NS)

        def is_f(at):
            return POST_AT.get(at, "")[:1] == "F"

        def chunk_of(at):
            return int(POST_AT[at][1])

        def ahead(b, g):
            return (b, g + 1) if g + 1 < NG else (b + 1, 0)

        def behind(b, g):
            return (b, g - 1) if g > 0 else (b - 1, NG - 1)

        @block.sync
        def _(sp):
            def load_pre(b):
                await_alone(sp, pre_full, PRE_USES * (b - 1) + U_ZT + 1)
                sp.dma_start(xz[:], x[b].rearrange("(p t) d -> p t d", t=TQ)).then_inc(x_in, 16)
                await_alone(sp, row_done, b)
                sp.dma_start(mask_u[:], mask[b:b + 1, :].partition_broadcast(P) if isinstance(b, int)
                             else mask[bass.ds(b, 1), :].partition_broadcast(P)).then_inc(mask_in, 16)
                await_alone(sp, pre_full, PRE_USES * (b - 1) + U_CT + DC)
                sp.dma_start(cx[:], ctx[b].rearrange("(p k) d -> p k d", k=TK)).then_inc(cx_in, 16)

            def stack_heads(b, c):
                heads = slice(c * HC, (c + 1) * HC)
                await_alone(sp, s2_full, NS * (b - 1) + SLOTS * (2 * c + 2))
                await_alone(sp, q_parts, b + 1)
                for i, part in enumerate(TERMS_Q):
                    sp.dma_start(q_stack[i * HD:(i + 1) * HD, heads, :], qp[:, part, c, :]).then_inc(stacked[c], 16)
                await_alone(sp, row_done, b + 1)
                sp.dma_start(k_stack[ROW_MASK:ROW_MASK + 1, heads, :],
                             mask_row[0:1, :].unsqueeze(1).to_broadcast([1, HC, LK])).then_inc(stacked[c], 16)
                await_alone(sp, k_parts, 2 * b + c + 1)
                for i, part in enumerate(TERMS_K):
                    sp.dma_start(k_stack[i * HD:(i + 1) * HD, heads, :], kp[:, part, c, :]).then_inc(stacked[c], 16)

            def prologue():
                sp.dma_start(xz[:], x[0].rearrange("(p t) d -> p t d", t=TQ)).then_inc(x_in, 16)
                sp.dma_start(cx[:], ctx[0].rearrange("(p k) d -> p k d", k=TK)).then_inc(cx_in, 16)
                sp.dma_start(raw_q, q_w.rearrange("(c p) n -> p c n", p=P)).then_inc(wq_in, 16)
                row = 0
                for v in (ln1_w, ln1_b, v_b, ln2_w, ln2_b, fc_b):
                    n = v.shape[0] // P
                    sp.dma_start(vec_rows[row:row + n, :], v.rearrange("(r p) -> r p", p=P)).then_inc(vec_in, 16)
                    row += n
                for i, v in enumerate((q_b, k_b)):
                    sp.dma_start(qk_rows[:, i, :], v.rearrange("(o n) -> o n", o=1)).then_inc(bias_in, 16)
                sp.dma_start(raw_k, k_w.rearrange("(c p) n -> p c n", p=P)).then_inc(wk_in, 16)
                sp.dma_start(mask_u[:], mask[0:1, :].partition_broadcast(P)).then_inc(mask_in, 16)
                sp.dma_start(raw_v, v_w.rearrange("(c p) n -> p c n", p=P)).then_inc(wv_in, 16)
                sp.wait_ge(consts, 2)
                for g in range(NG):
                    sp.dma_start(k_stack[ROW_MAX:ROWS, g * GH:(g + 1) * GH, :], sel[:]).then_inc(sel_in, 16)
                stack_heads(0, 0)
                for t, w in zip(raw_l1, (l1_q, l1_k, l1_v, l1_o)):
                    sp.dma_start(t, w.rearrange("(c p) n -> p c n", p=P)).then_inc(l1_in, 16)
                sp.dma_start(raw_c, cproj_w.rearrange("(c p) n -> p c n", p=P)).then_inc(wc_in, 16)
                sp.dma_start(raw_f, fc_w.rearrange("(c p) n -> p c n", p=P)).then_inc(wf_in, 16)
                sp.dma_start(cb[:], cproj_b.rearrange("(o n) -> o n", o=1).partition_broadcast(P)).then_inc(bc_in, 16)
                sp.dma_start(pb[:], proj_b.rearrange("(o n) -> o n", o=1).partition_broadcast(P)).then_inc(bc_in, 16)
                sp.dma_start(alpha_c[:], alpha.partition_broadcast(P)).then_inc(bc_in, 16)
                sp.dma_start(raw_p, proj_w.rearrange("(c p) n -> p c n", p=P)).then_inc(wp_in, 16)

            def iteration(b, first, last):
                if not last:
                    load_pre(b + 1)
                stack_heads(b, 1)
                if not last:
                    stack_heads(b + 1, 0)

            def epilogue():
                sp.wait_ge(h_free, 16 * (B + 1))

            run(sp, iteration, prologue, epilogue)

        @block.tensor
        def _(pe):
            def product(o, w, wi, v, vi, n, start=True, stop=True):
                for k in range(n):
                    for i, (a, c) in enumerate(((0, 0), (0, 1), (1, 0))):
                        mm = pe.matmul(o, wi(w[a], k), vi(v[c], k), start=start and k == 0 and i == 0,
                                       stop=stop and k == n - 1 and i == 2)
                return mm

            def products(terms, w, v, n, fresh, whole, start=True, stop=True):
                early, late = (((0, 0), (0, 1)), (1, 0)) if fresh is w else (((0, 0), (1, 0)), (0, 1))
                for i, (o, wi, vi) in enumerate(terms):
                    for k in range(n):
                        for a, c in early:
                            pe.matmul(o, wi(w[a], k), vi(v[c], k), start=start and i == k == a == c == 0, stop=False)
                whole()
                for i, (o, wi, vi) in enumerate(terms):
                    for k in range(n):
                        mm = pe.matmul(o, wi(w[late[0]], k), vi(v[late[1]], k), start=False,
                                       stop=stop and i == len(terms) - 1 and k == n - 1)
                return mm

            def pre(b, n):
                await_(pe, pre_free, PRE_USES * b + n)
                if n == U_ZT:
                    pe.wait_ge(z1_done, b + 1)
                    for c in range(DC):
                        for t in range(TQ):
                            mm = pe.transpose(pre_ps[:, c * LQ + t * P:c * LQ + (t + 1) * P], xz[:, t, chunk(c)], ident[:])
                elif n < U_Q:
                    c = n - U_CT
                    pe.wait_ge(cx_in, 16 * (b + 1))
                    for k in range(TK):
                        mm = pe.transpose(pre_ps[:, chunk(k)], cx[:, k, chunk(c)], ident[:])
                elif n == U_Q:
                    for c in range(DC):
                        mm = product(pre_ps[:, c * LQ:(c + 1) * LQ], wq, lambda w, k: w[:, k, chunk(c)],
                                     zT, lambda v, k: v[:, k, :], DC)
                elif n < U_V:
                    c = n - U_K
                    mm = product(pre_ps[:], wk, lambda w, k: w[:, k, chunk(c)],
                                 cT, lambda v, k: v[:, k, :], DC)
                else:
                    for i in range(2):
                        t = 2 * (n - U_V) + i
                        mm = product(pre_ps[:, i * D:(i + 1) * D], cT, lambda v, k: v[:, k, chunk(t)],
                                     wv, lambda w, k: w[:, k, :], DC)
                mm.then_inc(pre_full, 1)

            def max_tile(b, g, s):
                hd, t = g * GH + s // 2, s % 2
                if s == 0:
                    pe.wait_ge(stacked[g // 2], 16 * STACK_DMAS * (b + 1))
                n = NS * b + SLOTS * g + s
                await_(pe, s1_free, n - 1)
                pe.matmul(s1[:, s % 2, :], q_stack[0:ROW_MAX, hd, chunk(t)], k_stack[0:ROW_MAX, hd, :],
                          start=True, stop=True).then_inc(s1_full, 1)

            def max_rows(b, g):
                pe.wait_ge(max_split, NG * b + g + 1)
                await_(pe, o_done, NG * b + g - 1)
                for t in range(TQ):
                    mm = pe.transpose(om_rows[0:ROWS, chunk(t)], max_cols[:, t, :], ident_b[:])
                mm.then_inc(rows_ps, 1)

            def exp_tile(b, g, s):
                hd = g * GH + s // 2
                n = NS * b + SLOTS * g + s
                await_(pe, s2_free, n - 1)
                for i in range(2):
                    k = 2 * (s % 2) + i
                    mm = pe.matmul(s2[:, s % 2, i * LQ:(i + 1) * LQ], k_stack[:, hd, chunk(k)], q_stack[:, hd, :],
                                   start=True, stop=True)
                mm.then_inc(s2_full, 1)

            def pv(b, g, k):
                if k == 0:
                    await_(pe, s2_free, NS * b + SLOTS * (g + 1))
                    pe.wait_ge(pre_free, PRE_USES * (b + 1))
                for j in range(GH):
                    mm = pe.matmul(om[32 * j:32 * j + VW, 0:LQ], vals[:, k, g * GH + j, :], probs[:, g % 2, j, k, :],
                                   start=k == 0, stop=k == TK - 1)
                if k == TK - 1:
                    mm.then_inc(pv_done, 1)

            def post(b, step):
                def open_(n):
                    bank, count = post_use(b, n)
                    await_(pe, post_free[bank], count)
                    return post_ps[:, bank, :]

                def ready(n):
                    bank, count = post_use(b, n)
                    pe.wait_ge(post_free[bank], count + 1)

                def ready_high(n):
                    pe.wait_ge(post_hi, len(POST_SPLITS) * b + POST_SPLITS.index(n) + 1)

                def fill(mm, n):
                    mm.then_inc(post_full[n % 2], 1)

                if step in ("CT0", "CT1"):
                    c = int(step[2])
                    pe.wait_ge(pcx_in, 16 * (b + 1))
                    o = open_(W_CT + c)
                    for k in range(TK):
                        mm = pe.transpose(o[:, chunk(k)], pcx[:, k, chunk(c)], ident[:])
                    fill(mm, W_CT + c)
                elif step == "OT":
                    pe.wait_ge(o_done, NG * (b + 1))
                    for t in range(TQ):
                        o = open_(W_OT + t)
                        for g in range(NG):
                            mm = pe.transpose(o[:, chunk(g)], oT[:, g, chunk(t)], ident[:])
                        fill(mm, W_OT + t)
                elif step in ("NT", "ZT", "HT"):
                    n = {"NT": W_NT, "ZT": W_ZT, "HT": W_HT}[step]
                    src = {"NT": z2, "ZT": z2, "HT": h}[step]
                    if step == "NT":
                        ready(W_OT)
                        ready(W_OT + 1)
                    elif step == "ZT":
                        pe.wait_ge(z2_done, b + 1)
                    else:
                        ready(W_PJ)
                    o = open_(n)
                    for c in range(DC):
                        for t in range(TQ):
                            mm = pe.transpose(o[:, c * LQ + t * P:c * LQ + (t + 1) * P], src[:, t, chunk(c)], ident[:])
                    fill(mm, n)
                elif step in ("CP", "DL"):
                    n, act, w, src = (W_CP, aT, wc, W_NT) if step == "CP" else (W_DL, mixT, wo, W_PC)
                    ready_high(src)
                    o = open_(n)
                    mm = products([(o[:, t * D:(t + 1) * D], lambda v, k, t=t: v[:, k, chunk(t)], lambda v, k: v[:, k, :])
                                   for t in range(TQ)], act, w, DC, act, lambda: ready(src))
                    fill(mm, n)
                elif step[0] == "F":
                    i = int(step[1])
                    ready_high(W_ZT)
                    o = open_(W_F + i)
                    mm = products([(o[:, j * LQ:(j + 1) * LQ], lambda w, k, f=2 * i + j: w[:, k, chunk(f)],
                                    lambda v, k: v[:, k, :]) for j in range(2)], wf, aT, DC, aT, lambda: ready(W_ZT))
                    fill(mm, W_F + i)
                elif step[:2] == "PJ":
                    i = int(step[2])
                    pe.wait_ge(y_hi, 4 * b + i + 1)
                    o = open_(W_PJ) if i == 0 else post_ps[:, W_PJ % 2, :]
                    mm = products([(o[:, t * D:(t + 1) * D], lambda v, k, t=t: v[:, k + 2 * i, chunk(t)],
                                    lambda v, k: v[:, k + 2 * i, :]) for t in range(TQ)], y, wp, 2, y,
                                  lambda: pe.wait_ge(y_split, 4 * b + i + 1), start=i == 0, stop=i == 3)
                    if i == 3:
                        fill(mm, W_PJ)
                elif step == "G":
                    ready_high(W_HT)
                    o = open_(W_G)
                    mm = products([(o[:, c * LQ:(c + 1) * LQ], lambda w, k, c=c: w[:, k, chunk(c)], lambda v, k: v[:, k, :])
                                   for c in range(DC)], wa, aT, DC, aT, lambda: ready(W_HT))
                    fill(mm, W_G)
                elif step in ("S0", "S1"):
                    t = int(step[1])
                    ready_high(W_G)
                    o = open_(W_S + t)
                    mm = products([(o, lambda v, k: v[:, k, chunk(t)], lambda v, k: v[:, k, :])], gT, pT, DC, gT,
                                  lambda: ready(W_G))
                    fill(mm, W_S + t)
                elif step in ("PT0", "PT1"):
                    i = int(step[2])
                    ready(W_S)
                    ready(W_S + 1)
                    o = open_(W_PT + i)
                    for j in range(2):
                        for t in range(TQ):
                            mm = pe.transpose(o[:, j * LQ + t * P:j * LQ + (t + 1) * P],
                                              prob1[:, t, chunk(2 * i + j)], ident[:])
                    fill(mm, W_PT + i)
                elif step == "PC":
                    pe.wait_ge(cx_split, b + 1)
                    o = open_(W_PC)
                    ready_high(W_PT + 1)
                    mm = products([(o[:, c * LQ:(c + 1) * LQ], lambda v, k, c=c: v[:, k, chunk(c)], lambda v, k: v[:, k, :])
                                   for c in range(DC)], pc, p1T, TK, p1T, lambda: ready(W_PT + 1))
                    fill(mm, W_PC)

            def prepare(step):
                if step == "WA":
                    pe.wait_ge(l1_in, 16 * 4)
                    for c in range(DC):
                        for k in range(DC):
                            mm = pe.matmul(post_ps[:, 0, c * D:(c + 1) * D], raw_l1[0][:, k, chunk(c)], raw_l1[1][:, k, :],
                                           start=k == 0, stop=k == DC - 1)
                    mm.then_inc(prep_ps, 1)
                elif step == "WT":
                    for c in range(DC):
                        for k in range(DC):
                            mm = pe.transpose(post_ps[:, 1, c * D + k * P:c * D + (k + 1) * P], raw_l1[3][:, k, chunk(c)], ident[:])
                    mm.then_inc(prep_ps, 1)
                elif step == "CB":
                    pe.wait_ge(wc_in, 16)
                    pe.wait_ge(prep_step, 1)
                    pe.wait_ge(prep_done, 1)
                    for k in range(DC):
                        pe.matmul(post_ps[:, 1, 0:D], h[:, k, 0:P], raw_c[:, k, :], start=k == 0, stop=k == DC - 1)
                    pe.wait_ge(wf_in, 16)
                    for f in range(FC):
                        for k in range(DC):
                            mm = pe.matmul(post_ps[:, 1, D + f:D + f + 1], raw_f[:, k, chunk(f)],
                                           vecs[:, V_LN2B + k:V_LN2B + k + 1], start=k == 0, stop=k == DC - 1)
                    mm.then_inc(prep_ps, 1)
                elif step == "WO":
                    pe.wait_ge(w_lo, 4)
                    for c in range(DC):
                        for k in range(DC):
                            mm = pe.matmul(post_ps[:, 0, c * D:(c + 1) * D], raw_l1[2][:, k, chunk(c)], z2[:, k, :],
                                           start=k == 0, stop=k == DC - 1)
                    mm.then_inc(prep_ps, 1)
                elif step == "END":
                    pe.wait_ge(prep_done, 2)
                    pe.wait_ge(w_lo, 10)

            def prologue():
                pe.wait_ge(consts, 1)
                pre(0, U_CT)
                pe.wait_ge(vec_in, 16 * 6)
                pe.transpose(s2[:, 0, 0:VECS], vec_rows[:], ident[0:VECS, 0:VECS]).then_inc(vec_ps, 1)
                pe.wait_ge(wq_in, 16)
                pe.wait_ge(vec_done, 2)
                for k in range(DC):
                    mm = pe.matmul(s2[0:1, 1, 0:D], vecs[:, V_LN1B + k:V_LN1B + k + 1], raw_q[:, k, :],
                                   start=k == 0, stop=k == DC - 1)
                mm.then_inc(bq_ps, 1)
                pre(0, U_CT + 1)
                pe.wait_ge(bq_done, 2)
                for i in range(2 * DC):
                    mm = pe.matmul(s2[:, 1, D + i:D + i + 1], qk_perm[:, i // DC, chunk(i % DC)], ident[0:1, 0:1],
                                   start=True, stop=True)
                mm.then_inc(bq_ps, 1)
                pre(0, U_ZT)
                pe.wait_ge(w_lo, 1)
                pre(0, U_Q)
                pe.wait_ge(w_lo, 2)
                pre(0, U_K)
                pre(0, U_K + 1)
                pe.wait_ge(w_lo, 3)
                pre(0, U_V)
                pre(0, U_V + 1)
                pe.wait_ge(sel_in, 16 * NG)
                for s in range(SLOTS):
                    max_tile(0, 0, s)
                max_rows(0, 0)
                for s in range(START):
                    attend(0, 0, s, 0)
                    attend(0, 0, s, 1)

            def attend(b, g, s, part):
                if part == 0:
                    nb, ng = ahead(b, g)
                    if not (isinstance(nb, int) and nb == B):
                        for i in MAX_TILES[s]:
                            max_tile(nb, ng, i)
                else:
                    pb_, pg = behind(b, g)
                    if s == 0:
                        pe.wait_ge(rows_in, NG * b + g + 1)
                    if s < TK and not (isinstance(pb_, int) and pb_ < 0):
                        pv(pb_, pg, s)
                    exp_tile(b, g, s)
                    nb, ng = ahead(b, g)
                    if s == ROWS_AT and not (isinstance(nb, int) and nb == B):
                        max_rows(nb, ng)

            def iteration(b, first, last):
                for at, ab, g, s, attends in slots(b, last):
                    if attends:
                        attend(ab, g, s, 0)
                    if not last and at in PRE_AT:
                        pre(b + 1, PRE_AT[at])
                    if not last and at in V_AT:
                        pre(b + 1, U_V + V_AT[at])
                    if not first and at in POST_AT:
                        post(b - 1, POST_AT[at])
                    if first and at in PREP_AT:
                        prepare(PREP_AT[at])
                    if attends:
                        attend(ab, g, s, 1)

            def epilogue():
                for k in range(TK):
                    pv(B - 1, NG - 1, k)
                for step in POST_AT.values():
                    post(B - 1, step)

            run(pe, iteration, prologue, epilogue)

        @block.scalar
        def _(act):
            def pre(b, n):
                if U_K <= n < U_V:
                    return
                act.wait_ge(pre_full, PRE_USES * b + n + 1)
                if n < U_Q:
                    dst = zT[0][:].rearrange("p c n -> p (c n)") if n == U_ZT else cT[0][:, n - U_CT, :]
                    act.activation(dst, pre_ps[:], ACT.Copy).then_inc(pre_hi, 1)
                elif n == U_Q:
                    await_(act, stacked[0], 16 * STACK_DMAS * b)
                    await_(act, stacked[1], 16 * STACK_DMAS * b)
                    await_(act, q_parts, b)
                    for c in range(DC):
                        act.activation(qf[:, c, :], pre_ps[:, c * LQ:(c + 1) * LQ], ACT.Identity, bias=bq[:, c:c + 1])
                    for c in range(DC):
                        a = act.activation(qp[:, 0, c, :], pre_ps[:, c * LQ:(c + 1) * LQ], ACT.Identity, bias=bq[:, c:c + 1])
                    a.then_inc(pre_free, 1)
                elif n >= U_V:
                    i = n - U_V
                    await_(act, pv_done, NG * b)
                    act.activation(vals[:, 2 * i:2 * i + 2, :, 0:HD],
                                   pre_ps[:].rearrange("p (t h d) -> p t h d", t=2, h=H), ACT.Copy).then_inc(pre_free, 1)

            def query_middle(b):
                act.wait_ge(qr_done, b + 1)
                act.activation(qp[:, 1, :, :], qf[:], ACT.Copy).then_inc(qm_done, 1)

            def key_high(b, c):
                await_(act, stacked[c], 16 * STACK_DMAS * b)
                act.wait_ge(pre_free, PRE_USES * b + U_K + c + 1)
                act.activation(kp[:, 0, c, :], kf[:], ACT.Copy).then_inc(kh_done, 1)

            def key_middle(b, c):
                act.wait_ge(kr_done, 2 * b + c + 1)
                act.activation(kp[:, 1, c, :], kf[:], ACT.Copy).then_inc(km_done, 1)

            def rows(b, g):
                act.wait_ge(rows_ps, NG * b + g + 1)
                act.activation(q_stack[ROW_MASK:ROWS, g * GH:(g + 1) * GH, :],
                               om_rows[ROW_MASK:ROWS, :].unsqueeze(1).to_broadcast([ROWS - ROW_MASK, GH, LQ]),
                               ACT.Copy).then_inc(rows_in, 1)

            def exp(b, g, s):
                if s == 0:
                    await_(act, pv_done, NG * b + g - 1)
                act.wait_ge(s2_full, NS * b + SLOTS * g + s + 1)
                k = 2 * (s % 2)
                act.activation(probs[:, g % 2, s // 2, k:k + 2, :],
                               s2[:, s % 2, :].rearrange("p (k n) -> p k n", k=2), ACT.Exp).then_inc(s2_free, 1)

            def o_out(b, g):
                act.wait_ge(pv_done, NG * b + g + 1)
                act.activation(oT[:, g, :], om[:, 0:LQ], ACT.Copy).then_inc(o_done, 1)

            def post(b, step):
                def full(n):
                    bank, count = post_use(b, n)
                    act.wait_ge(post_full[bank], count)
                    return post_ps[:, bank, :]

                def high(dst, n):
                    act.activation(dst.rearrange("p c n -> p (c n)"), full(n), ACT.Copy).then_inc(post_hi, 1)

                if step in ("CT0", "CT1"):
                    c = int(step[2])
                    act.activation(pT[0][:, c, :], full(W_CT + c), ACT.Copy).then_inc(post_hi, 1)
                elif step in ("NT", "ZT", "HT"):
                    high(aT[0][:], {"NT": W_NT, "ZT": W_ZT, "HT": W_HT}[step])
                elif step[0] == "F":
                    i = int(step[1])
                    ps_ = full(W_F + i)
                    if i == 3:
                        act.wait_ge(y_split, 4 * b + 1)
                    for j in range(2):
                        a = act.activation(fx[i % 3][:, j * LQ:(j + 1) * LQ], ps_[:, j * LQ:(j + 1) * LQ], ACT.Identity,
                                           bias=bf[:, 2 * i + j:2 * i + j + 1])
                    a.then_inc(post_free[(W_F + i) % 2], 1)
                elif step == "G":
                    high(gT[0], W_G)
                elif step in ("PT0", "PT1"):
                    i = int(step[2])
                    high(p1T[0][:, 2 * i:2 * i + 2, :], W_PT + i)
                elif step == "PC":
                    high(mixT[0], W_PC)

            def exp1(b, t):
                bank, count = post_use(b, W_S + t)
                act.wait_ge(post_full[bank], count)
                act.wait_ge(max1, 2 * b + t + 1)
                act.wait_ge(cx_split, b + 1)
                act.activation(prob1[:, t, :], post_ps[:, bank, :], ACT.Exp, bias=stat1[:, 0, t:t + 1],
                               accum_out=stat1[:, 1, t:t + 1]).then_inc(post_free[bank], 1)

            def gelu_tanh(b, i):
                act.wait_ge(cube, 4 * b + i + 1)
                act.activation(ft[i % 3], ft[i % 3], ACT.Tanh, scale=GELU_SCALE * GELU_CUBIC).then_inc(tanh_done, 1)

            def gelu_high(b, i):
                act.wait_ge(y_done, 4 * b + i + 1)
                act.activation(y[0][:, 2 * i:2 * i + 2, :].rearrange("p c n -> p (c n)"), fx[i % 3], ACT.Copy)\
                   .then_inc(y_hi, 1)

            def post_slot(b, at):
                if is_f(at - GELU_SPLIT):
                    gelu_high(b, chunk_of(at - GELU_SPLIT))
                if at in POST_AT:
                    post(b, POST_AT[at])
                if at == CX_HIGH_AT:
                    act.wait_ge(pcx_in, 16 * (b + 1))
                    act.activation(pc[0][:], pcx[:], ACT.Copy).then_inc(cx_high, 1)
                if is_f(at - GELU_TANH):
                    gelu_tanh(b, chunk_of(at - GELU_TANH))

            def post_slot_end(b, at):
                if POST_AT.get(at - 1) in ("S0", "S1"):
                    exp1(b, int(POST_AT[at - 1][1]))

            def pre_slot_end(b, at):
                if PRE_AT.get(at - 2) == U_Q:
                    query_middle(b)
                if PRE_AT.get(at - 1, 0) >= U_K:
                    key_high(b, PRE_AT[at - 1] - U_K)
                if PRE_AT.get(at - 2, 0) >= U_K:
                    key_middle(b, PRE_AT[at - 2] - U_K)

            def load_post(b):
                act.wait_ge(h_free, 16 * (b + 1))
                act.dma_start(h[:], x[b].rearrange("(p t) d -> p t d", t=TQ)).then_inc(h_in, 16)
                act.dma_start(pcx[:], ctx[b].rearrange("(p k) d -> p k d", k=TK)).then_inc(pcx_in, 16)

            def store(b):
                bank, count = post_use(b, W_DL)
                act.wait_ge(post_free[bank], count + 1)
                act.dma_start(out[b].rearrange("(p t) d -> p t d", t=TQ), h[:]).then_inc(h_free, 16)

            def prepare(step):
                if step == "WA":
                    act.wait_ge(prep_ps, 1)
                    act.activation(wa[0][:].rearrange("p c n -> p (c n)"), post_ps[:, 0, :], ACT.Copy, scale=L1_SCALE)\
                       .then_inc(w_hi, 1)
                elif step == "WO":
                    act.wait_ge(prep_ps, 4)
                    act.activation(wo[0][:].rearrange("p c n -> p (c n)"), post_ps[:, 0, :], ACT.Copy).then_inc(w_hi, 1)
                elif step == "WC":
                    act.wait_ge(wc_in, 16)
                    act.activation(wc[0][:], raw_c, ACT.Copy).then_inc(w_hi, 1)
                elif step[:2] == "WF":
                    k = int(step[2])
                    act.wait_ge(wf_in, 16)
                    act.activation(wf[0][:, k, :], raw_f[:, k, :], ACT.Copy, scale=vecs[:, V_LN2W + k:V_LN2W + k + 1])\
                       .then_inc(w_hi, 1)
                elif step[:2] == "WP":
                    half = slice(int(step[2]) * FC // 2, (int(step[2]) + 1) * FC // 2)
                    act.wait_ge(wp_in, 16)
                    act.activation(wp[0][:, half, :], raw_p[:, half, :], ACT.Copy, scale=0.5).then_inc(w_hi, 1)

            def prologue():
                pre(0, U_CT)
                act.wait_ge(wq_in, 16)
                act.wait_ge(vec_done, 2)
                for k in range(DC):
                    a = act.activation(parts_of(wq[0][:, k, :]), by_head(raw_q[:, k, :]), ACT.Copy, scale=lnq[:, k:k + 1])
                a.then_inc(w_hi, 1)
                for n in range(U_CT + 1, U_ZT + 1):
                    pre(0, n)
                act.wait_ge(wk_in, 16)
                for k in range(DC):
                    a = act.activation(parts_of(wk[0][:, k, :]), by_head(raw_k[:, k, :]), ACT.Copy)
                a.then_inc(w_hi, 1)
                act.wait_ge(sel_done, 1)
                act.activation(sel[:], sel_small[:].unsqueeze(2).to_broadcast([3 * GH, GH, LK]), ACT.Copy).then_inc(consts, 1)
                act.wait_ge(bq_done, 4)
                pre(0, U_Q)
                query_middle(0)
                key_high(0, 0)
                key_middle(0, 0)
                act.wait_ge(wv_in, 16)
                act.activation(wv[0][:], raw_v, ACT.Copy).then_inc(w_hi, 1)
                key_high(0, 1)
                key_middle(0, 1)
                pre(0, U_V)
                pre(0, U_V + 1)
                rows(0, 0)
                for s in range(START):
                    attend(0, 0, s)

            def attend(b, g, s):
                nb, ng = ahead(b, g)
                pb_, pg = behind(b, g)
                if s == O_AT and not (isinstance(pb_, int) and pb_ < 0):
                    o_out(pb_, pg)
                exp(b, g, s)
                if s == ROWS_AT and not (isinstance(nb, int) and nb == B):
                    rows(nb, ng)

            def iteration(b, first, last):
                for at, ab, g, s, attends in slots(b, last):
                    if not first and at == LOAD_AT:
                        load_post(b - 1)
                    if not last and at in PRE_AT:
                        pre(b + 1, PRE_AT[at])
                    if not last and at in V_AT:
                        pre(b + 1, U_V + V_AT[at])
                    if not first:
                        post_slot(b - 1, at)
                    elif at in PREP_AT:
                        prepare(PREP_AT[at])
                    if attends:
                        attend(ab, g, s)
                    if not last:
                        pre_slot_end(b + 1, at)
                    if not first:
                        post_slot_end(b - 1, at)
                    if not first and at == STORE_AT:
                        store(b - 1)

            def epilogue():
                o_out(B - 1, NG - 1)
                load_post(B - 1)
                for at in range(START, START + NS):
                    post_slot(B - 1, at)
                    post_slot_end(B - 1, at)
                store(B - 1)

            run(act, iteration, prologue, epilogue)

        @block.vector
        def _(dve):
            def norm_stats(src, st, step, b):
                for t in range(TQ):
                    i = dve.bn_stats(st[:, t, 0:6], src[:, t, :])
                i.then_inc(step, 1)
                await_alone(dve, step, 3 * b + 1)
                for t in range(TQ):
                    i = dve.bn_aggr(st[:, t, 6:8], st[:, t, 0:6])
                i.then_inc(step, 1)
                dve.wait_ge(step, 3 * b + 2)
                dve.tensor_scalar(st[:, :, 8], st[:, :, 7], EPS, None, ALU.add).then_inc(step, 1)

            def norm_apply(src, st, z, rstd, b, done):
                dve.wait_ge(rstd, b + 1)
                for t in range(TQ):
                    i = dve.tensor_scalar(z[:, t, :], src[:, t, :], st[:, t, 6:7], st[:, t, 8:9], ALU.subtract, ALU.mult)
                i.then_inc(done, 1)

            def take_mask(b):
                dve.wait_ge(mask_in, 16 * (b + 1))
                dve.tensor_copy(mask_f[:].rearrange("q (k p) -> q k p", k=TK),
                                mask_u[:].rearrange("q (p k) -> q k p", k=TK)).then_inc(mask_done, 1)

            def pre(b, n):
                if n < U_Q:
                    i = PRE_SPLITS.index(n)
                    dve.wait_ge(pre_hi, len(PRE_SPLITS) * b + i + 1)
                    j = 0 if n == U_ZT else n - U_CT
                    dst, hi = [t[:].rearrange("p c n -> p (c n)") if n == U_ZT else t[:, j, :]
                               for t in ((zT[1], zT[0]) if n == U_ZT else (cT[1], cT[0]))]
                    dve.tensor_tensor(dst, pre_ps[:], hi.bitcast(F32), ALU.subtract).then_inc(pre_free, 1)
                elif U_K <= n < U_V:
                    c = n - U_K
                    dve.wait_ge(pre_full, PRE_USES * b + n + 1)
                    dve.wait_ge(mask_done, b + 1)
                    await_(dve, k_parts, 2 * b + c)
                    dve.scalar_tensor_tensor(kf[:], pre_ps[:], bk[:, c:c + 1], mask_f[:], ALU.add, ALU.mult)\
                       .then_inc(pre_free, 1)

            def take_max(b, g, s):
                dve.wait_ge(s1_full, NS * b + SLOTS * g + s + 1)
                dve.tensor_reduce(neg_max[:, g % 2, s % 2, s // 2:s // 2 + 1], s1[:, s % 2, :], AX.X, ALU.max,
                                  negate=True).then_inc(s1_free, 1)

            def split_max(b, g):
                step = 3 * (NG * b + g)
                part = [max_cols[:, :, ROW_MAX + i:ROWS:3] for i in range(3)]
                neg = neg_max[:, g % 2, :, :]
                dve.wait_ge(s1_free, NS * b + SLOTS * (g + 1))
                await_(dve, rows_ps, NG * b + g)
                dve.tensor_copy(part[0], neg).then_inc(max_step, 1)
                dve.wait_ge(max_step, step + 1)
                dve.tensor_tensor(max_rest[:], neg, part[0], ALU.subtract).then_inc(max_step, 1)
                dve.wait_ge(max_step, step + 2)
                dve.tensor_copy(part[1], max_rest[:]).then_inc(max_step, 1)
                dve.wait_ge(max_step, step + 3)
                dve.tensor_tensor(part[2], max_rest[:], part[1], ALU.subtract).then_inc(max_split, 1)

            def post(b, step):
                def full(n):
                    bank, count = post_use(b, n)
                    dve.wait_ge(post_full[bank], count)
                    return post_ps[:, bank, :]

                def low(dst, hi, n):
                    dve.wait_ge(post_hi, len(POST_SPLITS) * b + POST_SPLITS.index(n) + 1)
                    dve.tensor_tensor(dst, post_ps[:, n % 2, :].rearrange("p (c n) -> p c n", c=dst.shape[1]),
                                      hi.bitcast(F32), ALU.subtract).then_inc(post_free[n % 2], 1)

                if step in ("CT0", "CT1"):
                    c = int(step[2])
                    low(pT[1][:, c:c + 1, :], pT[0][:, c:c + 1, :], W_CT + c)
                elif step == "OT":
                    for t in range(TQ):
                        o = full(W_OT + t).rearrange("p (h e) -> p h e", h=H)
                        dve.reciprocal(rden[:, t, :], o[:, :, HD]).then_inc(rden_done, 1)
                        dve.wait_ge(rden_done, 2 * b + t + 1)
                        dve.tensor_tensor(z2[:, t, :].rearrange("p (h d) -> p h d", h=H), o[:, :, 0:HD],
                                          rden[:, t, :].unsqueeze(2).to_broadcast([P, H, HD]), ALU.mult)\
                           .then_inc(post_free[(W_OT + t) % 2], 1)
                elif step in ("NT", "ZT", "HT"):
                    low(aT[1][:], aT[0][:], {"NT": W_NT, "ZT": W_ZT, "HT": W_HT}[step])
                elif step == "CP":
                    o = full(W_CP)
                    dve.wait_ge(xb_done, b + 1)
                    dve.tensor_tensor(h[:].rearrange("p t n -> p (t n)"), o, h[:].rearrange("p t n -> p (t n)"), ALU.add)\
                       .then_inc(post_free[W_CP % 2], 1)
                    bank, count = post_use(b, W_CP)
                    dve.wait_ge(post_free[bank], count + 1)
                    norm_stats(h, ln2, ln2_step, b)
                elif step == "PJ3":
                    o = full(W_PJ)
                    dve.wait_ge(hb_done, b + 1)
                    dve.tensor_tensor(h[:].rearrange("p t n -> p (t n)"), o, h[:].rearrange("p t n -> p (t n)"), ALU.add)\
                       .then_inc(post_free[W_PJ % 2], 1)
                elif step == "G":
                    low(gT[1], gT[0], W_G)
                elif step in ("S0", "S1"):
                    t = int(step[1])
                    dve.tensor_reduce(stat1[:, 0, t:t + 1], full(W_S + t), AX.X, ALU.max, negate=True).then_inc(max1, 1)
                elif step in ("PT0", "PT1"):
                    i = int(step[2])
                    low(p1T[1][:, 2 * i:2 * i + 2, :], p1T[0][:, 2 * i:2 * i + 2, :], W_PT + i)
                elif step == "PC":
                    low(mixT[1], mixT[0], W_PC)
                elif step == "DL":
                    for n in range(2):
                        bank, count = post_use(b, W_S + n)
                        dve.wait_ge(post_free[bank], count + 1)
                    dve.reciprocal(stat1[:, 2, :], stat1[:, 1, :]).then_inc(d_step, 1)
                    dve.wait_ge(d_step, 2 * b + 1)
                    dve.tensor_scalar(stat1[:, 3, :], stat1[:, 2, :], alpha_c[:, 0:1], None, ALU.mult).then_inc(d_step, 1)
                    dve.wait_ge(d_step, 2 * b + 2)
                    o = full(W_DL)
                    for t in range(TQ):
                        i = dve.scalar_tensor_tensor(h[:, t, :], o[:, t * D:(t + 1) * D], stat1[:, 3, t:t + 1], h[:, t, :],
                                                     ALU.mult, ALU.add)
                    i.then_inc(post_free[W_DL % 2], 1)

            def gelu_cube(b, i):
                f = ft[i % 3]
                dve.wait_ge(square, 4 * b + i + 1)
                dve.scalar_tensor_tensor(f, f, 1.0 / GELU_CUBIC, fx[i % 3], ALU.add, ALU.mult).then_inc(cube, 1)

            def gelu_y(b, i):
                dve.wait_ge(tanh_done, 4 * b + i + 1)
                dve.scalar_tensor_tensor(fx[i % 3], ft[i % 3], 1.0, fx[i % 3], ALU.add, ALU.mult)\
                   .then_inc(y_done, 1)

            def gelu_split(b, i):
                hi, lo = [t[:, 2 * i:2 * i + 2, :].rearrange("p c n -> p (c n)") for t in y]
                dve.wait_ge(y_hi, 4 * b + i + 1)
                dve.tensor_tensor(lo, fx[i % 3], hi.bitcast(F32), ALU.subtract).then_inc(y_split, 1)

            def low_weights(dst, src, hi, n):
                dve.wait_ge(w_hi, n)
                return dve.tensor_tensor(dst, src, hi.bitcast(F32), ALU.subtract).then_inc(w_lo, 1)

            def prepare(step):
                if step == "WA":
                    dve.wait_ge(w_hi, 4)
                    dve.scalar_tensor_tensor(wa[1][:].rearrange("p c n -> p (c n)"), post_ps[:, 0, :], L1_SCALE,
                                             wa[0][:].rearrange("p c n -> p (c n)").bitcast(F32), ALU.mult, ALU.subtract)\
                       .then_inc(w_lo, 1)
                elif step == "WT":
                    dve.wait_ge(prep_ps, 2)
                    dve.tensor_copy(z2[:].rearrange("p c n -> p (c n)"), post_ps[:, 1, :]).then_inc(prep_done, 1)
                elif step == "CB":
                    dve.wait_ge(bc_in, 48)
                    dve.wait_ge(prep_ps, 3)
                    dve.tensor_tensor(cb[:], post_ps[:, 1, 0:D], cb[:], ALU.add).then_inc(h_free, 16)
                    dve.tensor_tensor(bf[:], post_ps[:, 1, D:D + FC], vecs[:, V_FCB:VECS], ALU.add).then_inc(prep_done, 1)
                elif step == "WO":
                    low_weights(wo[1][:].rearrange("p c n -> p (c n)"), post_ps[:, 0, :],
                                wo[0][:].rearrange("p c n -> p (c n)"), 5)
                elif step == "WC":
                    low_weights(wc[1][:], raw_c, wc[0][:], 6)
                elif step[:2] == "WF":
                    k = int(step[2])
                    dve.wait_ge(w_hi, 7 + k)
                    dve.scalar_tensor_tensor(wf[1][:, k, :], raw_f[:, k, :], vecs[:, V_LN2W + k:V_LN2W + k + 1],
                                             wf[0][:, k, :].bitcast(F32), ALU.mult, ALU.subtract).then_inc(w_lo, 1)
                elif step[:2] == "WP":
                    half = slice(int(step[2]) * FC // 2, (int(step[2]) + 1) * FC // 2)
                    dve.wait_ge(w_hi, 9 + int(step[2]))
                    dve.scalar_tensor_tensor(wp[1][:, half, :], raw_p[:, half, :], 0.5, wp[0][:, half, :].bitcast(F32),
                                             ALU.mult, ALU.subtract).then_inc(w_lo, 1)

            def prologue():
                dve.memset(max_cols[:], 0.0).then_inc(dve_const, 1)
                dve.wait_ge(dve_const, 1)
                dve.memset(max_cols[:, :, ROW_MASK:ROW_MAX], 1.0).then_inc(dve_const, 1)
                dve.memset(om[:], 0.0).then_inc(post_free[0], 1)
                dve.memset(vals[:, :, :, HD:VW], 1.0).then_inc(post_free[1], 1)
                dve.wait_ge(x_in, 16)
                norm_stats(xz, ln1, ln1_step, 0)
                norm_apply(xz, ln1, xz, rstd1, 0, z1_done)
                pre(0, U_CT)
                dve.wait_ge(vec_ps, 1)
                dve.tensor_copy(vecs[:], s2[:, 0, 0:VECS]).then_inc(vec_done, 1)
                dve.wait_ge(vec_done, 1)
                dve.tensor_scalar(lnq[:], vecs[:, V_LN1W:V_LN1W + DC], Q_SCALE, None, ALU.mult).then_inc(vec_done, 1)
                dve.wait_ge(w_hi, 1)
                for k in range(DC):
                    for c in range(DC):
                        i = dve.scalar_tensor_tensor(
                            parts_of(wq[1][:, k, :])[:, c], by_head(raw_q[:, k, :])[:, c], lnq[:, k:k + 1],
                            parts_of(wq[0][:, k, :])[:, c].bitcast(F32), ALU.mult, ALU.subtract)
                i.then_inc(w_lo, 1)
                dve.wait_ge(bq_ps, 1)
                dve.wait_ge(bias_in, 32)
                dve.tensor_tensor(parts_of(qk_perm[:, 0, :]), by_head(s2[0:1, 1, 0:D]), by_head(qk_rows[:, 0, :]), ALU.add)\
                   .then_inc(bq_done, 1)
                dve.tensor_copy(parts_of(qk_perm[:, 1, :]), by_head(qk_rows[:, 1, :])).then_inc(bq_done, 1)
                for n in range(U_CT + 1, U_ZT + 1):
                    pre(0, n)
                dve.wait_ge(w_hi, 2)
                for k in range(DC):
                    i = dve.tensor_tensor(parts_of(wk[1][:, k, :]), by_head(raw_k[:, k, :]),
                                          parts_of(wk[0][:, k, :]).bitcast(F32), ALU.subtract)
                i.then_inc(w_lo, 1)
                dve.wait_ge(bq_ps, 2)
                dve.tensor_scalar(bq[:], s2[:, 1, D:D + DC], Q_SCALE, None, ALU.mult).then_inc(bq_done, 1)
                dve.tensor_copy(bk[:], s2[:, 1, D + DC:D + 2 * DC]).then_inc(bq_done, 1)
                take_mask(0)
                dve.memset(q_stack[ROW_MASK:ROWS, :, :], 1.0).then_inc(dve_const, 1)
                pre(0, U_K)
                pre(0, U_K + 1)
                low_weights(wv[1][:], raw_v, wv[0][:], 3)
                for s in range(SLOTS):
                    take_max(0, 0, s)
                split_max(0, 0)
                for s in range(START):
                    attend(0, 0, s)

            def attend(b, g, s):
                nb, ng = ahead(b, g)
                if not (isinstance(nb, int) and nb == B):
                    for i in MAX_TILES[s]:
                        take_max(nb, ng, i)
                    if s == SPLIT_AT:
                        split_max(nb, ng)

            def post_slot(b, at):
                if is_f(at - GELU_Y):
                    gelu_y(b, chunk_of(at - GELU_Y))
                if at - 1 in POST_AT:
                    post(b, POST_AT[at - 1])
                if POST_AT.get(at - 2) == "CP":
                    norm_apply(h, ln2, z2, rstd2, b, z2_done)

            def post_slot_end(b, at):
                if is_f(at - GELU_CUBE):
                    gelu_cube(b, chunk_of(at - GELU_CUBE))

            def pre_slot(b, at):
                if at == LN1_AT:
                    dve.wait_ge(x_in, 16 * (b + 1))
                    norm_stats(xz, ln1, ln1_step, b)
                elif at == LN1_AT + 1:
                    norm_apply(xz, ln1, xz, rstd1, b, z1_done)
                if at - 1 in PRE_AT:
                    if PRE_AT[at - 1] == U_Q:
                        take_mask(b)
                    pre(b, PRE_AT[at - 1])

            def iteration(b, first, last):
                for at, ab, g, s, attends in slots(b, last):
                    if not last:
                        pre_slot(b + 1, at)
                    if not first:
                        post_slot(b - 1, at)
                    elif at - 1 in PREP_AT:
                        prepare(PREP_AT[at - 1])
                    if attends:
                        attend(ab, g, s)
                    if not first:
                        post_slot_end(b - 1, at)

            def epilogue():
                for at in range(START, START + NS):
                    if is_f(at - GELU_SPLIT):
                        gelu_split(B - 1, chunk_of(at - GELU_SPLIT))
                    post_slot(B - 1, at)
                    post_slot_end(B - 1, at)

            run(dve, iteration, prologue, epilogue)

        @block.gpsimd
        def _(pool):
            def rstd(st, step, b, done):
                pool.wait_ge(step, 3 * b + 3)
                pool.tensor_tensor(st[:, :, 8], st[:, :, 8], minus_half[:], ALU.pow).then_inc(done, 1)

            def mask_row_of(b):
                await_alone(pool, mask_done, b + 1)
                for c in range(2):
                    await_alone(pool, stacked[c], 16 * STACK_DMAS * b)
                pool.tensor_scalar(mask_row[:], mask_f[0:1, :], -1.0, MASKED, ALU.add, ALU.mult).then_inc(row_done, 1)

            def query_rest(b):
                pool.wait_ge(pre_free, PRE_USES * b + U_Q + 1)
                pool.tensor_tensor(qf[:], qf[:], qp[:, 0, :, :], ALU.subtract).then_inc(qr_done, 1)

            def query_low(b):
                pool.wait_ge(qm_done, b + 1)
                pool.tensor_tensor(qp[:, 2, :, :], qf[:], qp[:, 1, :, :], ALU.subtract).then_inc(q_parts, 1)

            def key_rest(b, c):
                pool.wait_ge(kh_done, 2 * b + c + 1)
                pool.tensor_tensor(kf[:], kf[:], kp[:, 0, c, :], ALU.subtract).then_inc(kr_done, 1)

            def key_low(b, c):
                pool.wait_ge(km_done, 2 * b + c + 1)
                pool.tensor_tensor(kp[:, 2, c, :], kf[:], kp[:, 1, c, :], ALU.subtract).then_inc(k_parts, 1)

            def pre_slot(b, at):
                before = PRE_AT.get(at - 1, 0)
                two_before = PRE_AT.get(at - 2, 0)
                if before == U_Q:
                    query_rest(b)
                    mask_row_of(b)
                elif before >= U_K:
                    key_rest(b, before - U_K)
                if PRE_AT.get(at - 3) == U_Q:
                    query_low(b)
                if two_before >= U_K:
                    key_low(b, two_before - U_K)

            def post(b, step):
                if step == "NT":
                    pool.wait_ge(h_in, 16 * (b + 1))
                    pool.tensor_tensor(h[:], h[:], cb[:].unsqueeze(1).to_broadcast([P, TQ, D]), ALU.add).then_inc(xb_done, 1)
                elif step == "ZT":
                    pool.wait_ge(cx_high, b + 1)
                    pool.tensor_tensor(pc[1][:], pcx[:], pc[0][:].bitcast(F32), ALU.subtract).then_inc(cx_split, 1)
                elif step == "CP":
                    rstd(ln2, ln2_step, b, rstd2)
                elif step == "PJ0":
                    pool.wait_ge(z2_done, b + 1)
                    pool.tensor_tensor(h[:], h[:], pb[:].unsqueeze(1).to_broadcast([P, TQ, D]), ALU.add).then_inc(hb_done, 1)
                elif step[0] == "F":
                    i = int(step[1])
                    bank, count = post_use(b, W_F + i)
                    if i < 2:
                        pool.wait_ge(cx_split, b + 1)
                    elif i == 2:
                        pool.wait_ge(q_parts, min(b + 3, B) if isinstance(b, int) else b + 3)
                    pool.wait_ge(post_free[bank], count + 1)
                    pool.tensor_tensor(ft[i % 3], fx[i % 3], fx[i % 3], ALU.mult).then_inc(square, 1)

            def gelu_split(b, i):
                hi, lo = [t[:, 2 * i:2 * i + 2, :].rearrange("p c n -> p (c n)") for t in y]
                pool.wait_ge(y_hi, 4 * b + i + 1)
                pool.tensor_tensor(lo, fx[i % 3], hi.bitcast(F32), ALU.subtract).then_inc(y_split, 1)

            def post_slot(b, at):
                if is_f(at - GELU_SPLIT) and not (isinstance(b, int) and b == B - 1):
                    gelu_split(b, chunk_of(at - GELU_SPLIT))
                if at in POST_AT:
                    post(b, POST_AT[at])

            def prologue():
                pool.memset(ident[:], 0.0).then_inc(pool_step, 1)
                pool.memset(sel_small[:], 1.0).then_inc(pool_step, 1)
                pool.wait_ge(pool_step, 2)
                pool.affine_select(out=ident[:], in_=ident[:], compare_op=ALU.not_equal, fill=1.0, base=0,
                                   pattern=[[-1, P]], channel_multiplier=1).then_inc(pool_step, 1)
                pool.affine_select(out=sel_small[:], in_=sel_small[:], compare_op=ALU.is_ge, fill=0.0, base=0,
                                   pattern=[[-3, GH]], channel_multiplier=1).then_inc(pool_step, 1)
                pool.memset(minus_half[:], -0.5).then_inc(pool_step, 1)
                pool.wait_ge(pool_step, 5)
                pool.affine_select(out=sel_small[:], in_=sel_small[:], compare_op=ALU.is_ge, fill=0.0, base=2,
                                   pattern=[[3, GH]], channel_multiplier=-1).then_inc(sel_done, 1)
                pool.tensor_scalar(ident_b[:], ident[:], 1.0, None, ALU.mult).then_inc(consts, 1)
                rstd(ln1, ln1_step, 0, rstd1)
                pool.wait_ge(vec_done, 1)
                pool.tensor_scalar(h[:, :, 0:P], vecs[:, V_VB:V_VB + DC].unsqueeze(2).to_broadcast([P, DC, P]), 1.0, None, ALU.mult)\
                    .then_inc(prep_step, 1)
                mask_row_of(0)
                query_rest(0)
                query_low(0)
                for c in range(DC):
                    key_rest(0, c)
                    key_low(0, c)

            def iteration(b, first, last):
                for at in range(START, START + NS):
                    if not last and at == LN1_AT:
                        rstd(ln1, ln1_step, b + 1, rstd1)
                    if not first:
                        post_slot(b - 1, at)
                    if not last:
                        pre_slot(b + 1, at)

            def epilogue():
                for at in range(START, START + NS):
                    post_slot(B - 1, at)

            run(pool, iteration, prologue, epilogue)


_INS = ["x", "ctx_2048", "mask_BxS2_bf1", "L0_xattn_ln1_w", "L0_xattn_ln1_b", "L0_xattn_q_w", "L0_xattn_q_b",
        "L0_xattn_k_w", "L0_xattn_k_b", "L0_xattn_v_w", "L0_xattn_v_b", "L0_xattn_cproj_w", "L0_xattn_cproj_b",
        "L0_xattn_ln2_w", "L0_xattn_ln2_b", "L0_xattn_fc_w", "L0_xattn_fc_b", "L0_xattn_proj_w",
        "L0_xattn_proj_b", "L1_xattn_w_q", "L1_xattn_w_k", "L1_xattn_w_v", "L1_xattn_w_o", "L1_xattn_alpha"]


def kernel(**inputs):
    import numpy as _np
    import concourse.bacc as _bacc
    from concourse import mybir as _mybir
    from concourse.bass_utils import run_bass_kernel_spmd as _run

    nc = _bacc.Bacc("TRN2", target_bir_lowering=False, num_devices=1)
    arrays, args = {}, []
    for name in _INS:
        a = _np.ascontiguousarray(inputs[name])
        if a.dtype == _np.bool_:
            a = a.view(_np.uint8)
        if a.ndim == 0 or name.endswith("alpha"):
            a = a.reshape(1, 1)
        arrays[f"in_{name}_dram"] = a
        args.append(nc.dram_tensor(f"in_{name}_dram", a.shape, _mybir.dt.from_np(a.dtype), kind="ExternalInput").ap())
    args.append(nc.dram_tensor("out_0_dram", (B, LQ, D), _mybir.dt.float32, kind="ExternalOutput").ap())
    build(nc, *args)
    r = _run(nc, [arrays], core_ids=[0])
    return r.results[0]["out_0_dram"]
```

```python
from contextlib import ExitStack

import concourse.bass as bass
from concourse import mybir

F32 = mybir.dt.float32
F32R = mybir.dt.float32r
BF16 = mybir.dt.bfloat16
U8 = mybir.dt.uint8
ACT = mybir.ActivationFunctionType
ALU = mybir.AluOpType
AX = mybir.AxisListType

P = 128
B, LQ, D = 4, 256, 256
LK = 512
H, HD = 16, 16
INNER = 4 * D
EPS = 1e-5
GELU_SCALE = (2.0 / 3.141592653589793) ** 0.5
GELU_CUBIC = 0.044715
DC = D // P
TQ = LQ // P
TK = LK // P
FC = INNER // P
GH = 4
NG = H // GH
HC = P // HD
SLOTS = 8
VW = HD + 1
TERMS_Q = (0, 0, 1, 0, 1, 2)
TERMS_K = (0, 1, 0, 2, 1, 0)
ROW_MASK = len(TERMS_Q) * HD
ROW_MAX = ROW_MASK + 1
ROWS = ROW_MAX + 3 * GH
MASKED = 2.0 ** 126
Q_SCALE = HD ** -0.5
L1_SCALE = D ** -0.5
NS = NG * SLOTS

START = 7
U_CT, U_ZT, U_Q, U_K, U_V, PRE_USES = 0, 2, 3, 4, 6, 8
LN1_AT = 7
PRE_AT = {7: U_CT, 8: U_CT + 1, 9: U_ZT, 11: U_Q, 14: U_K, 22: U_K + 1}
V_AT = {36: 0, 38: 1}
POST_AT = {7: "OT", 8: "NT", 9: "CP", 11: "ZT", 13: "F0", 15: "F1", 16: "F2", 19: "F3", 20: "PJ0",
           21: "PJ1", 22: "CT0", 23: "PJ2", 24: "CT1", 25: "PJ3", 26: "CX", 27: "HT", 28: "G", 30: "S0",
           31: "S1", 33: "PT0", 34: "PT1", 36: "PC", 37: "DL"}
EARLY_AT = {7: U_CT, 8: U_CT + 1, 9: U_ZT, 10: U_Q, 14: U_K, 22: U_K + 1}
LATE_AT = {7: "OT", 8: "NT", 9: "CP", 12: "ZT", 13: "F0", 15: "F1", 16: "F2", 18: "PJ0", 19: "F3",
           21: "PJ1", 22: "CT0", 23: "PJ2", 24: "CT1", 25: "PJ3", 26: "CX", 27: "HT", 28: "G", 29: "S0",
           31: "S1", 33: "PT0", 34: "PT1", 36: "PC", 37: "DL"}
PREP_AT = {8: "WA", 10: "WT", 12: "CB", 13: "WO", 14: "WC", 16: "WF0", 18: "WF1", 24: "WP0", 26: "WP1",
           38: "END"}
PREP_LOW_AT = {11: "WT", 12: "WA", 13: "CB", 14: "WO", 15: "WC", 22: "WF0", 23: "WF1", 28: "WP1", 30: "WP0"}
GELU_CUBE, GELU_TANH, GELU_Y, GELU_SPLIT = 1, 2, 3, 4
LOAD_AT, STORE_AT = 8, 38
MAX_TILES = ((0, 1), (2, 3), (4,), (5,), (6,), (7,), (), ())
SPLIT_AT, ROWS_AT, O_AT = 5, 6, 5

(W_OT, W_NT, W_CP, W_ZT, W_F, W_PJ, W_CT, W_HT, W_G, W_S, W_PT, W_PC, W_DL) = 0, 2, 3, 4, 5, 9, 10, 12, 13, 14, 16, 18, 19
POST_BANK = (0, 1, 0, 1, 0, 1, 0, 1, 0, 1, 0, 0, 0, 1, 0, 1, 0, 1, 0, 1)
LAST_ORDER = [W_OT, W_OT + 1, W_NT, W_CP, W_CT, W_CT + 1, W_ZT, W_F, W_F + 1, W_F + 2, W_F + 3, W_PJ,
              W_HT, W_G, W_S, W_S + 1, W_PT, W_PT + 1, W_PC, W_DL]
LAST_AT = {7: "OT", 8: "NT", 9: "CP", 10: "CT0", 11: "CT1", 12: "ZT", 14: "F0", 15: "F1", 16: "F2",
           18: "F3", 19: "PJ0", 20: "PJ1", 21: "PJ2", 22: "PJ3", 23: "CX", 24: "HT", 25: "G", 26: "S0",
           27: "S1", 29: "PT0", 30: "PT1", 31: "PC", 32: "DL"}
POST_SPLITS = [W_NT, W_ZT, W_CT, W_CT + 1, W_HT, W_G, W_PT, W_PT + 1, W_PC]
PRE_SPLITS = [U_CT, U_CT + 1, U_ZT]
V_LN1W, V_LN1B, V_VB, V_LN2W, V_LN2B, V_FCB, VECS = 0, 2, 4, 6, 8, 10, 18
STACK_DMAS = 2 * len(TERMS_Q) + 1


def build(nc, x, ctx, mask, ln1_w, ln1_b, q_w, q_b, k_w, k_b, v_w, v_b, cproj_w, cproj_b, ln2_w, ln2_b,
          fc_w, fc_b, proj_w, proj_b, l1_q, l1_k, l1_v, l1_o, alpha, out):
    with ExitStack() as stack:
        def sb(name, shape, dt=F32):
            return stack.enter_context(nc.sbuf_tensor(name, shape, dt))

        def ps(name, shape):
            return stack.enter_context(nc.psum_tensor(name, shape, F32))

        def sem(name):
            return stack.enter_context(nc.semaphore(name))

        ident = sb("ident", [P, P])
        ident_b = sb("ident_b", [P, P], BF16)
        sel_small = sb("sel_small", [3 * GH, GH])
        def pair(name, shape):
            return sb(name + "_h", shape, F32R), sb(name + "_l", shape, F32R)
        wq = pair("wq", [P, DC, D])
        wk = pair("wk", [P, DC, D])
        wv = pair("wv", [P, DC, D])
        wc = pair("wc", [P, DC, D])
        wf = pair("wf", [P, DC, INNER])
        wp = pair("wp", [P, FC, D])
        wa = pair("wa", [P, DC, D])
        wo = pair("wo", [P, DC, D])
        vec_rows = sb("vec_rows", [VECS, P])
        vecs = sb("vecs", [P, VECS])
        lnq = sb("lnq", [P, DC])
        bq = sb("bq", [P, DC])
        bk = sb("bk", [P, DC])
        bf = sb("bf", [P, FC])
        cb = sb("cb", [P, D])
        pb = sb("pb", [P, D])
        alpha_c = sb("alpha_c", [P, 1])
        xz = sb("xz", [P, TQ, D])
        minus_half = sb("minus_half", [P, TQ])
        ln1 = sb("ln1", [P, TQ, 9])
        cx = sb("cx", [P, TK, D])
        zT = pair("zT", [P, DC, LQ])
        cT = pair("cT", [P, DC, LK])
        mask_u = sb("mask_u", [P, LK], U8)
        mask_f = sb("mask_f", [P, LK])
        mask_row = sb("mask_row", [1, LK], BF16)
        qf = sb("qf", [P, DC, LQ])
        qp = sb("qp", [P, 3, DC, LQ], BF16)
        kf = sb("kf", [P, LK])
        kp = sb("kp", [P, 3, DC, LK], BF16)
        q_stack = sb("q_stack", [ROWS, H, LQ], BF16)
        k_stack = sb("k_stack", [ROWS, H, LK], BF16)
        vals = sb("vals", [P, TK, H, VW])
        neg_max = sb("neg_max", [P, 2, TQ, GH])
        max_rest = sb("max_rest", [P, TQ, GH])
        max_cols = sb("max_cols", [P, TQ, ROWS], BF16)
        probs = sb("probs", [P, 2, GH, TK, LQ])
        oT = sb("oT", [P, NG, LQ])
        qk_rows = oT[0:1, 0:2, :]
        qk_perm = oT[0:1, 2:4, :]
        with nc.sbuf_tensor("raw_late", [P, 5 * DC * D + 2 * FC * D], F32) as raw_late:
            raw_l1 = [raw_late[:, i * DC * D:(i + 1) * DC * D].rearrange("p (c n) -> p c n", c=DC) for i in range(5)]
            raw_c = raw_l1.pop()
            raw_f, raw_p = [raw_late[:, 5 * DC * D + i * FC * D:5 * DC * D + (i + 1) * FC * D] for i in range(2)]
            raw_f = raw_f.rearrange("p (c n) -> p c n", c=DC)
            raw_p = raw_p.rearrange("p (c n) -> p c n", c=FC)
        y = pair("y", [P, FC, LQ])
        with nc.sbuf_tensor("ft2", [P, 2, 2 * LQ], F32) as ft2:
            pass
        pc = pair("pc", [P, TK, D])
        pT = pair("pT", [P, DC, LK])
        h = sb("h", [P, TQ, D])
        ln2 = sb("ln2", [P, TQ, 9])
        z2 = sb("z2", [P, TQ, D])
        pcx = sb("pcx", [P, TK, D])
        aT = pair("aT", [P, DC, LQ])
        rden = sb("rden", [P, TQ, H])
        fx2 = sb("fx2", [P, 2, 2 * LQ])
        stat1 = sb("stat1", [P, 4, TQ])
        sel = fx2[0:3 * GH].rearrange("p a n -> p (a n)").bitcast(BF16).rearrange("p (h n) -> p h n", h=GH)
        fx = [fx2[:, 0, :], fx2[:, 1, :], z2[:].rearrange("p c n -> p (c n)")]
        ft = [ft2[:, 0, :], ft2[:, 1, :],
              qf[:].rearrange("p c n -> p (c n)")]
        p1T = [t[:, 0:TK, :] for t in y]
        mixT = [t[:, TK:TK + DC, :] for t in y]
        gT = [t[:, TK + DC:TK + 2 * DC, :] for t in y]

        raw_q, raw_k, raw_v = [probs[:, 1, 0, 0:2, :], probs[:, 1, 0, 2:4, :], probs[:, 1, 1, 0:2, :]]
        s1 = ps("s1", [P, 2, 512])
        s2 = ps("s2", [P, 2, 512])
        om = ps("om", [P, 512])
        pre_ps = ps("pre_ps", [P, 512])
        post_ps = ps("post_ps", [P, 2, 512])
        om_rows = om[:, LQ:LQ + LQ // 2].bitcast(BF16)

        vec_in, bias_in, bc_in = sem("vec_in"), sem("bias_in"), sem("bc_in")
        wq_in, wk_in, wv_in, wc_in = sem("wq_in"), sem("wk_in"), sem("wv_in"), sem("wc_in")
        l1_in, wf_in, wp_in = sem("l1_in"), sem("wf_in"), sem("wp_in")
        x_in, mask_in, cx_in = sem("x_in"), sem("mask_in"), sem("cx_in")
        h_in, pcx_in, h_free = sem("h_in"), sem("pcx_in"), sem("h_free")
        last_h_in, last_cx_in = sem("last_h_in"), sem("last_cx_in")
        sel_in = sem("sel_in")
        pool_step = sem("pool_step")
        consts = sem("consts")
        dve_const = sem("dve_const")
        vec_ps, vec_done = sem("vec_ps"), sem("vec_done")
        bq_ps, bq_done, prep_ps, prep_done = sem("bq_ps"), sem("bq_done"), sem("prep_ps"), sem("prep_done")
        w_hi, w_lo = sem("w_hi"), sem("w_lo")
        prep_step, sel_done = sem("prep_step"), sem("sel_done")
        ln1_step, z1_done = sem("ln1_step"), sem("z1_done")
        rstd1, rstd2 = sem("rstd1"), sem("rstd2")
        pre_full, pre_free, pre_hi = sem("pre_full"), sem("pre_free"), sem("pre_hi")
        mask_done, row_done = sem("mask_done"), sem("row_done")
        qr_done, qm_done, q_parts = sem("qr_done"), sem("qm_done"), sem("q_parts")
        kh_done, kr_done, km_done, k_parts = (
            sem("kh_done"), sem("kr_done"), sem("km_done"), sem("k_parts"))
        stacked = [sem("stacked0"), sem("stacked1")]
        s1_full, s1_free = sem("s1_full"), sem("s1_free")
        s2_full, s2_free = sem("s2_full"), sem("s2_free")
        max_step, max_split, rows_ps, rows_in = sem("max_step"), sem("max_split"), sem("rows_ps"), sem("rows_in")
        pv_done, o_done = sem("pv_done"), sem("o_done")
        post_full = [sem("post_full0"), sem("post_full1")]
        post_free = [sem("post_free0"), sem("post_free1")]
        post_hi = sem("post_hi")
        cx_high, cx_split, xb_done, rden_done = sem("cx_high"), sem("cx_split"), sem("xb_done"), sem("rden_done")
        h1_done, ln2_step, z2_done, hb_done = sem("h1_done"), sem("ln2_step"), sem("z2_done"), sem("hb_done")
        square, cube, tanh_done = sem("square"), sem("cube"), sem("tanh_done")
        y_done, y_hi, y_split = sem("y_done"), sem("y_hi"), sem("y_split")
        max1, d_step = sem("max1"), sem("d_step")

        def await_(eng, s, n):
            if not isinstance(n, int) or n > 0:
                eng.wait_ge(s, n)

        def await_alone(eng, s, n):
            await_(eng, s, n)
            if not isinstance(n, int):
                eng.nop(nofuse=True)

        def is_last(b):
            return isinstance(b, int) and b == B - 1

        def bank_of(b, n):
            return POST_BANK[n] if not is_last(b) else LAST_ORDER.index(n) % 2

        def pre_bank(b, n):
            if isinstance(b, int) and b == 0:
                return (pre_ps[:], post_ps[:, 0, :], post_ps[:, 1, :])[n % 3]
            return pre_ps[:]

        def post_use(b, n):
            bank = bank_of(b, n)
            before = POST_BANK[:n] if not is_last(b) else [bank_of(b, m) for m in LAST_ORDER[:LAST_ORDER.index(n)]]
            return bank, POST_BANK.count(bank) * b + before.count(bank) + 1

        def split_count(b, n):
            splits = POST_SPLITS if not is_last(b) else [m for m in LAST_ORDER if m in POST_SPLITS]
            return len(POST_SPLITS) * b + splits.index(n) + 1

        def by_head(ap):
            return ap.rearrange("p (c h d) -> p c d h", c=DC, h=HC)

        def parts_of(ap):
            return ap.rearrange("p (c d h) -> p c d h", c=DC, h=HC)

        def chunk(i):
            return slice(i * P, (i + 1) * P)

        block = stack.enter_context(nc.Block())

        def run(eng, iteration, prologue, epilogue):
            prologue()
            iteration(0, True, False)
            with eng.Fori(1, B - 1) as b:
                iteration(b, False, False)
            iteration(B - 1, False, True)
            epilogue()

        def slots(b, last):
            for at in range(START, START + NS):
                ab = b + 1 if at >= NS else b
                yield at, ab, at % NS // SLOTS, at % SLOTS, not (last and at >= NS)

        def residual(b):
            return xz if is_last(b) else h

        def context(b):
            return cx if is_last(b) else pcx

        def probs1(b):
            return context(b)[:].rearrange("p (t k) d -> p t (k d)", t=TQ)

        def wait_residual(eng, b):
            eng.wait_ge(*((last_h_in, 16) if is_last(b) else (h_in, 16 * (b + 1))))

        def wait_context(eng, b):
            eng.wait_ge(*((last_cx_in, 16) if is_last(b) else (pcx_in, 16 * (b + 1))))

        def steps_at(b):
            return LAST_AT if is_last(b) else LATE_AT if isinstance(b, int) and b == B - 2 else POST_AT

        def pre_at(b):
            return EARLY_AT if isinstance(b, int) and b == 1 else PRE_AT

        def is_f(b, at):
            return steps_at(b).get(at, "")[:1] == "F"

        def chunk_of(b, at):
            return int(steps_at(b)[at][1])

        def ahead(b, g):
            return (b, g + 1) if g + 1 < NG else (b + 1, 0)

        def behind(b, g):
            return (b, g - 1) if g > 0 else (b - 1, NG - 1)

        @block.sync
        def _(sp):
            def load_pre(b):
                await_alone(sp, pre_full, PRE_USES * (b - 1) + U_ZT + 1)
                sp.dma_start(xz[:], x[b].rearrange("(p t) d -> p t d", t=TQ)).then_inc(x_in, 16)
                await_alone(sp, row_done, b)
                sp.dma_start(mask_u[:], mask[b:b + 1, :].partition_broadcast(P) if isinstance(b, int)
                             else mask[bass.ds(b, 1), :].partition_broadcast(P)).then_inc(mask_in, 16)
                await_alone(sp, pre_full, PRE_USES * (b - 1) + U_CT + DC)
                sp.dma_start(cx[:], ctx[b].rearrange("(p k) d -> p k d", k=TK)).then_inc(cx_in, 16)

            def stack_heads(b, c):
                heads = slice(c * HC, (c + 1) * HC)
                await_alone(sp, s2_full, NS * (b - 1) + SLOTS * (2 * c + 2))
                made = ((pre_free, PRE_USES * b + U_Q + 1), (qm_done, b + 1), (q_parts, b + 1))
                for part, (sem_, n) in enumerate(made):
                    await_alone(sp, sem_, n)
                    for i in [i for i, p in enumerate(TERMS_Q) if p == part]:
                        sp.dma_start(q_stack[i * HD:(i + 1) * HD, heads, :], qp[:, part, c, :]).then_inc(stacked[c], 16)
                await_alone(sp, row_done, b + 1)
                sp.dma_start(k_stack[ROW_MASK:ROW_MASK + 1, heads, :],
                             mask_row[0:1, :].unsqueeze(1).to_broadcast([1, HC, LK])).then_inc(stacked[c], 16)
                made = ((kh_done, 2 * b + c + 1), (km_done, 2 * b + c + 1), (k_parts, 2 * b + c + 1))
                for part, (sem_, n) in enumerate(made):
                    await_alone(sp, sem_, n)
                    for i in [i for i, p in enumerate(TERMS_K) if p == part]:
                        sp.dma_start(k_stack[i * HD:(i + 1) * HD, heads, :], kp[:, part, c, :]).then_inc(stacked[c], 16)

            def prologue():
                sp.dma_start(xz[:], x[0].rearrange("(p t) d -> p t d", t=TQ)).then_inc(x_in, 16)
                sp.dma_start(cx[:], ctx[0].rearrange("(p k) d -> p k d", k=TK)).then_inc(cx_in, 16)
                sp.dma_start(raw_q, q_w.rearrange("(c p) n -> p c n", p=P)).then_inc(wq_in, 16)
                row = 0
                for v in (ln1_w, ln1_b, v_b, ln2_w, ln2_b, fc_b):
                    n = v.shape[0] // P
                    sp.dma_start(vec_rows[row:row + n, :], v.rearrange("(r p) -> r p", p=P)).then_inc(vec_in, 16)
                    row += n
                for i, v in enumerate((q_b, k_b)):
                    sp.dma_start(qk_rows[:, i, :], v.rearrange("(o n) -> o n", o=1)).then_inc(bias_in, 16)
                sp.dma_start(raw_k, k_w.rearrange("(c p) n -> p c n", p=P)).then_inc(wk_in, 16)
                sp.dma_start(mask_u[:], mask[0:1, :].partition_broadcast(P)).then_inc(mask_in, 16)
                sp.dma_start(raw_v, v_w.rearrange("(c p) n -> p c n", p=P)).then_inc(wv_in, 16)
                sp.wait_ge(consts, 2)
                for g in range(NG):
                    sp.dma_start(k_stack[ROW_MAX:ROWS, g * GH:(g + 1) * GH, :], sel[:]).then_inc(sel_in, 16)
                stack_heads(0, 0)
                load_pre(1)
                stack_heads(0, 1)
                for t, w in zip(raw_l1, (l1_q, l1_k, l1_v, l1_o)):
                    sp.dma_start(t, w.rearrange("(c p) n -> p c n", p=P)).then_inc(l1_in, 16)
                sp.dma_start(raw_c, cproj_w.rearrange("(c p) n -> p c n", p=P)).then_inc(wc_in, 16)
                sp.dma_start(raw_f, fc_w.rearrange("(c p) n -> p c n", p=P)).then_inc(wf_in, 16)
                sp.dma_start(cb[:], cproj_b.rearrange("(o n) -> o n", o=1).partition_broadcast(P)).then_inc(bc_in, 16)
                sp.dma_start(pb[:], proj_b.rearrange("(o n) -> o n", o=1).partition_broadcast(P)).then_inc(bc_in, 16)
                sp.dma_start(alpha_c[:], alpha.partition_broadcast(P)).then_inc(bc_in, 16)
                sp.dma_start(raw_p, proj_w.rearrange("(c p) n -> p c n", p=P)).then_inc(wp_in, 16)

            def iteration(b, first, last):
                if first:
                    stack_heads(1, 0)
                    return
                if not last:
                    load_pre(b + 1)
                else:
                    sp.wait_ge(pre_full, PRE_USES * b + U_ZT + 1)
                    sp.dma_start(xz[:], x[b].rearrange("(p t) d -> p t d", t=TQ)).then_inc(last_h_in, 16)
                    sp.dma_start(cx[:], ctx[b].rearrange("(p k) d -> p k d", k=TK)).then_inc(last_cx_in, 16)
                stack_heads(b, 1)
                if not last:
                    stack_heads(b + 1, 0)

            def epilogue():
                sp.wait_ge(h_free, 16 * (B + 1))

            run(sp, iteration, prologue, epilogue)

        @block.tensor
        def _(pe):
            def product(o, w, wi, v, vi, n, start=True, stop=True):
                for k in range(n):
                    for i, (a, c) in enumerate(((0, 0), (0, 1), (1, 0))):
                        mm = pe.matmul(o, wi(w[a], k), vi(v[c], k), start=start and k == 0 and i == 0,
                                       stop=stop and k == n - 1 and i == 2)
                return mm

            def products(terms, w, v, n, fresh, whole, start=True, stop=True):
                early, late = (((0, 0), (0, 1)), (1, 0)) if fresh is w else (((0, 0), (1, 0)), (0, 1))
                for i, (o, wi, vi) in enumerate(terms):
                    for k in range(n):
                        for a, c in early:
                            pe.matmul(o, wi(w[a], k), vi(v[c], k), start=start and i == k == a == c == 0, stop=False)
                whole()
                for i, (o, wi, vi) in enumerate(terms):
                    for k in range(n):
                        mm = pe.matmul(o, wi(w[late[0]], k), vi(v[late[1]], k), start=False,
                                       stop=stop and i == len(terms) - 1 and k == n - 1)
                return mm

            def pre(b, n):
                await_(pe, pre_free, PRE_USES * b + n if not (isinstance(b, int) and b == 0) else
                       n - 2 if n < U_Q else max(n - 2, U_ZT + 1))
                if n == U_ZT:
                    pe.wait_ge(z1_done, b + 1)
                    for c in range(DC):
                        for t in range(TQ):
                            mm = pe.transpose(pre_bank(b, n)[:, c * LQ + t * P:c * LQ + (t + 1) * P], xz[:, t, chunk(c)], ident[:])
                elif n < U_Q:
                    c = n - U_CT
                    pe.wait_ge(cx_in, 16 * (b + 1))
                    for k in range(TK):
                        mm = pe.transpose(pre_bank(b, n)[:, chunk(k)], cx[:, k, chunk(c)], ident[:])
                elif n == U_Q:
                    for c in range(DC):
                        mm = product(pre_bank(b, n)[:, c * LQ:(c + 1) * LQ], wq, lambda w, k: w[:, k, chunk(c)],
                                     zT, lambda v, k: v[:, k, :], DC)
                elif n < U_V:
                    c = n - U_K
                    mm = product(pre_bank(b, n), wk, lambda w, k: w[:, k, chunk(c)],
                                 cT, lambda v, k: v[:, k, :], DC)
                else:
                    for i in range(2):
                        t = 2 * (n - U_V) + i
                        mm = product(pre_bank(b, n)[:, i * D:(i + 1) * D], cT, lambda v, k: v[:, k, chunk(t)],
                                     wv, lambda w, k: w[:, k, :], DC)
                mm.then_inc(pre_full, 1)

            def max_tile(b, g, s):
                hd, t = g * GH + s // 2, s % 2
                if s == 0:
                    pe.wait_ge(stacked[g // 2], 16 * STACK_DMAS * (b + 1))
                n = NS * b + SLOTS * g + s
                await_(pe, s1_free, n - 1)
                pe.matmul(s1[:, s % 2, :], q_stack[0:ROW_MAX, hd, chunk(t)], k_stack[0:ROW_MAX, hd, :],
                          start=True, stop=True).then_inc(s1_full, 1)

            def max_rows(b, g):
                pe.wait_ge(max_split, NG * b + g + 1)
                await_(pe, o_done, NG * b + g - 1)
                for t in range(TQ):
                    mm = pe.transpose(om_rows[0:ROWS, chunk(t)], max_cols[:, t, :], ident_b[:])
                mm.then_inc(rows_ps, 1)

            def exp_tile(b, g, s):
                hd = g * GH + s // 2
                n = NS * b + SLOTS * g + s
                await_(pe, s2_free, n - 1)
                for i in range(2):
                    k = 2 * (s % 2) + i
                    mm = pe.matmul(s2[:, s % 2, i * LQ:(i + 1) * LQ], k_stack[:, hd, chunk(k)], q_stack[:, hd, :],
                                   start=True, stop=True)
                mm.then_inc(s2_full, 1)

            def pv(b, g, k):
                if k == 0:
                    await_(pe, s2_free, NS * b + SLOTS * (g + 1))
                    pe.wait_ge(pre_free, PRE_USES * (b + 1))
                for j in range(GH):
                    mm = pe.matmul(om[32 * j:32 * j + VW, 0:LQ], vals[:, k, g * GH + j, :], probs[:, g % 2, j, k, :],
                                   start=k == 0, stop=k == TK - 1)
                if k == TK - 1:
                    mm.then_inc(pv_done, 1)

            def post(b, step):
                def open_(n):
                    bank, count = post_use(b, n)
                    await_(pe, post_free[bank], count)
                    return post_ps[:, bank, :]

                def ready(n):
                    bank, count = post_use(b, n)
                    pe.wait_ge(post_free[bank], count + 1)

                def ready_high(n):
                    pe.wait_ge(post_hi, split_count(b, n))

                def fill(mm, n):
                    mm.then_inc(post_full[bank_of(b, n)], 1)

                if step in ("CT0", "CT1"):
                    c = int(step[2])
                    wait_context(pe, b)
                    o = open_(W_CT + c)
                    for k in range(TK):
                        mm = pe.transpose(o[:, chunk(k)], context(b)[:, k, chunk(c)], ident[:])
                    fill(mm, W_CT + c)
                elif step == "OT":
                    pe.wait_ge(o_done, NG * (b + 1))
                    for t in range(TQ):
                        o = open_(W_OT + t)
                        for g in range(NG):
                            mm = pe.transpose(o[:, chunk(g)], oT[:, g, chunk(t)], ident[:])
                        fill(mm, W_OT + t)
                elif step in ("NT", "ZT", "HT"):
                    n = {"NT": W_NT, "ZT": W_ZT, "HT": W_HT}[step]
                    src = {"NT": z2, "ZT": z2, "HT": residual(b)}[step]
                    if step == "NT":
                        ready(W_OT)
                        ready(W_OT + 1)
                    elif step == "ZT":
                        pe.wait_ge(z2_done, b + 1)
                    else:
                        ready(W_PJ)
                    o = open_(n)
                    for c in range(DC):
                        for t in range(TQ):
                            mm = pe.transpose(o[:, c * LQ + t * P:c * LQ + (t + 1) * P], src[:, t, chunk(c)], ident[:])
                    fill(mm, n)
                elif step in ("CP", "DL"):
                    n, act, w, src = (W_CP, aT, wc, W_NT) if step == "CP" else (W_DL, mixT, wo, W_PC)
                    ready_high(src)
                    o = open_(n)
                    mm = products([(o[:, t * D:(t + 1) * D], lambda v, k, t=t: v[:, k, chunk(t)], lambda v, k: v[:, k, :])
                                   for t in range(TQ)], act, w, DC, act, lambda: ready(src))
                    fill(mm, n)
                elif step[0] == "F":
                    i = int(step[1])
                    ready_high(W_ZT)
                    o = open_(W_F + i)
                    mm = products([(o[:, j * LQ:(j + 1) * LQ], lambda w, k, f=2 * i + j: w[:, k, chunk(f)],
                                    lambda v, k: v[:, k, :]) for j in range(2)], wf, aT, DC, aT, lambda: ready(W_ZT))
                    fill(mm, W_F + i)
                elif step[:2] == "PJ":
                    i = int(step[2])
                    pe.wait_ge(y_hi, 4 * b + i + 1)
                    o = open_(W_PJ) if i == 0 else post_ps[:, bank_of(b, W_PJ), :]
                    mm = products([(o[:, t * D:(t + 1) * D], lambda v, k, t=t: v[:, k + 2 * i, chunk(t)],
                                    lambda v, k: v[:, k + 2 * i, :]) for t in range(TQ)], y, wp, 2, y,
                                  lambda: pe.wait_ge(y_split, 4 * b + i + 1), start=i == 0, stop=i == 3)
                    if i == 3:
                        fill(mm, W_PJ)
                elif step == "G":
                    ready_high(W_HT)
                    o = open_(W_G)
                    mm = products([(o[:, c * LQ:(c + 1) * LQ], lambda w, k, c=c: w[:, k, chunk(c)], lambda v, k: v[:, k, :])
                                   for c in range(DC)], wa, aT, DC, aT, lambda: ready(W_HT))
                    fill(mm, W_G)
                elif step in ("S0", "S1"):
                    t = int(step[1])
                    ready_high(W_G)
                    o = open_(W_S + t)
                    mm = products([(o, lambda v, k: v[:, k, chunk(t)], lambda v, k: v[:, k, :])], gT, pT, DC, gT,
                                  lambda: ready(W_G))
                    fill(mm, W_S + t)
                elif step in ("PT0", "PT1"):
                    i = int(step[2])
                    ready(W_S)
                    ready(W_S + 1)
                    o = open_(W_PT + i)
                    for j in range(2):
                        for t in range(TQ):
                            mm = pe.transpose(o[:, j * LQ + t * P:j * LQ + (t + 1) * P],
                                              probs1(b)[:, t, chunk(2 * i + j)], ident[:])
                    fill(mm, W_PT + i)
                elif step == "PC":
                    pe.wait_ge(cx_split, b + 1)
                    o = open_(W_PC)
                    ready_high(W_PT + 1)
                    mm = products([(o[:, c * LQ:(c + 1) * LQ], lambda v, k, c=c: v[:, k, chunk(c)], lambda v, k: v[:, k, :])
                                   for c in range(DC)], pc, p1T, TK, p1T, lambda: ready(W_PT + 1))
                    fill(mm, W_PC)

            def prepare(step):
                if step == "WA":
                    pe.wait_ge(l1_in, 16 * 4)
                    for c in range(DC):
                        for k in range(DC):
                            mm = pe.matmul(post_ps[:, 0, c * D:(c + 1) * D], raw_l1[0][:, k, chunk(c)], raw_l1[1][:, k, :],
                                           start=k == 0, stop=k == DC - 1)
                    mm.then_inc(prep_ps, 1)
                elif step == "WT":
                    for c in range(DC):
                        for k in range(DC):
                            mm = pe.transpose(post_ps[:, 1, c * D + k * P:c * D + (k + 1) * P], raw_l1[3][:, k, chunk(c)], ident[:])
                    mm.then_inc(prep_ps, 1)
                elif step == "CB":
                    pe.wait_ge(wc_in, 16)
                    pe.wait_ge(prep_step, 1)
                    pe.wait_ge(prep_done, 1)
                    for k in range(DC):
                        pe.matmul(post_ps[:, 1, 0:D], h[:, k, 0:P], raw_c[:, k, :], start=k == 0, stop=k == DC - 1)
                    pe.wait_ge(wf_in, 16)
                    for f in range(FC):
                        for k in range(DC):
                            mm = pe.matmul(post_ps[:, 1, D + f:D + f + 1], raw_f[:, k, chunk(f)],
                                           vecs[:, V_LN2B + k:V_LN2B + k + 1], start=k == 0, stop=k == DC - 1)
                    mm.then_inc(prep_ps, 1)
                elif step == "WO":
                    pe.wait_ge(w_lo, 4)
                    for c in range(DC):
                        for k in range(DC):
                            mm = pe.matmul(post_ps[:, 0, c * D:(c + 1) * D], raw_l1[2][:, k, chunk(c)], z2[:, k, :],
                                           start=k == 0, stop=k == DC - 1)
                    mm.then_inc(prep_ps, 1)
                elif step == "END":
                    pe.wait_ge(prep_done, 2)
                    pe.wait_ge(w_lo, 10)

            def prologue():
                pe.wait_ge(consts, 1)
                for n in range(U_CT, U_ZT + 1):
                    pre(0, n)
                pe.wait_ge(vec_in, 16 * 6)
                pe.transpose(s2[:, 0, 0:VECS], vec_rows[:], ident[0:VECS, 0:VECS]).then_inc(vec_ps, 1)
                pe.wait_ge(wq_in, 16)
                pe.wait_ge(vec_done, 2)
                for k in range(DC):
                    mm = pe.matmul(s2[0:1, 1, 0:D], vecs[:, V_LN1B + k:V_LN1B + k + 1], raw_q[:, k, :],
                                   start=k == 0, stop=k == DC - 1)
                mm.then_inc(bq_ps, 1)
                pe.wait_ge(bq_done, 2)
                for i in range(2 * DC):
                    mm = pe.matmul(s2[:, 1, D + i:D + i + 1], qk_perm[:, i // DC, chunk(i % DC)], ident[0:1, 0:1],
                                   start=True, stop=True)
                mm.then_inc(bq_ps, 1)
                pe.wait_ge(w_lo, 1)
                pre(0, U_Q)
                pe.wait_ge(w_lo, 2)
                pre(0, U_K)
                pre(0, U_K + 1)
                pe.wait_ge(w_lo, 3)
                pre(0, U_V)
                pe.wait_ge(sel_in, 16 * NG)
                for s in range(SLOTS):
                    max_tile(0, 0, s)
                pre(0, U_V + 1)
                max_rows(0, 0)
                for s in range(START):
                    attend(0, 0, s, 0)
                    attend(0, 0, s, 1)

            def attend(b, g, s, part):
                if part == 0:
                    nb, ng = ahead(b, g)
                    if not (isinstance(nb, int) and nb == B):
                        for i in MAX_TILES[s]:
                            max_tile(nb, ng, i)
                else:
                    pb_, pg = behind(b, g)
                    if s == 0:
                        pe.wait_ge(rows_in, NG * b + g + 1)
                    if s < TK and not (isinstance(pb_, int) and pb_ < 0):
                        pv(pb_, pg, s)
                    exp_tile(b, g, s)
                    nb, ng = ahead(b, g)
                    if s == ROWS_AT and not (isinstance(nb, int) and nb == B):
                        max_rows(nb, ng)

            def iteration(b, first, last):
                for at, ab, g, s, attends in slots(b, last):
                    if attends:
                        attend(ab, g, s, 0)
                    if not last and at in pre_at(b + 1):
                        pre(b + 1, pre_at(b + 1)[at])
                    if not last and at in V_AT:
                        pre(b + 1, U_V + V_AT[at])
                    if not first and at in steps_at(b - 1):
                        post(b - 1, steps_at(b - 1)[at])
                    if first and at in PREP_AT:
                        prepare(PREP_AT[at])
                    if attends:
                        attend(ab, g, s, 1)
                    elif s < TK:
                        pv(b, NG - 1, s)

            def epilogue():
                for step in LAST_AT.values():
                    post(B - 1, step)

            run(pe, iteration, prologue, epilogue)

        @block.scalar
        def _(act):
            def pre(b, n):
                if U_K <= n < U_V:
                    return
                act.wait_ge(pre_full, PRE_USES * b + n + 1)
                if n < U_Q:
                    dst = zT[0][:].rearrange("p c n -> p (c n)") if n == U_ZT else cT[0][:, n - U_CT, :]
                    act.activation(dst, pre_bank(b, n), ACT.Copy).then_inc(pre_hi, 1)
                elif n == U_Q:
                    await_(act, stacked[0], 16 * STACK_DMAS * b)
                    await_(act, stacked[1], 16 * STACK_DMAS * b)
                    await_(act, q_parts, b)
                    for c in range(DC):
                        act.activation(qf[:, c, :], pre_bank(b, n)[:, c * LQ:(c + 1) * LQ], ACT.Identity, bias=bq[:, c:c + 1])
                    for c in range(DC):
                        a = act.activation(qp[:, 0, c, :], pre_bank(b, n)[:, c * LQ:(c + 1) * LQ], ACT.Identity, bias=bq[:, c:c + 1])
                    a.then_inc(pre_free, 1)
                elif n >= U_V:
                    i = n - U_V
                    await_(act, pv_done, NG * b)
                    act.activation(vals[:, 2 * i:2 * i + 2, :, 0:HD],
                                   pre_bank(b, n).rearrange("p (t h d) -> p t h d", t=2, h=H), ACT.Copy).then_inc(pre_free, 1)

            def query_middle(b):
                act.wait_ge(qr_done, b + 1)
                act.activation(qp[:, 1, :, :], qf[:], ACT.Copy).then_inc(qm_done, 1)

            def key_high(b, c):
                await_(act, stacked[c], 16 * STACK_DMAS * b)
                act.wait_ge(pre_free, PRE_USES * b + U_K + c + 1)
                act.activation(kp[:, 0, c, :], kf[:], ACT.Copy).then_inc(kh_done, 1)

            def key_middle(b, c):
                act.wait_ge(kr_done, 2 * b + c + 1)
                act.activation(kp[:, 1, c, :], kf[:], ACT.Copy).then_inc(km_done, 1)

            def rows(b, g):
                act.wait_ge(rows_ps, NG * b + g + 1)
                act.activation(q_stack[ROW_MASK:ROWS, g * GH:(g + 1) * GH, :],
                               om_rows[ROW_MASK:ROWS, :].unsqueeze(1).to_broadcast([ROWS - ROW_MASK, GH, LQ]),
                               ACT.Copy).then_inc(rows_in, 1)

            def exp(b, g, s):
                if s == 0:
                    await_(act, pv_done, NG * b + g - 1)
                act.wait_ge(s2_full, NS * b + SLOTS * g + s + 1)
                k = 2 * (s % 2)
                act.activation(probs[:, g % 2, s // 2, k:k + 2, :],
                               s2[:, s % 2, :].rearrange("p (k n) -> p k n", k=2), ACT.Exp).then_inc(s2_free, 1)

            def o_out(b, g):
                act.wait_ge(pv_done, NG * b + g + 1)
                act.activation(oT[:, g, :], om[:, 0:LQ], ACT.Copy).then_inc(o_done, 1)

            def post(b, step):
                def full(n):
                    bank, count = post_use(b, n)
                    act.wait_ge(post_full[bank], count)
                    return post_ps[:, bank, :]

                def high(dst, n):
                    act.activation(dst.rearrange("p c n -> p (c n)"), full(n), ACT.Copy).then_inc(post_hi, 1)

                if step in ("CT0", "CT1"):
                    c = int(step[2])
                    act.activation(pT[0][:, c, :], full(W_CT + c), ACT.Copy).then_inc(post_hi, 1)
                elif step in ("NT", "ZT", "HT"):
                    high(aT[0][:], {"NT": W_NT, "ZT": W_ZT, "HT": W_HT}[step])
                elif step[0] == "F":
                    i = int(step[1])
                    ps_ = full(W_F + i)
                    if i == 3:
                        act.wait_ge(y_split, 4 * b + 1)
                    for j in range(2):
                        a = act.activation(fx[i % 3][:, j * LQ:(j + 1) * LQ], ps_[:, j * LQ:(j + 1) * LQ], ACT.Identity,
                                           bias=bf[:, 2 * i + j:2 * i + j + 1])
                    a.then_inc(post_free[bank_of(b, W_F + i)], 1)
                elif step == "G":
                    high(gT[0], W_G)
                elif step in ("PT0", "PT1"):
                    i = int(step[2])
                    high(p1T[0][:, 2 * i:2 * i + 2, :], W_PT + i)
                elif step == "PC":
                    high(mixT[0], W_PC)

            def exp1(b, t):
                bank, count = post_use(b, W_S + t)
                act.wait_ge(post_full[bank], count)
                act.wait_ge(max1, 2 * b + t + 1)
                act.wait_ge(cx_split, b + 1)
                act.activation(probs1(b)[:, t, :], post_ps[:, bank, :], ACT.Exp, bias=stat1[:, 0, t:t + 1],
                               accum_out=stat1[:, 1, t:t + 1]).then_inc(post_free[bank], 1)

            def gelu_tanh(b, i):
                act.wait_ge(cube, 4 * b + i + 1)
                act.activation(ft[i % 3], ft[i % 3], ACT.Tanh, scale=GELU_SCALE * GELU_CUBIC).then_inc(tanh_done, 1)

            def gelu_high(b, i):
                act.wait_ge(y_done, 4 * b + i + 1)
                act.activation(y[0][:, 2 * i:2 * i + 2, :].rearrange("p c n -> p (c n)"), fx[i % 3], ACT.Copy)\
                   .then_inc(y_hi, 1)

            def post_slot(b, at):
                if is_f(b, at - GELU_SPLIT):
                    gelu_high(b, chunk_of(b, at - GELU_SPLIT))
                if at in steps_at(b):
                    post(b, steps_at(b)[at])
                if steps_at(b).get(at) == "CX":
                    wait_context(act, b)
                    act.activation(pc[0][:], context(b)[:], ACT.Copy).then_inc(cx_high, 1)
                if is_f(b, at - GELU_TANH):
                    gelu_tanh(b, chunk_of(b, at - GELU_TANH))

            def post_slot_end(b, at):
                if steps_at(b).get(at - 1) in ("S0", "S1"):
                    exp1(b, int(steps_at(b)[at - 1][1]))

            def pre_slot_end(b, at):
                if pre_at(b).get(at - 2) == U_Q:
                    query_middle(b)
                if pre_at(b).get(at - 1, 0) >= U_K:
                    key_high(b, pre_at(b)[at - 1] - U_K)
                if pre_at(b).get(at - 2, 0) >= U_K:
                    key_middle(b, pre_at(b)[at - 2] - U_K)

            def load_post(b):
                act.wait_ge(h_free, 16 * (b + 1))
                act.dma_start(h[:], x[b].rearrange("(p t) d -> p t d", t=TQ)).then_inc(h_in, 16)
                act.dma_start(pcx[:], ctx[b].rearrange("(p k) d -> p k d", k=TK)).then_inc(pcx_in, 16)

            def store(b):
                bank, count = post_use(b, W_DL)
                act.wait_ge(post_free[bank], count + 1)
                act.dma_start(out[b].rearrange("(p t) d -> p t d", t=TQ), residual(b)[:]).then_inc(h_free, 16)

            def prepare(step):
                if step == "WA":
                    act.wait_ge(prep_ps, 1)
                    act.activation(wa[0][:].rearrange("p c n -> p (c n)"), post_ps[:, 0, :], ACT.Copy, scale=L1_SCALE)\
                       .then_inc(w_hi, 1)
                elif step == "WO":
                    act.wait_ge(prep_ps, 4)
                    act.activation(wo[0][:].rearrange("p c n -> p (c n)"), post_ps[:, 0, :], ACT.Copy).then_inc(w_hi, 1)
                elif step == "WC":
                    act.wait_ge(wc_in, 16)
                    act.activation(wc[0][:], raw_c, ACT.Copy).then_inc(w_hi, 1)
                elif step[:2] == "WF":
                    k = int(step[2])
                    act.wait_ge(wf_in, 16)
                    act.activation(wf[0][:, k, :], raw_f[:, k, :], ACT.Copy, scale=vecs[:, V_LN2W + k:V_LN2W + k + 1])\
                       .then_inc(w_hi, 1)
                elif step[:2] == "WP":
                    half = slice(int(step[2]) * FC // 2, (int(step[2]) + 1) * FC // 2)
                    act.wait_ge(wp_in, 16)
                    act.activation(wp[0][:, half, :], raw_p[:, half, :], ACT.Copy, scale=0.5).then_inc(w_hi, 1)

            def prologue():
                for n in range(U_CT, U_ZT + 1):
                    pre(0, n)
                act.wait_ge(wq_in, 16)
                act.wait_ge(vec_done, 2)
                for k in range(DC):
                    a = act.activation(parts_of(wq[0][:, k, :]), by_head(raw_q[:, k, :]), ACT.Copy, scale=lnq[:, k:k + 1])
                a.then_inc(w_hi, 1)
                act.wait_ge(wk_in, 16)
                for k in range(DC):
                    a = act.activation(parts_of(wk[0][:, k, :]), by_head(raw_k[:, k, :]), ACT.Copy)
                a.then_inc(w_hi, 1)
                act.wait_ge(sel_done, 1)
                act.activation(sel[:], sel_small[:].unsqueeze(2).to_broadcast([3 * GH, GH, LK]), ACT.Copy).then_inc(consts, 1)
                act.wait_ge(bq_done, 4)
                pre(0, U_Q)
                act.wait_ge(wv_in, 16)
                act.activation(wv[0][:], raw_v, ACT.Copy).then_inc(w_hi, 1)
                query_middle(0)
                key_high(0, 0)
                key_middle(0, 0)
                key_high(0, 1)
                key_middle(0, 1)
                pre(0, U_V)
                rows(0, 0)
                pre(0, U_V + 1)
                for s in range(START):
                    attend(0, 0, s)

            def attend(b, g, s):
                nb, ng = ahead(b, g)
                pb_, pg = behind(b, g)
                if s == O_AT and not (isinstance(pb_, int) and pb_ < 0):
                    o_out(pb_, pg)
                exp(b, g, s)
                if s == ROWS_AT and not (isinstance(nb, int) and nb == B):
                    rows(nb, ng)

            def iteration(b, first, last):
                for at, ab, g, s, attends in slots(b, last):
                    if not first and at == LOAD_AT:
                        load_post(b - 1)
                    if not last and at in pre_at(b + 1):
                        pre(b + 1, pre_at(b + 1)[at])
                    if not last and at in V_AT:
                        pre(b + 1, U_V + V_AT[at])
                    if not first:
                        post_slot(b - 1, at)
                    elif at in PREP_AT:
                        prepare(PREP_AT[at])
                    if attends:
                        attend(ab, g, s)
                    elif s == O_AT:
                        o_out(b, NG - 1)
                    if not last:
                        pre_slot_end(b + 1, at)
                    if not first:
                        post_slot_end(b - 1, at)
                    if not first and at == STORE_AT:
                        store(b - 1)

            def epilogue():
                for at in range(START, START + NS):
                    post_slot(B - 1, at)
                    post_slot_end(B - 1, at)
                store(B - 1)

            run(act, iteration, prologue, epilogue)

        @block.vector
        def _(dve):
            def norm_stats(src, st, step, b):
                for t in range(TQ):
                    i = dve.bn_stats(st[:, t, 0:6], src[:, t, :])
                i.then_inc(step, 1)
                await_alone(dve, step, 3 * b + 1)
                for t in range(TQ):
                    i = dve.bn_aggr(st[:, t, 6:8], st[:, t, 0:6])
                i.then_inc(step, 1)
                dve.wait_ge(step, 3 * b + 2)
                dve.tensor_scalar(st[:, :, 8], st[:, :, 7], EPS, None, ALU.add).then_inc(step, 1)

            def norm_apply(src, st, z, rstd, b, done):
                dve.wait_ge(rstd, b + 1)
                for t in range(TQ):
                    i = dve.tensor_scalar(z[:, t, :], src[:, t, :], st[:, t, 6:7], st[:, t, 8:9], ALU.subtract, ALU.mult)
                i.then_inc(done, 1)

            def take_mask(b):
                dve.wait_ge(mask_in, 16 * (b + 1))
                dve.tensor_copy(mask_f[:].rearrange("q (k p) -> q k p", k=TK),
                                mask_u[:].rearrange("q (p k) -> q k p", k=TK)).then_inc(mask_done, 1)

            def pre(b, n):
                if n < U_Q:
                    i = PRE_SPLITS.index(n)
                    dve.wait_ge(pre_hi, len(PRE_SPLITS) * b + i + 1)
                    j = 0 if n == U_ZT else n - U_CT
                    dst, hi = [t[:].rearrange("p c n -> p (c n)") if n == U_ZT else t[:, j, :]
                               for t in ((zT[1], zT[0]) if n == U_ZT else (cT[1], cT[0]))]
                    dve.tensor_tensor(dst, pre_bank(b, n), hi.bitcast(F32), ALU.subtract).then_inc(pre_free, 1)
                elif U_K <= n < U_V:
                    c = n - U_K
                    dve.wait_ge(pre_full, PRE_USES * b + n + 1)
                    dve.wait_ge(mask_done, b + 1)
                    if isinstance(b, int) and b == 0:
                        dve.wait_ge(pre_free, n)
                    await_(dve, k_parts, 2 * b + c)
                    dve.scalar_tensor_tensor(kf[:], pre_bank(b, n), bk[:, c:c + 1], mask_f[:], ALU.add, ALU.mult)\
                       .then_inc(pre_free, 1)

            def take_max(b, g, s):
                dve.wait_ge(s1_full, NS * b + SLOTS * g + s + 1)
                dve.tensor_reduce(neg_max[:, g % 2, s % 2, s // 2:s // 2 + 1], s1[:, s % 2, :], AX.X, ALU.max,
                                  negate=True).then_inc(s1_free, 1)

            def split_max(b, g):
                step = 3 * (NG * b + g)
                part = [max_cols[:, :, ROW_MAX + i:ROWS:3] for i in range(3)]
                neg = neg_max[:, g % 2, :, :]
                dve.wait_ge(s1_free, NS * b + SLOTS * (g + 1))
                await_(dve, rows_ps, NG * b + g)
                dve.tensor_copy(part[0], neg).then_inc(max_step, 1)
                dve.wait_ge(max_step, step + 1)
                dve.tensor_tensor(max_rest[:], neg, part[0], ALU.subtract).then_inc(max_step, 1)
                dve.wait_ge(max_step, step + 2)
                dve.tensor_copy(part[1], max_rest[:]).then_inc(max_step, 1)
                dve.wait_ge(max_step, step + 3)
                dve.tensor_tensor(part[2], max_rest[:], part[1], ALU.subtract).then_inc(max_split, 1)

            def post(b, step):
                def full(n):
                    bank, count = post_use(b, n)
                    dve.wait_ge(post_full[bank], count)
                    return post_ps[:, bank, :]

                def low(dst, hi, n):
                    dve.wait_ge(post_hi, split_count(b, n))
                    dve.tensor_tensor(dst, post_ps[:, bank_of(b, n), :].rearrange("p (c n) -> p c n", c=dst.shape[1]),
                                      hi.bitcast(F32), ALU.subtract).then_inc(post_free[bank_of(b, n)], 1)

                if step in ("CT0", "CT1"):
                    c = int(step[2])
                    low(pT[1][:, c:c + 1, :], pT[0][:, c:c + 1, :], W_CT + c)
                elif step == "OT":
                    for t in range(TQ):
                        o = full(W_OT + t).rearrange("p (h e) -> p h e", h=H)
                        dve.reciprocal(rden[:, t, :], o[:, :, HD]).then_inc(rden_done, 1)
                        dve.wait_ge(rden_done, 2 * b + t + 1)
                        dve.tensor_tensor(z2[:, t, :].rearrange("p (h d) -> p h d", h=H), o[:, :, 0:HD],
                                          rden[:, t, :].unsqueeze(2).to_broadcast([P, H, HD]), ALU.mult)\
                           .then_inc(post_free[bank_of(b, W_OT + t)], 1)
                elif step in ("NT", "ZT", "HT"):
                    low(aT[1][:], aT[0][:], {"NT": W_NT, "ZT": W_ZT, "HT": W_HT}[step])
                elif step == "CP":
                    o = full(W_CP)
                    dve.wait_ge(xb_done, b + 1)
                    dve.tensor_tensor(residual(b)[:].rearrange("p t n -> p (t n)"), o, residual(b)[:].rearrange("p t n -> p (t n)"), ALU.add)\
                       .then_inc(post_free[bank_of(b, W_CP)], 1)
                    bank, count = post_use(b, W_CP)
                    dve.wait_ge(post_free[bank], count + 1)
                    norm_stats(residual(b), ln2, ln2_step, b)
                elif step == "PJ3":
                    o = full(W_PJ)
                    dve.wait_ge(hb_done, b + 1)
                    dve.tensor_tensor(residual(b)[:].rearrange("p t n -> p (t n)"), o, residual(b)[:].rearrange("p t n -> p (t n)"), ALU.add)\
                       .then_inc(post_free[bank_of(b, W_PJ)], 1)
                elif step == "G":
                    low(gT[1], gT[0], W_G)
                elif step in ("S0", "S1"):
                    t = int(step[1])
                    dve.tensor_reduce(stat1[:, 0, t:t + 1], full(W_S + t), AX.X, ALU.max, negate=True).then_inc(max1, 1)
                elif step in ("PT0", "PT1"):
                    i = int(step[2])
                    low(p1T[1][:, 2 * i:2 * i + 2, :], p1T[0][:, 2 * i:2 * i + 2, :], W_PT + i)
                elif step == "PC":
                    low(mixT[1], mixT[0], W_PC)
                elif step == "DL":
                    for n in range(2):
                        bank, count = post_use(b, W_S + n)
                        dve.wait_ge(post_free[bank], count + 1)
                    dve.reciprocal(stat1[:, 2, :], stat1[:, 1, :]).then_inc(d_step, 1)
                    dve.wait_ge(d_step, 2 * b + 1)
                    dve.tensor_scalar(stat1[:, 3, :], stat1[:, 2, :], alpha_c[:, 0:1], None, ALU.mult).then_inc(d_step, 1)
                    dve.wait_ge(d_step, 2 * b + 2)
                    o = full(W_DL)
                    for t in range(TQ):
                        i = dve.scalar_tensor_tensor(residual(b)[:, t, :], o[:, t * D:(t + 1) * D], stat1[:, 3, t:t + 1], residual(b)[:, t, :],
                                                     ALU.mult, ALU.add)
                    i.then_inc(post_free[bank_of(b, W_DL)], 1)

            def gelu_cube(b, i):
                f = ft[i % 3]
                dve.wait_ge(square, 4 * b + i + 1)
                dve.scalar_tensor_tensor(f, f, 1.0 / GELU_CUBIC, fx[i % 3], ALU.add, ALU.mult).then_inc(cube, 1)

            def gelu_y(b, i):
                dve.wait_ge(tanh_done, 4 * b + i + 1)
                dve.scalar_tensor_tensor(fx[i % 3], ft[i % 3], 1.0, fx[i % 3], ALU.add, ALU.mult)\
                   .then_inc(y_done, 1)

            def gelu_split(b, i):
                hi, lo = [t[:, 2 * i:2 * i + 2, :].rearrange("p c n -> p (c n)") for t in y]
                dve.wait_ge(y_hi, 4 * b + i + 1)
                dve.tensor_tensor(lo, fx[i % 3], hi.bitcast(F32), ALU.subtract).then_inc(y_split, 1)

            def low_weights(dst, src, hi, n):
                dve.wait_ge(w_hi, n)
                return dve.tensor_tensor(dst, src, hi.bitcast(F32), ALU.subtract).then_inc(w_lo, 1)

            def prepare(step):
                if step == "WA":
                    dve.wait_ge(w_hi, 4)
                    dve.scalar_tensor_tensor(wa[1][:].rearrange("p c n -> p (c n)"), post_ps[:, 0, :], L1_SCALE,
                                             wa[0][:].rearrange("p c n -> p (c n)").bitcast(F32), ALU.mult, ALU.subtract)\
                       .then_inc(w_lo, 1)
                elif step == "WT":
                    dve.wait_ge(prep_ps, 2)
                    dve.tensor_copy(z2[:].rearrange("p c n -> p (c n)"), post_ps[:, 1, :]).then_inc(prep_done, 1)
                elif step == "CB":
                    dve.wait_ge(bc_in, 48)
                    dve.wait_ge(prep_ps, 3)
                    dve.tensor_tensor(cb[:], post_ps[:, 1, 0:D], cb[:], ALU.add).then_inc(h_free, 16)
                    dve.tensor_tensor(bf[:], post_ps[:, 1, D:D + FC], vecs[:, V_FCB:VECS], ALU.add).then_inc(prep_done, 1)
                elif step == "WO":
                    low_weights(wo[1][:].rearrange("p c n -> p (c n)"), post_ps[:, 0, :],
                                wo[0][:].rearrange("p c n -> p (c n)"), 5)
                elif step == "WC":
                    low_weights(wc[1][:], raw_c, wc[0][:], 6)
                elif step[:2] == "WF":
                    k = int(step[2])
                    dve.wait_ge(w_hi, 7 + k)
                    dve.scalar_tensor_tensor(wf[1][:, k, :], raw_f[:, k, :], vecs[:, V_LN2W + k:V_LN2W + k + 1],
                                             wf[0][:, k, :].bitcast(F32), ALU.mult, ALU.subtract).then_inc(w_lo, 1)
                elif step[:2] == "WP":
                    half = slice(int(step[2]) * FC // 2, (int(step[2]) + 1) * FC // 2)
                    dve.wait_ge(w_hi, 9 + int(step[2]))
                    dve.scalar_tensor_tensor(wp[1][:, half, :], raw_p[:, half, :], 0.5, wp[0][:, half, :].bitcast(F32),
                                             ALU.mult, ALU.subtract).then_inc(w_lo, 1)

            def prologue():
                dve.memset(max_cols[:], 0.0).then_inc(dve_const, 1)
                dve.wait_ge(dve_const, 1)
                dve.memset(max_cols[:, :, ROW_MASK:ROW_MAX], 1.0).then_inc(dve_const, 1)
                dve.memset(om[:], 0.0).then_inc(post_free[0], 1)
                dve.memset(vals[:, :, :, HD:VW], 1.0).then_inc(post_free[1], 1)
                dve.wait_ge(x_in, 16)
                norm_stats(xz, ln1, ln1_step, 0)
                norm_apply(xz, ln1, xz, rstd1, 0, z1_done)
                for n in range(U_CT, U_ZT + 1):
                    pre(0, n)
                dve.wait_ge(vec_ps, 1)
                dve.tensor_copy(vecs[:], s2[:, 0, 0:VECS]).then_inc(vec_done, 1)
                dve.wait_ge(vec_done, 1)
                dve.tensor_scalar(lnq[:], vecs[:, V_LN1W:V_LN1W + DC], Q_SCALE, None, ALU.mult).then_inc(vec_done, 1)
                dve.wait_ge(w_hi, 1)
                for k in range(DC):
                    for c in range(DC):
                        i = dve.scalar_tensor_tensor(
                            parts_of(wq[1][:, k, :])[:, c], by_head(raw_q[:, k, :])[:, c], lnq[:, k:k + 1],
                            parts_of(wq[0][:, k, :])[:, c].bitcast(F32), ALU.mult, ALU.subtract)
                i.then_inc(w_lo, 1)
                dve.wait_ge(bq_ps, 1)
                dve.wait_ge(bias_in, 32)
                dve.tensor_tensor(parts_of(qk_perm[:, 0, :]), by_head(s2[0:1, 1, 0:D]), by_head(qk_rows[:, 0, :]), ALU.add)\
                   .then_inc(bq_done, 1)
                dve.tensor_copy(parts_of(qk_perm[:, 1, :]), by_head(qk_rows[:, 1, :])).then_inc(bq_done, 1)
                dve.wait_ge(w_hi, 2)
                for k in range(DC):
                    i = dve.tensor_tensor(parts_of(wk[1][:, k, :]), by_head(raw_k[:, k, :]),
                                          parts_of(wk[0][:, k, :]).bitcast(F32), ALU.subtract)
                i.then_inc(w_lo, 1)
                dve.wait_ge(bq_ps, 2)
                dve.tensor_scalar(bq[:], s2[:, 1, D:D + DC], Q_SCALE, None, ALU.mult).then_inc(bq_done, 1)
                dve.tensor_copy(bk[:], s2[:, 1, D + DC:D + 2 * DC]).then_inc(bq_done, 1)
                take_mask(0)
                dve.memset(q_stack[ROW_MASK:ROWS, :, :], 1.0).then_inc(dve_const, 1)
                pre(0, U_K)
                low_weights(wv[1][:], raw_v, wv[0][:], 3)
                pre(0, U_K + 1)
                for s in range(SLOTS):
                    take_max(0, 0, s)
                split_max(0, 0)
                for s in range(START):
                    attend(0, 0, s)

            def attend(b, g, s):
                nb, ng = ahead(b, g)
                if not (isinstance(nb, int) and nb == B):
                    for i in MAX_TILES[s]:
                        take_max(nb, ng, i)
                    if s == SPLIT_AT:
                        split_max(nb, ng)

            def post_slot(b, at):
                if is_f(b, at - GELU_Y):
                    gelu_y(b, chunk_of(b, at - GELU_Y))
                if at - 1 in steps_at(b):
                    post(b, steps_at(b)[at - 1])
                if steps_at(b).get(at - 2) == "CP":
                    norm_apply(residual(b), ln2, z2, rstd2, b, z2_done)

            def post_slot_end(b, at):
                if is_f(b, at - GELU_CUBE):
                    gelu_cube(b, chunk_of(b, at - GELU_CUBE))

            def pre_slot(b, at):
                if at == LN1_AT:
                    dve.wait_ge(x_in, 16 * (b + 1))
                    norm_stats(xz, ln1, ln1_step, b)
                elif at == LN1_AT + 1:
                    norm_apply(xz, ln1, xz, rstd1, b, z1_done)
                if at - 1 in pre_at(b):
                    if pre_at(b)[at - 1] == U_Q:
                        take_mask(b)
                    pre(b, pre_at(b)[at - 1])

            def iteration(b, first, last):
                for at, ab, g, s, attends in slots(b, last):
                    if not last:
                        pre_slot(b + 1, at)
                    if not first:
                        post_slot(b - 1, at)
                    elif at in PREP_LOW_AT:
                        prepare(PREP_LOW_AT[at])
                    if attends:
                        attend(ab, g, s)
                    if not first:
                        post_slot_end(b - 1, at)

            def epilogue():
                for at in range(START, START + NS):
                    if is_f(B - 1, at - GELU_SPLIT):
                        gelu_split(B - 1, chunk_of(B - 1, at - GELU_SPLIT))
                    post_slot(B - 1, at)
                    post_slot_end(B - 1, at)

            run(dve, iteration, prologue, epilogue)

        @block.gpsimd
        def _(pool):
            def rstd(st, step, b, done):
                pool.wait_ge(step, 3 * b + 3)
                pool.tensor_tensor(st[:, :, 8], st[:, :, 8], minus_half[:], ALU.pow).then_inc(done, 1)

            def mask_row_of(b):
                await_alone(pool, mask_done, b + 1)
                for c in range(2):
                    await_alone(pool, stacked[c], 16 * STACK_DMAS * b)
                pool.tensor_scalar(mask_row[:], mask_f[0:1, :], -1.0, MASKED, ALU.add, ALU.mult).then_inc(row_done, 1)

            def query_rest(b):
                pool.wait_ge(pre_free, PRE_USES * b + U_Q + 1)
                pool.tensor_tensor(qf[:], qf[:], qp[:, 0, :, :], ALU.subtract).then_inc(qr_done, 1)

            def query_low(b):
                pool.wait_ge(qm_done, b + 1)
                pool.tensor_tensor(qp[:, 2, :, :], qf[:], qp[:, 1, :, :], ALU.subtract).then_inc(q_parts, 1)

            def key_rest(b, c):
                pool.wait_ge(kh_done, 2 * b + c + 1)
                pool.tensor_tensor(kf[:], kf[:], kp[:, 0, c, :], ALU.subtract).then_inc(kr_done, 1)

            def key_low(b, c):
                pool.wait_ge(km_done, 2 * b + c + 1)
                pool.tensor_tensor(kp[:, 2, c, :], kf[:], kp[:, 1, c, :], ALU.subtract).then_inc(k_parts, 1)

            def pre_slot(b, at):
                before = pre_at(b).get(at - 1, 0)
                two_before = pre_at(b).get(at - 2, 0)
                if before == U_Q:
                    query_rest(b)
                    mask_row_of(b)
                elif before >= U_K:
                    key_rest(b, before - U_K)
                if pre_at(b).get(at - 3) == U_Q:
                    query_low(b)
                if two_before >= U_K:
                    key_low(b, two_before - U_K)

            def post(b, step):
                if step == "NT":
                    wait_residual(pool, b)
                    pool.tensor_tensor(residual(b)[:], residual(b)[:], cb[:].unsqueeze(1).to_broadcast([P, TQ, D]), ALU.add).then_inc(xb_done, 1)
                elif step == "CP":
                    rstd(ln2, ln2_step, b, rstd2)
                elif step == "PJ0":
                    pool.wait_ge(z2_done, b + 1)
                    pool.tensor_tensor(residual(b)[:], residual(b)[:], pb[:].unsqueeze(1).to_broadcast([P, TQ, D]), ALU.add).then_inc(hb_done, 1)
                elif step[0] == "F":
                    i = int(step[1])
                    bank, count = post_use(b, W_F + i)
                    if i == 2:
                        pool.wait_ge(q_parts, min(b + 3, B) if isinstance(b, int) else b + 3)
                    pool.wait_ge(post_free[bank], count + 1)
                    pool.tensor_tensor(ft[i % 3], fx[i % 3], fx[i % 3], ALU.mult).then_inc(square, 1)

            def gelu_split(b, i):
                hi, lo = [t[:, 2 * i:2 * i + 2, :].rearrange("p c n -> p (c n)") for t in y]
                pool.wait_ge(y_hi, 4 * b + i + 1)
                pool.tensor_tensor(lo, fx[i % 3], hi.bitcast(F32), ALU.subtract).then_inc(y_split, 1)

            def post_slot(b, at):
                if is_f(b, at - GELU_SPLIT) and not is_last(b):
                    gelu_split(b, chunk_of(b, at - GELU_SPLIT))
                if at in steps_at(b):
                    post(b, steps_at(b)[at])
                if steps_at(b).get(at - 1) == "CX":
                    pool.wait_ge(cx_high, b + 1)
                    pool.tensor_tensor(pc[1][:], context(b)[:], pc[0][:].bitcast(F32), ALU.subtract).then_inc(cx_split, 1)

            def prologue():
                pool.memset(ident[:], 0.0).then_inc(pool_step, 1)
                pool.memset(sel_small[:], 1.0).then_inc(pool_step, 1)
                pool.wait_ge(pool_step, 2)
                pool.affine_select(out=ident[:], in_=ident[:], compare_op=ALU.not_equal, fill=1.0, base=0,
                                   pattern=[[-1, P]], channel_multiplier=1).then_inc(pool_step, 1)
                pool.affine_select(out=sel_small[:], in_=sel_small[:], compare_op=ALU.is_ge, fill=0.0, base=0,
                                   pattern=[[-3, GH]], channel_multiplier=1).then_inc(pool_step, 1)
                pool.memset(minus_half[:], -0.5).then_inc(pool_step, 1)
                pool.wait_ge(pool_step, 5)
                pool.affine_select(out=sel_small[:], in_=sel_small[:], compare_op=ALU.is_ge, fill=0.0, base=2,
                                   pattern=[[3, GH]], channel_multiplier=-1).then_inc(sel_done, 1)
                pool.tensor_scalar(ident_b[:], ident[:], 1.0, None, ALU.mult).then_inc(consts, 1)
                rstd(ln1, ln1_step, 0, rstd1)
                pool.wait_ge(vec_done, 1)
                pool.tensor_scalar(h[:, :, 0:P], vecs[:, V_VB:V_VB + DC].unsqueeze(2).to_broadcast([P, DC, P]), 1.0, None, ALU.mult)\
                    .then_inc(prep_step, 1)
                mask_row_of(0)
                query_rest(0)
                query_low(0)
                for c in range(DC):
                    key_rest(0, c)
                    key_low(0, c)

            def iteration(b, first, last):
                for at in range(START, START + NS):
                    if not last and at == LN1_AT:
                        rstd(ln1, ln1_step, b + 1, rstd1)
                    if not first:
                        post_slot(b - 1, at)
                    if not last:
                        pre_slot(b + 1, at)

            def epilogue():
                for at in range(START, START + NS):
                    post_slot(B - 1, at)

            run(pool, iteration, prologue, epilogue)


_INS = ["x", "ctx_2048", "mask_BxS2_bf1", "L0_xattn_ln1_w", "L0_xattn_ln1_b", "L0_xattn_q_w", "L0_xattn_q_b",
        "L0_xattn_k_w", "L0_xattn_k_b", "L0_xattn_v_w", "L0_xattn_v_b", "L0_xattn_cproj_w", "L0_xattn_cproj_b",
        "L0_xattn_ln2_w", "L0_xattn_ln2_b", "L0_xattn_fc_w", "L0_xattn_fc_b", "L0_xattn_proj_w",
        "L0_xattn_proj_b", "L1_xattn_w_q", "L1_xattn_w_k", "L1_xattn_w_v", "L1_xattn_w_o", "L1_xattn_alpha"]


def kernel(**inputs):
    import numpy as _np
    import concourse.bacc as _bacc
    from concourse import mybir as _mybir
    from concourse.bass_utils import run_bass_kernel_spmd as _run

    nc = _bacc.Bacc("TRN2", target_bir_lowering=False, num_devices=1)
    arrays, args = {}, []
    for name in _INS:
        a = _np.ascontiguousarray(inputs[name])
        if a.dtype == _np.bool_:
            a = a.view(_np.uint8)
        if a.ndim == 0 or name.endswith("alpha"):
            a = a.reshape(1, 1)
        arrays[f"in_{name}_dram"] = a
        args.append(nc.dram_tensor(f"in_{name}_dram", a.shape, _mybir.dt.from_np(a.dtype), kind="ExternalInput").ap())
    args.append(nc.dram_tensor("out_0_dram", (B, LQ, D), _mybir.dt.float32, kind="ExternalOutput").ap())
    build(nc, *args)
    r = _run(nc, [arrays], core_ids=[0])
    return r.results[0]["out_0_dram"]
```
